# Optimizing a Trainium2 kernel written in Bass

```python
import numpy as np
import jax
import jax.numpy as jnp

def _softmax(x, axis=-1):
    return jax.nn.softmax(x, axis=axis)

def _gelu(x):
    return jax.nn.gelu(x, approximate=True)

def _silu(x):
    return jax.nn.silu(x)

def _sigmoid(x):
    return jax.nn.sigmoid(x)

def _layernorm(x, axis=-1, eps=1e-05):
    m = jnp.mean(x, axis=axis, keepdims=True)
    v = jnp.var(x, axis=axis, keepdims=True)
    return (x - m) / jnp.sqrt(v + eps)

def _scatter_add(tgt, idx, src, axis=0):
    return tgt.at[idx].add(src)

def _segment_sum(src, seg, n):
    return jax.ops.segment_sum(src, seg, n)
kernel_name = 'mk_flamingo_gated_d1_seqx_r4_c58f4e'

def setup_inputs(seed: int=0):
    np.random.seed(seed)
    _w = jnp.asarray

    def _rec_inputs():
        import jax
        import jax.numpy as jnp
        _rk = jax.random.key(seed)
        x = -0.0003929 + 0.9999 * jax.random.normal(jax.random.fold_in(_rk, 1), (4, 1024, 256), jnp.float32)
        _lenS = 1024 - jax.random.randint(jax.random.fold_in(_rk, 7), (4,), 0, max(1, 1024 // 4) + 1, jnp.int32)
        _lenS2 = 77 - jax.random.randint(jax.random.fold_in(_rk, 8), (4,), 0, max(1, 77 // 4) + 1, jnp.int32)
        _ctx_1024P = jax.random.normal(jax.random.fold_in(_rk, 11), (4, 16, 256), jnp.float32)
        _ctx_1024c = jax.random.dirichlet(jax.random.fold_in(_rk, 511), 0.3 * jnp.ones((16,), jnp.float32), (4, 77))
        _ctx_1024t = jnp.einsum('bsk,bkd->bsd', _ctx_1024c, _ctx_1024P)
        _ctx_1024t = _ctx_1024t * jax.lax.rsqrt(jnp.mean(jnp.square(_ctx_1024t)) + 1e-12) * 0.953939
        ctx_1024 = 2.81802e-05 + 1.00001 * (_ctx_1024t + 0.3 * jax.random.normal(jax.random.fold_in(_rk, 611), (4, 77, 256), jnp.float32))
        _validS = jnp.arange(1024)[None, :] < _lenS[:, None]
        _validS2 = jnp.arange(77)[None, :] < _lenS2[:, None]
        _causal = jnp.tril(jnp.ones((1024, 1024), dtype=bool))
        mask_BxS2_ff1 = jnp.where(jnp.ones((4, 77), dtype=bool), 1.0, 0.0).astype(jnp.float32)
        _g = jax.random.normal(jax.random.fold_in(_rk, 9001), (2, 1), jnp.float32)
        _g = jnp.sign(_g) * jnp.maximum(jnp.abs(_g), 1.0) + (_g == 0) * 1.0
        g_xattn = _g[0]
        g_ffn = _g[1]
        return (x, ctx_1024, mask_BxS2_ff1, g_xattn, g_ffn)
    x, ctx_1024, mask_BxS2_ff1, g_xattn, g_ffn = _rec_inputs()

    def _L0_xattn_setup():
        import jax, jax.numpy as jnp
        import numpy as np
        D_MODEL = 256
        HEADS = 16
        DEPTH = D_MODEL // HEADS
        B, S = (4, 1024)
        EPS_K = 1e-06
        EPS_LN = 1e-06

        def _layernorm(x, g, b):
            m = jnp.mean(x, axis=-1, keepdims=True)
            var = jnp.var(x, axis=-1, keepdims=True)
            return (x - m) * jax.lax.rsqrt(var + EPS_LN) * g + b

        def _split_heads(x):
            bsz, sl, _ = x.shape
            return x.reshape(bsz, sl, HEADS, DEPTH).transpose(0, 2, 1, 3)
        key = jax.random.key(seed)
        ks = jax.random.split(key, 8)
        lecun = 1.0 / np.sqrt(D_MODEL)
        glorot = np.sqrt(2.0 / (D_MODEL + D_MODEL))
        return {'q': jax.random.normal(ks[0], (B, S, D_MODEL), jnp.float32), 'k': jax.random.normal(ks[1], (B, S, D_MODEL), jnp.float32), 'v': jax.random.normal(ks[2], (B, S, D_MODEL), jnp.float32), 'mask': jnp.ones((B, S), jnp.float32), 'wq': jax.random.normal(ks[3], (D_MODEL, D_MODEL), jnp.float32) * lecun, 'wk': jax.random.normal(ks[4], (D_MODEL, D_MODEL), jnp.float32) * lecun, 'wv': jax.random.normal(ks[5], (D_MODEL, D_MODEL), jnp.float32) * lecun, 'ln_gamma': jnp.ones((D_MODEL,), jnp.float32), 'ln_beta': jnp.zeros((D_MODEL,), jnp.float32), 'dense_w': jax.random.normal(ks[6], (D_MODEL, D_MODEL), jnp.float32) * glorot, 'dense_b': jnp.zeros((D_MODEL,), jnp.float32)}
    _L0_xattn_all = _L0_xattn_setup()
    _L0_xattn_in = {k: v for k, v in _L0_xattn_all.items() if k in ('wq', 'wk', 'wv', 'ln_gamma', 'ln_beta', 'dense_w', 'dense_b')}
    del _L0_xattn_all

    def _L0_ffn_setup():
        import jax, jax.numpy as jnp
        import numpy as np
        DIM = 256
        DEPTH = 2
        HEADS = 8
        DIM_HEAD = 64
        WINDOW = 128
        INNER = HEADS * DIM_HEAD
        HID = int(DIM * 4 * 2 / 3)
        B, N = (2, 2048)
        QK_SCALE = 8.0

        def shift_token(t):
            t1, t2 = jnp.split(t, 2, axis=-1)
            t2 = jnp.pad(t2, ((0, 0), (1, 0), (0, 0)))[:, :-1]
            return jnp.concatenate([t1, t2], axis=-1)

        def l2norm(t):
            return t / jnp.clip(jnp.linalg.norm(t, axis=-1, keepdims=True), 1e-12)

        def rotate_half(x):
            x1, x2 = jnp.split(x, 2, axis=-1)
            return jnp.concatenate([-x2, x1], axis=-1)

        def rotary_xpos(q, k):
            n = q.shape[-2]
            half_idx = jnp.arange(0, DIM_HEAD, 2, dtype=jnp.float32)
            inv_freq = 1.0 / 10000.0 ** (half_idx / DIM_HEAD)
            t = jnp.arange(n, dtype=jnp.float32)
            freqs = t[:, None] * inv_freq[None, :]
            freqs = jnp.concatenate([freqs, freqs], axis=-1)
            base = (half_idx + 0.4 * DIM_HEAD) / (1.4 * DIM_HEAD)
            power = (t - n // 2) / float(WINDOW // 2)
            scale = base[None, :] ** power[:, None]
            scale = jnp.concatenate([scale, scale], axis=-1)
            cos, sin = (jnp.cos(freqs), jnp.sin(freqs))
            q = q * cos * scale + rotate_half(q) * sin * scale
            k = k * cos / scale + rotate_half(k) * sin / scale
            return (q, k)

        def local_attention(q, k, v):
            b, h, n, d = q.shape
            w = n // WINDOW
            bq = q.reshape(b, h, w, WINDOW, d) * QK_SCALE
            bk = k.reshape(b, h, w, WINDOW, d)
            bv = v.reshape(b, h, w, WINDOW, d)

            def look_around(t):
                p = jnp.pad(t, ((0, 0), (0, 0), (1, 0), (0, 0), (0, 0)))
                return jnp.concatenate([p[:, :, :w], p[:, :, 1:]], axis=3)
            bk, bv = (look_around(bk), look_around(bv))
            bt = jnp.arange(n).reshape(w, WINDOW)
            btp = jnp.pad(bt, ((1, 0), (0, 0)), constant_values=-1)
            btk = jnp.concatenate([btp[:w], btp[1:]], axis=1)
            sim = jnp.einsum('bhwid,bhwjd->bhwij', bq, bk)
            i = bt[:, :, None]
            j = btk[:, None, :]
            mask = (i < j) | (i > j + WINDOW) | (j == -1)
            sim = jnp.where(mask, -jnp.finfo(sim.dtype).max, sim)
            attn = jax.nn.softmax(sim, axis=-1)
            out = jnp.einsum('bhwij,bhwjd->bhwid', attn, bv)
            return out.reshape(b, h, n, d)

        def _layer(x, wqkv, qs, ksc, wo, lg, lb, w1, b1, w2, b2):
            b, n, _ = x.shape
            h = shift_token(x)
            qkv = h @ wqkv
            q, k, v = jnp.split(qkv, 3, axis=-1)
            to_heads = lambda t: t.reshape(b, n, HEADS, DIM_HEAD).transpose(0, 2, 1, 3)
            q, k, v = (to_heads(q), to_heads(k), to_heads(v))
            q = l2norm(q) * qs
            k = l2norm(k) * ksc
            q, k = rotary_xpos(q, k)
            o = local_attention(q, k, v)
            o = o.transpose(0, 2, 1, 3).reshape(b, n, INNER)
            x = x + o @ wo
            h = shift_token(x)
            mu = h.mean(-1, keepdims=True)
            var = h.var(-1, keepdims=True)
            h = (h - mu) / jnp.sqrt(var + 1e-05) * lg + lb
            h = h @ w1 + b1
            a, g = jnp.split(h, 2, axis=-1)
            h = a * jax.nn.gelu(g, approximate=False)
            x = x + h @ w2 + b2
            return x
        key = jax.random.key(seed)
        ks = jax.random.split(key, 6)
        return {'x': jax.random.normal(ks[0], (B, N, DIM), jnp.float32), 'wqkv': jax.random.normal(ks[1], (DEPTH, DIM, 3 * INNER), jnp.float32) * 0.02, 'q_scale': jnp.ones((DEPTH, DIM_HEAD), jnp.float32), 'k_scale': jnp.ones((DEPTH, DIM_HEAD), jnp.float32), 'wo': jax.random.normal(ks[2], (DEPTH, INNER, DIM), jnp.float32) * 0.02, 'ln_g': jnp.ones((DEPTH, DIM), jnp.float32), 'ln_b': jnp.zeros((DEPTH, DIM), jnp.float32), 'w1': jax.random.normal(ks[3], (DEPTH, DIM, 2 * HID), jnp.float32) * 0.02, 'b1': jnp.zeros((DEPTH, 2 * HID), jnp.float32), 'w2': jax.random.normal(ks[4], (DEPTH, HID, DIM), jnp.float32) * 0.02, 'b2': jnp.zeros((DEPTH, DIM), jnp.float32)}
    _L0_ffn_all = _L0_ffn_setup()
    _L0_ffn_in = {k: v for k, v in _L0_ffn_all.items() if k in ('wqkv', 'q_scale', 'k_scale', 'wo', 'ln_g', 'ln_b', 'w1', 'b1', 'w2', 'b2')}
    del _L0_ffn_all
    return {'x': x, 'ctx_1024': ctx_1024, 'mask_BxS2_ff1': mask_BxS2_ff1, 'g_xattn': g_xattn, 'g_ffn': g_ffn, 'L0_xattn_wq': _L0_xattn_in['wq'], 'L0_xattn_wk': _L0_xattn_in['wk'], 'L0_xattn_wv': _L0_xattn_in['wv'], 'L0_xattn_ln_gamma': _L0_xattn_in['ln_gamma'], 'L0_xattn_ln_beta': _L0_xattn_in['ln_beta'], 'L0_xattn_dense_w': _L0_xattn_in['dense_w'], 'L0_xattn_dense_b': _L0_xattn_in['dense_b'], 'L0_ffn_wqkv': _L0_ffn_in['wqkv'], 'L0_ffn_q_scale': _L0_ffn_in['q_scale'], 'L0_ffn_k_scale': _L0_ffn_in['k_scale'], 'L0_ffn_wo': _L0_ffn_in['wo'], 'L0_ffn_ln_g': _L0_ffn_in['ln_g'], 'L0_ffn_ln_b': _L0_ffn_in['ln_b'], 'L0_ffn_w1': _L0_ffn_in['w1'], 'L0_ffn_b1': _L0_ffn_in['b1'], 'L0_ffn_w2': _L0_ffn_in['w2'], 'L0_ffn_b2': _L0_ffn_in['b2']}

def reference(x, ctx_1024, mask_BxS2_ff1, g_xattn, g_ffn, L0_xattn_wq, L0_xattn_wk, L0_xattn_wv, L0_xattn_ln_gamma, L0_xattn_ln_beta, L0_xattn_dense_w, L0_xattn_dense_b, L0_ffn_wqkv, L0_ffn_q_scale, L0_ffn_k_scale, L0_ffn_wo, L0_ffn_ln_g, L0_ffn_ln_b, L0_ffn_w1, L0_ffn_b1, L0_ffn_w2, L0_ffn_b2):
    import jax
    import jax.numpy as jnp

    def _L0_xattn_ref(q, k, v, mask, wq, wk, wv, ln_gamma, ln_beta, dense_w, dense_b):
        import jax, jax.numpy as jnp
        import numpy as np
        D_MODEL = 256
        HEADS = 16
        DEPTH = D_MODEL // HEADS
        B, S = (4, 1024)
        EPS_K = 1e-06
        EPS_LN = 1e-06

        def _layernorm(x, g, b):
            m = jnp.mean(x, axis=-1, keepdims=True)
            var = jnp.var(x, axis=-1, keepdims=True)
            return (x - m) * jax.lax.rsqrt(var + EPS_LN) * g + b

        def _split_heads(x):
            bsz, sl, _ = x.shape
            return x.reshape(bsz, sl, HEADS, DEPTH).transpose(0, 2, 1, 3)
        bsz = q.shape[0]
        em = mask[:, None, :, None]
        qh = _split_heads(_layernorm(q @ wq, ln_gamma, ln_beta))
        kh = _split_heads(_layernorm(k @ wk, ln_gamma, ln_beta))
        vh = _split_heads(_layernorm(v @ wv, ln_gamma, ln_beta))
        q_prime = jax.nn.relu(qh) + EPS_K
        k_prime = (jax.nn.relu(kh) + EPS_K) * em
        vh = vh * em
        kv = jnp.einsum('bhnd,bhne->bhde', k_prime, vh)
        z = 1.0 / (jnp.einsum('bhnd,bhd->bhn', q_prime, k_prime.sum(axis=-2)) + EPS_K)
        att = jnp.einsum('bhnd,bhde,bhn->bhne', q_prime, kv, z)
        att = att.reshape(bsz, -1, D_MODEL)
        out = att @ dense_w + dense_b
        return _layernorm(out, ln_gamma, ln_beta)

    def _L0_ffn_ref(x, wqkv, q_scale, k_scale, wo, ln_g, ln_b, w1, b1, w2, b2):
        import jax, jax.numpy as jnp
        import numpy as np
        DIM = 256
        DEPTH = 2
        HEADS = 8
        DIM_HEAD = 64
        WINDOW = 128
        INNER = HEADS * DIM_HEAD
        HID = int(DIM * 4 * 2 / 3)
        B, N = (2, 2048)
        QK_SCALE = 8.0

        def shift_token(t):
            t1, t2 = jnp.split(t, 2, axis=-1)
            t2 = jnp.pad(t2, ((0, 0), (1, 0), (0, 0)))[:, :-1]
            return jnp.concatenate([t1, t2], axis=-1)

        def l2norm(t):
            return t / jnp.clip(jnp.linalg.norm(t, axis=-1, keepdims=True), 1e-12)

        def rotate_half(x):
            x1, x2 = jnp.split(x, 2, axis=-1)
            return jnp.concatenate([-x2, x1], axis=-1)

        def rotary_xpos(q, k):
            n = q.shape[-2]
            half_idx = jnp.arange(0, DIM_HEAD, 2, dtype=jnp.float32)
            inv_freq = 1.0 / 10000.0 ** (half_idx / DIM_HEAD)
            t = jnp.arange(n, dtype=jnp.float32)
            freqs = t[:, None] * inv_freq[None, :]
            freqs = jnp.concatenate([freqs, freqs], axis=-1)
            base = (half_idx + 0.4 * DIM_HEAD) / (1.4 * DIM_HEAD)
            power = (t - n // 2) / float(WINDOW // 2)
            scale = base[None, :] ** power[:, None]
            scale = jnp.concatenate([scale, scale], axis=-1)
            cos, sin = (jnp.cos(freqs), jnp.sin(freqs))
            q = q * cos * scale + rotate_half(q) * sin * scale
            k = k * cos / scale + rotate_half(k) * sin / scale
            return (q, k)

        def local_attention(q, k, v):
            b, h, n, d = q.shape
            w = n // WINDOW
            bq = q.reshape(b, h, w, WINDOW, d) * QK_SCALE
            bk = k.reshape(b, h, w, WINDOW, d)
            bv = v.reshape(b, h, w, WINDOW, d)

            def look_around(t):
                p = jnp.pad(t, ((0, 0), (0, 0), (1, 0), (0, 0), (0, 0)))
                return jnp.concatenate([p[:, :, :w], p[:, :, 1:]], axis=3)
            bk, bv = (look_around(bk), look_around(bv))
            bt = jnp.arange(n).reshape(w, WINDOW)
            btp = jnp.pad(bt, ((1, 0), (0, 0)), constant_values=-1)
            btk = jnp.concatenate([btp[:w], btp[1:]], axis=1)
            sim = jnp.einsum('bhwid,bhwjd->bhwij', bq, bk)
            i = bt[:, :, None]
            j = btk[:, None, :]
            mask = (i < j) | (i > j + WINDOW) | (j == -1)
            sim = jnp.where(mask, -jnp.finfo(sim.dtype).max, sim)
            attn = jax.nn.softmax(sim, axis=-1)
            out = jnp.einsum('bhwij,bhwjd->bhwid', attn, bv)
            return out.reshape(b, h, n, d)

        def _layer(x, wqkv, qs, ksc, wo, lg, lb, w1, b1, w2, b2):
            b, n, _ = x.shape
            h = shift_token(x)
            qkv = h @ wqkv
            q, k, v = jnp.split(qkv, 3, axis=-1)
            to_heads = lambda t: t.reshape(b, n, HEADS, DIM_HEAD).transpose(0, 2, 1, 3)
            q, k, v = (to_heads(q), to_heads(k), to_heads(v))
            q = l2norm(q) * qs
            k = l2norm(k) * ksc
            q, k = rotary_xpos(q, k)
            o = local_attention(q, k, v)
            o = o.transpose(0, 2, 1, 3).reshape(b, n, INNER)
            x = x + o @ wo
            h = shift_token(x)
            mu = h.mean(-1, keepdims=True)
            var = h.var(-1, keepdims=True)
            h = (h - mu) / jnp.sqrt(var + 1e-05) * lg + lb
            h = h @ w1 + b1
            a, g = jnp.split(h, 2, axis=-1)
            h = a * jax.nn.gelu(g, approximate=False)
            x = x + h @ w2 + b2
            return x
        for l in range(DEPTH):
            x = _layer(x, wqkv[l], q_scale[l], k_scale[l], wo[l], ln_g[l], ln_b[l], w1[l], b1[l], w2[l], b2[l])
        return x
    x = x + jnp.tanh(g_xattn[0]) * _L0_xattn_ref(_layernorm(x, axis=-1), ctx_1024, ctx_1024, mask_BxS2_ff1, L0_xattn_wq, L0_xattn_wk, L0_xattn_wv, L0_xattn_ln_gamma, L0_xattn_ln_beta, L0_xattn_dense_w, L0_xattn_dense_b)
    x = x + jnp.tanh(g_ffn[0]) * _L0_ffn_ref(_layernorm(x, axis=-1), L0_ffn_wqkv, L0_ffn_q_scale, L0_ffn_k_scale, L0_ffn_wo, L0_ffn_ln_g, L0_ffn_ln_b, L0_ffn_w1, L0_ffn_b1, L0_ffn_w2, L0_ffn_b2)
    return x

_drawn_inputs = setup_inputs


def setup_inputs(seed=0):
    import zlib

    import numpy as np

    out = dict(_drawn_inputs(seed))
    spreads = {'L0_xattn_ln_gamma': (1.0, 0.2),
     'L0_xattn_ln_beta': (0.0, 0.1),
     'L0_xattn_dense_b': (0.0, 0.1),
     'L0_ffn_q_scale': (1.0, 0.6),
     'L0_ffn_k_scale': (1.0, 0.6),
     'L0_ffn_ln_g': (1.0, 0.2),
     'L0_ffn_ln_b': (0.0, 0.517),
     'L0_ffn_b1': (0.0, 0.1),
     'L0_ffn_b2': (0.0, 0.1)}
    factors = {}
    for name, (base, spread) in spreads.items():
        noise = np.random.default_rng([zlib.crc32(name.encode()), seed]).standard_normal(out[name].shape)
        drawn = base * np.exp(spread * noise) if base else spread * noise
        out[name] = jnp.asarray(drawn.astype(out[name].dtype))
    for name, factor in factors.items():
        out[name] = (out[name] * factor).astype(out[name].dtype)
    return out
```

```python
from contextlib import ExitStack

import numpy as np

import concourse.bass as bass
from concourse import mybir
from concourse.alu_op_type import AluOpType as ALU

ACT = mybir.ActivationFunctionType
AX = mybir.AxisListType
F32 = mybir.dt.float32
BF16 = mybir.dt.bfloat16

P = 128
D = 256
DC = D // P
NB, S = 4, 1024
WPB = S // P
NT = NB * WPB
G = 4
NG = NT // G
SLOTS = WPB + 1
CTX = 77
XH, XD = 16, 16
XHC = P // XD
KVC = P + XHC
LAYERS = 2
H, HD = 8, 64
INNER = H * HD
HP = H // 2
HID = 682
MC = 114
NM = 6
MW = [MC] * (NM - 1) + [HID - MC * (NM - 1)]
MASKED = -1e30
LN_SCALE = 2.0 ** 20
EPS5, EPS6 = 1e-5, 1e-6


def position_tables():
    half = np.arange(0, HD, 2, dtype=np.float32)
    inv = (np.float32(1.0) / np.float32(10000.0) ** (half / np.float32(HD))).astype(np.float32)
    t = np.arange(S, dtype=np.float32)
    freqs = (t[:, None] * inv[None, :]).astype(np.float32)
    freqs = np.concatenate([freqs, freqs], -1)
    base = ((half + np.float32(0.4 * HD)) / np.float32(1.4 * HD)).astype(np.float32)
    power = ((t - S // 2) / np.float32(64.0)).astype(np.float32)
    scale = (base[None, :] ** power[:, None]).astype(np.float32)
    scale = np.concatenate([scale, scale], -1)
    cos, sin = np.cos(freqs), np.sin(freqs)
    sign = np.concatenate([np.ones(HD // 2), -np.ones(HD // 2)]).astype(np.float32)
    t4 = np.stack([np.stack([cos * scale, sin * scale * sign], 1),
                   np.stack([cos / scale, sin / scale * sign], 1)], 1).astype(np.float32)
    return np.ascontiguousarray(t4.reshape(WPB, P, 2, 2, HD).transpose(1, 0, 2, 3, 4))


def block_order(u):
    return (1, 0) if u else (0, 1)


def masks():
    q, k = np.arange(P)[:, None], np.arange(P)[None, :]
    m = np.zeros((P, 2, G, 2, P), np.float32)
    for half in range(2):
        for u in range(G):
            cur, prev = block_order(u)
            m[:, half, u, cur] = np.where(k > q, MASKED, 0.0)
            m[:, half, u, prev] = MASKED if half == 0 and u == 0 else np.where(k < q, MASKED, 0.0)
    return m


def block_diagonal():
    f = np.arange(P)[:, None] // XD
    c = np.concatenate([np.arange(P) // XD, np.arange(XHC)])[None, :]
    return np.repeat((f == c).astype(np.float32)[:, None, :], DC, 1)


def program(nc, x, ctx_in, mask_in, g_xattn, g_ffn, wq, wk, wv, xg, xb, dw, db,
            wqkv, q_scale, k_scale, wo, ln_g, ln_b, w1, b1, w2, b2,
            tables_in, masks_in, blocks_in, ident_in, out):
    ctx = ExitStack()
    with ctx:
        def sb(name, shape, dt=F32):
            return ctx.enter_context(nc.sbuf_tensor(name, shape, dt))

        def sem(name):
            return ctx.enter_context(nc.semaphore(name))

        x1 = sb("x1", [P, NT, D])
        state = sb("state", [P, NB * SLOTS, D])
        ident = sb("ident", [P, P])
        identb = sb("identb", [P, P], BF16)
        tanh_g = sb("tanh_g", [P, 2])
        wqkv_sb = sb("wqkv_sb", [P, DC, 3 * INNER])
        wo_sb = sb("wo_sb", [P, HP, D])
        w1_sb = sb("w1_sb", [P, DC, 2 * HID])
        w2_sb = sb("w2_sb", [MC, NM, D])
        lnc = sb("lnc", [P, 2, DC])
        b1c = sb("b1c", [MC, 2, NM])
        b2r = sb("b2r", [P, D])
        qks = sb("qks", [P, 2, HD])
        tab = sb("tab", [P, WPB, 2, 2, HD])
        mask_sb = sb("mask_sb", [P, 2, G, 2, P], BF16)
        hs = sb("hs", [P, 2, D])
        hT = sb("hT", [P, DC, P])
        vring = sb("vring", [P, G, INNER])
        ktring = sb("ktring", [P, HP, G, P])
        sq = sb("sq", [P, 2, INNER])
        ssum = sb("ssum", [P, 2 * H])
        lns = sb("lns", [P, 2 * H])
        y0 = sb("y0", [P, 2 * H])
        ya = sb("ya", [P, 2 * H])
        yb = sb("yb", [P, 2 * H])
        rn = sb("rn", [P, 2, 2 * H])
        khat = sb("khat", [P, INNER])
        rot = sb("rot", [P, 2, 2, INNER])
        qT = sb("qT", [P, HP, P])
        negmax = sb("negmax", [P, 2, H])
        rowmax = sb("rowmax", [P, 2, H])
        lsum = sb("lsum", [P, 2, H])
        linv = sb("linv", [P, H])
        probs = sb("probs", [P, 2, 4, 2 * P])
        pT = sb("pT", [P, 2, 4, 2, P])
        onorm = sb("onorm", [P, INNER])
        oT = sb("oT", [P, HP, P])
        hf = sb("hf", [P, G, D])
        fst = sb("fst", [P, G, 2, 6])
        fmv = sb("fmv", [P, G, 2])
        fve = sb("fve", [P, G])
        frs = sb("frs", [P, G])
        hn = sb("hn", [P, G, D])
        hnT = sb("hnT", [P, DC, G * P])
        gel = sb("gel", [MC, 2, G * P])
        hid = sb("hid", [MC, NM, G * P])
        minus_half = sb("minus_half", [P, G])
        half_log = sb("half_log", [P, 1])

        ps = [ctx.enter_context(nc.psum_tensor(f"ps{i}", [P, 512], F32)) for i in range(8)]

        xw = wqkv_sb[:, :, 0:3 * D]
        dw_sb = wo_sb[:, 0:DC, :]
        gam_r = sb("gam_r", [P, D])
        bet_r = sb("bet_r", [P, D])
        db_r = sb("db_r", [P, D])
        gT = sb("gT", [P, D])
        bT = sb("bT", [P, D])
        xgc = sb("xgc", [P, 2, DC])
        em = sb("em", [CTX, NB])
        blocks = sb("blocks", [P, DC, KVC])
        kvs = ktring[:, :, :, :].rearrange("p a g k -> p (a g k)")[:, 0:NB * DC * KVC].rearrange(
            "p (b c n) -> p b c n", b=NB, c=DC)
        cst = sb("cst", [P, 2 * G, 6])
        cmv = sb("cmv", [P, 2 * G, 2])
        cve = sb("cve", [P, 2 * G])
        crs = sb("crs", [P, 2 * G])
        eps_row = sb("eps_row", [P, D])
        mh8 = sb("mh8", [P, 2 * G])
        cst_of, cmv_of, cve_of, crs_of = ({t: sb(f"{t}_{w}", [P, *shape]) for t in ("lnx", "lnq", "lno", "lnf")}
                                          for w, shape in (("st", (G, 6)), ("mv", (G, 2)), ("ve", (G,)), ("rs", (G,))))
        kvh = vring[0:CTX, :, :].rearrange("p g (i d) -> p g i d", i=2)
        kp = gel[0:CTX, :, :].rearrange("p a t -> p (a t)").rearrange("p (b d) -> p b d", b=NB)
        vp = hid[0:CTX, :, :].rearrange("p m t -> p (m t)")[:, 0:NB * DC * KVC].rearrange(
            "p (b c n) -> p b c n", b=NB, c=DC)
        zinv = sb("zinv", [P, G, XH])
        ctx_sb = hf[0:CTX, :, :]
        ctxT = hnT[:, :, :].rearrange("p c (b t) -> p c b t", b=NB)
        xn = probs[:, :, :, :].rearrange("p a h k -> p (a h k)")[:, 0:G * D].rearrange("p (g d) -> p g d", g=G)
        xnT = probs[:, :, :, :].rearrange("p a h k -> p (a h k)")[:, G * D:2 * G * D].rearrange("p (g d) -> p g d", g=G)
        qn = hf[:, :, :]
        qTs = rot[:, :, :, :].rearrange("p c a n -> p c (a n)").rearrange("p c (m n) -> p c m n", m=WPB)
        qTv = rot[:, :, :, :].rearrange("p c a n -> p c (a n)").rearrange("p c (m i a) -> p c m i a", m=WPB, i=2)
        att = pT[:, :, :, :, :].rearrange("p a h b k -> p (a h b k)").rearrange("p (h m e) -> p h m e", h=XH, m=WPB)
        attT = tab[:, :, :, :, :].rearrange("p w i a d -> p (w i a d)").rearrange("p (c t) -> p c t", c=DC)
        yx = sq[:, :, :].rearrange("p a i -> p (a i)").rearrange("p (g d) -> p g d", g=G)

        d_const = sem("d_const"); d_x = sem("d_x"); d_small = sem("d_small")
        d_attn_w = sem("d_attn_w"); d_ffn_w = sem("d_ffn_w"); d_hs = sem("d_hs"); d_hf = sem("d_hf")
        d_out = sem("d_out")
        rings_zeroed = sem("rings_zeroed")
        zeroed = sem("zeroed"); consts_set = sem("consts_set"); tanh_done = sem("tanh_done")
        folded = sem("folded")
        c_T = sem("c_T"); c_Tc = sem("c_Tc"); c_kv = sem("c_kv"); c_st = sem("c_st"); c_ag = sem("c_ag")
        c_ve = sem("c_ve"); c_rs = sem("c_rs"); c_norm = sem("c_norm"); c_aff = sem("c_aff")
        c_kvs = sem("c_kvs"); c_done = sem("c_done"); c_ones = sem("c_ones")
        L = {t: [sem(f"{t}_{w}") for w in ("stats", "moments", "var", "rstd", "normed")]
             for t in ("lnx", "lnq", "lno", "lnf")}
        x_ready = sem("x_ready")
        L["lnf"][4] = x_ready
        a_xT = sem("a_xT"); a_xTc = sem("a_xTc"); a_q = sem("a_q"); a_qT = sem("a_qT")
        a_relu = sem("a_relu"); a_qp = sem("a_qp"); a_att = sem("a_att"); a_zd = sem("a_zd"); a_z = sem("a_z")
        a_an = sem("a_an"); a_aT = sem("a_aT"); a_aTc = sem("a_aTc"); a_y = sem("a_y"); a_yb = sem("a_yb")
        a_g = sem("a_g"); a_b = sem("a_b"); a_x1 = sem("a_x1")
        tab_sin = sem("tab_sin"); tab_ready = sem("tab_ready")
        hT_ps = sem("hT_ps"); hT_ready = sem("hT_ready"); proj_done = sem("proj_done"); v_ready = sem("v_ready")
        squared = sem("squared"); summed = sem("summed"); clipped = sem("clipped"); logged = sem("logged")
        guessed = sem("guessed"); newton = sem("newton"); rn_ready = sem("rn_ready"); q_prod = sem("q_prod")
        khat_ready = sem("khat_ready"); k_prod = sem("k_prod"); qkT_ps = sem("qkT_ps"); qkT_ready = sem("qkT_ready")
        scored = sem("scored"); maxed = sem("maxed"); bias_ready = sem("bias_ready"); exped = sem("exped")
        pT_ps = sem("pT_ps"); pTA_ready = sem("pTA_ready"); pTB_ready = sem("pTB_ready"); pv_done = sem("pv_done")
        linv_ready = sem("linv_ready"); on_ready = sem("on_ready"); oT_ps = sem("oT_ps"); oT_ready = sem("oT_ready")
        wo_done = sem("wo_done"); x_attn = sem("x_attn")
        f_st = sem("f_st"); f_mv = sem("f_mv"); f_ve = sem("f_ve"); f_rs = sem("f_rs"); f_hn = sem("f_hn")
        f_hT = sem("f_hT"); f_hTc = sem("f_hTc"); f_w1 = sem("f_w1"); f_gel = sem("f_gel"); f_hid = sem("f_hid")
        f_w2 = sem("f_w2"); f_x = sem("f_x")
        summed_out = sem("summed_out")

        block = ctx.enter_context(nc.Block())

        N_CONST = 15

        def slot(k, u):
            v = G * k + (k >> 1) + u + 1
            return v if isinstance(v, int) else v.with_bounds(min_val=1, max_val=NB * SLOTS - G + u)

        x_view = x.rearrange("b (w p) d -> p (b w) d", p=P)
        out_view = out.rearrange("b (w p) d -> p (b w) d", p=P)

        @block.sync
        def _(sp):
            sp.dma_start(ctx_sb, ctx_in.rearrange("b p d -> p b d")).then_inc(d_const, 16)
            sp.dma_start(ident[:, :], ident_in).then_inc(d_const, 16)
            for i, w in enumerate((wq, wk, wv)):
                sp.dma_start(xw[:, :, i * D:(i + 1) * D], w.rearrange("(c p) n -> p c n", p=P)).then_inc(d_const, 16)
            sp.dma_start(dw_sb, dw.rearrange("(c p) n -> p c n", p=P)).then_inc(d_const, 16)
            sp.dma_start(blocks[:, :, :], blocks_in).then_inc(d_const, 16)
            for r, v in ((gam_r, xg), (bet_r, xb), (db_r, db)):
                sp.dma_start(r[:, :], v.partition_broadcast(P)).then_inc(d_const, 16)
            sp.dma_start(tanh_g[:, 0:1], g_xattn.partition_broadcast(P)).then_inc(d_const, 16)
            sp.dma_start(tanh_g[:, 1:2], g_ffn.partition_broadcast(P)).then_inc(d_const, 16)
            with nc.allow_non_contiguous_dma(reason="columns of small vectors"):
                sp.dma_start(xgc[:, 0, :], xg.rearrange("(c p) -> p c", p=P)).then_inc(d_const, 16)
                sp.dma_start(xgc[:, 1, :], xb.rearrange("(c p) -> p c", p=P)).then_inc(d_const, 16)
                sp.dma_start(em[:, :], mask_in.rearrange("b p -> p b")).then_inc(d_const, 16)
            for k in range(NG):
                sp.dma_start(x1[:, k * G:(k + 1) * G, :], x_view[:, k * G:(k + 1) * G, :]).then_inc(d_x, 16)

            def load_attn_weights(l):
                sp.dma_start(wqkv_sb[:, :, :], wqkv[l].rearrange("(c p) n -> p c n", p=P)).then_inc(d_attn_w, 16)
                sp.dma_start(wo_sb[:, :, :], wo[l].rearrange("(c p) n -> p c n", p=P)).then_inc(d_attn_w, 16)
                sp.dma_start(tab[:, :, :, :, :], tables_in).then_inc(d_attn_w, 16)
                sp.dma_start(qks[:, 0, :], q_scale[l].partition_broadcast(P)).then_inc(d_attn_w, 16)
                sp.dma_start(qks[:, 1, :], k_scale[l].partition_broadcast(P)).then_inc(d_attn_w, 16)

            def load_ffn_weights(l):
                sp.dma_start(w1_sb[:, :, :], w1[l].rearrange("(c p) n -> p c n", p=P)).then_inc(d_ffn_w, 16)
                sp.dma_start(w2_sb[:, 0:NM - 1, :], w2[l][0:MC * (NM - 1), :].rearrange("(m p) n -> p m n", p=MC))\
                  .then_inc(d_ffn_w, 16)
                sp.dma_start(w2_sb[0:MW[-1], NM - 1, :], w2[l][MC * (NM - 1):HID, :]).then_inc(d_ffn_w, 16)
                sp.dma_start(b2r[:, :], b2[l].partition_broadcast(P)).then_inc(d_ffn_w, 16)
                with nc.allow_non_contiguous_dma(reason="columns of small vectors"):
                    sp.dma_start(lnc[:, 0, :], ln_g[l].rearrange("(c p) -> p c", p=P)).then_inc(d_ffn_w, 16)
                    sp.dma_start(lnc[:, 1, :], ln_b[l].rearrange("(c p) -> p c", p=P)).then_inc(d_ffn_w, 16)
                    for a in range(2):
                        v = b1[l][a * HID:(a + 1) * HID]
                        sp.dma_start(b1c[:, a, 0:NM - 1], v[0:MC * (NM - 1)].rearrange("(m p) -> p m", p=MC))\
                          .then_inc(d_ffn_w, 16)
                        sp.dma_start(b1c[0:MW[-1], a, NM - 1:NM], v[MC * (NM - 1):HID].rearrange("(m p) -> p m", m=1))\
                          .then_inc(d_ffn_w, 16)

            def load_shifted(dst, s, s_before, n, done):
                half = slice(P, D)
                sp.dma_start(dst[:, :, 0:P], state[:, bass.ds(s, n), 0:P]).then_inc(done, 16)
                sp.dma_start(dst[1:P - 1, :, half], state[0:P - 2, bass.ds(s, n), half]).then_inc(done, 16)
                sp.dma_start(dst[P - 1:P, :, half], state[P - 2:P - 1, bass.ds(s, n), half]).then_inc(done, 16)
                sp.dma_start(dst[0:1, :, half], state[P - 1:P, bass.ds(s_before, n), half]).then_inc(done, 16)

            load_ffn_weights(0)
            sp.wait_ge(a_y, NT)
            load_attn_weights(0)
            sp.wait_ge(zeroed, 1)
            for l in range(LAYERS):
                with sp.Fori(l * NT, (l + 1) * NT, 2) as tile:
                    first = sp.snap((tile + (tile >> 3) + 1 - l * NB * SLOTS).with_bounds(min_val=1, max_val=NB * SLOTS - 2))
                    before = sp.snap(first - 1)
                    sp.wait_ge(x_ready, tile + 2)
                    sp.wait_ge(hT_ps, tile)
                    load_shifted(hs, first, before, 2, d_hs)
                if l + 1 < LAYERS:
                    sp.wait_ge(x_attn, (l + 1) * NT)
                    load_attn_weights(l + 1)
                with sp.Fori(l * NT, (l + 1) * NT, G) as tile:
                    first = sp.snap((tile + (tile >> 3) + 1 - l * NB * SLOTS).with_bounds(min_val=1, max_val=NB * SLOTS - G))
                    before = sp.snap(first - 1)
                    sp.wait_ge(x_attn, tile + G)
                    sp.wait_ge(f_hn, tile)
                    load_shifted(hf, first, before, G, d_hf)
                if l + 1 < LAYERS:
                    sp.wait_ge(f_w2, (l + 1) * NT)
                    sp.wait_ge(x_ready, (l + 2) * NT)
                    load_ffn_weights(l + 1)
            with sp.Fori(0, NG) as g:
                sp.wait_ge(summed_out, g + 1)
                sp.dma_start(out_view[:, bass.ds(g * G, G), :], x1[:, bass.ds(g * G, G), :]).then_inc(d_out, 16)
            sp.wait_ge(d_out, 16 * NG)

        @block.gpsimd
        def _(pool):
            pool.dma_start(mask_sb[:, :, :, :, :], masks_in).then_inc(d_small, 16)
            pool.dma_start(identb[:, :], ident_in).then_inc(d_small, 16)
            pool.memset(minus_half[:, :], -0.5)
            pool.memset(eps_row[:, :], EPS6)
            pool.memset(mh8[:, :], -0.5).then_inc(consts_set, 1)
            pool.memset(state[:, :, :].rearrange("p (b s) d -> p b s d", b=NB)[:, :, 0, :], 0.0).then_inc(zeroed, 1)
            pool.wait_ge(consts_set, 1)

            pool.wait_ge(c_ve, 1)
            pool.tensor_tensor(crs[0:CTX, :], cve[0:CTX, :], mh8[0:CTX, :], ALU.pow).then_inc(c_rs, 1)

            def rstd(t, k):
                pool.wait_ge(L[t][2], k + 1)
                pool.tensor_tensor(crs_of[t][:, :], cve_of[t][:, :], mh8[:, 0:G], ALU.pow).then_inc(L[t][3], 1)

            with pool.Fori(0, NB) as b:
                for s in range(2):
                    k = 2 * b + s
                    rstd("lnx", k)
                    rstd("lnq", k)
                for m in range(WPB):
                    pool.wait_ge(a_relu, WPB * b + WPB)
                    pool.tensor_tensor(qTs[:, :, m, :], qTs[:, :, m, :],
                                       eps_row[:, :].rearrange("p (c t) -> p c t", c=DC), ALU.add).then_inc(a_qp, 1)
                for s in range(2):
                    k = 2 * b + s
                    rstd("lno", k)
                    pool.wait_ge(folded, 1)
                    for j in range(G):
                        pool.wait_ge(L["lno"][4], G * k + j + 1)
                        pool.tensor_tensor(yx[:, j, :], yx[:, j, :], gT[:, :], ALU.mult).then_inc(a_g, 1)
                    for j in range(G):
                        pool.wait_ge(a_g, G * k + j + 1)
                        pool.tensor_tensor(yx[:, j, :], yx[:, j, :], bT[:, :], ALU.add).then_inc(a_b, 1)
                    rstd("lnf", k)

            pool.wait_ge(x_ready, NT)
            pool.memset(ktring[:, :, G - 1, :], 0.0).then_inc(rings_zeroed, 1)
            pool.memset(vring[:, G - 1, :], 0.0).then_inc(rings_zeroed, 1)

            with pool.Fori(0, LAYERS) as l:
                def rotate_keys(t, w):
                    pool.wait_ge(khat_ready, t + 1)
                    pool.wait_ge(qkT_ps, 2 * t)
                    src = khat[:, :].rearrange("p (h d) -> p h d", h=H)
                    pool.tensor_tensor(rot[:, 1, 0, :].rearrange("p (h d) -> p h d", h=H), src,
                                       tab[:, bass.ds(w, 1), 1, 0, :].to_broadcast((P, H, HD)), ALU.mult)
                    dst = rot[:, 1, 1, :].rearrange("p (h a e) -> p h a e", h=H, a=2)
                    src = khat[:, :].rearrange("p (h a e) -> p h a e", h=H, a=2)
                    for a in range(2):
                        ins = pool.tensor_tensor(
                            dst[:, :, 1 - a, :], src[:, :, a, :],
                            tab[:, bass.ds(w, 1), 1, 1, a * 32:a * 32 + 32].to_broadcast((P, H, 32)), ALU.mult)
                    ins.then_inc(k_prod, 1)

                pool.wait_ge(tab_ready, l + 1)
                rotate_keys(l * NT, 0)
                with pool.Fori(0, NG - 1) as k:
                    for u in range(G):
                        rotate_keys(l * NT + G * k + u + 1, (G * k + u + 1) & (WPB - 1))
                for u in range(G - 1):
                    rotate_keys(l * NT + G * (NG - 1) + u + 1, (G * (NG - 1) + u + 1) % WPB)

                def group_rstd(g):
                    pool.wait_ge(f_ve, l * NG + g + 1)
                    pool.tensor_tensor(frs[:, :], fve[:, :], minus_half[:, :], ALU.pow).then_inc(f_rs, 1)

                def add_b2(g):
                    for j in range(G):
                        pool.wait_ge(f_x, l * NT + G * g + j + 1)
                        tile = state[:, bass.ds(slot(g, j), 1), :].rearrange("p a d -> p (a d)")
                        pool.tensor_tensor(tile, tile, b2r[:, :], ALU.add).then_inc(x_ready, 1)

                group_rstd(0)
                with pool.Fori(0, NG - 1) as g:
                    group_rstd(g + 1)
                    add_b2(g)
                add_b2(NG - 1)

        @block.scalar
        def _(act):
            act.wait_ge(d_const, 16 * N_CONST)
            act.activation(tanh_g[:, :], tanh_g[:, :], ACT.Tanh).then_inc(tanh_done, 1)

            for b in range(NB):
                act.wait_ge(c_T, b + 1)
                act.activation(ctxT[:, :, b, 0:CTX], ps[b][:, 0:D].rearrange("p (c t) -> p c t", c=DC)[:, :, 0:CTX],
                               ACT.Copy).then_inc(c_Tc, 1)

            with act.Fori(0, NB) as b:
                for s in range(2):
                    k = 2 * b + s
                    for j in range(G):
                        act.wait_ge(a_xT, G * k + j + 1)
                        act.activation(xnT[:, j, :], ps[j][:, 0:D], ACT.Copy).then_inc(a_xTc, 1)
                    for j in range(G):
                        t = s * G + j
                        act.wait_ge(a_qT, G * k + j + 1)
                        for c in range(DC):
                            ins = act.activation(qTv[:, c, :, :, t * P // 16:(t + 1) * P // 16],
                                                 ps[j][:, c * P:(c + 1) * P].rearrange("p (a i m) -> p m i a", i=2, m=WPB),
                                                 ACT.Relu,
                                                 bias=xgc[:, 1, c:c + 1], scale=xgc[:, 0, c:c + 1])
                        ins.then_inc(a_relu, 1)
                for n in range(4):
                    act.wait_ge(a_aT, 4 * b + n + 1)
                    act.activation(attT[:, :, n * 2 * P:(n + 1) * 2 * P].rearrange("p i (h a) -> p i h a", h=4),
                                   ps[n][:, :].rearrange("p (h i a) -> p i h a", h=4, i=2), ACT.Copy)\
                       .then_inc(a_aTc, 1)

            act.wait_ge(rings_zeroed, 2)
            with act.Fori(0, LAYERS) as l:
                act.preload_act_table_set("natural_log_exp_and_others")

                def copy_hT(t):
                    act.wait_ge(hT_ps, t + 1)
                    act.activation(hT[:, :, :], ps[6][:, 0:D].rearrange("p (c t) -> p c t", c=DC), ACT.Copy)\
                       .then_inc(hT_ready, 1)

                def square(t):
                    act.wait_ge(summed, t)
                    for i in range(2):
                        act.wait_ge(proj_done, 3 * t + i + 1)
                        act.activation(sq[:, i, :], ps[4 + i][:, :], ACT.Square).then_inc(squared, 1)

                def guess_rsqrt(t):
                    act.wait_ge(clipped, t + 1)
                    act.activation(lns[:, :], ssum[:, :], ACT.Ln, scale=LN_SCALE).then_inc(logged, 1)
                    act.wait_ge(logged, t + 1)
                    act.activation(y0[:, :], lns[:, :], ACT.Exp, scale=-0.5, bias=half_log[:, 0:1]).then_inc(guessed, 1)

                def copy_v(t, u):
                    act.wait_ge(proj_done, 3 * t + 3)
                    act.activation(vring[:, u, :], ps[6][:, :], ACT.Copy).then_inc(v_ready, 1)

                def copy_qkT(t, u):
                    act.wait_ge(qkT_ps, 2 * t + 1)
                    act.activation(qT[:, :, :], ps[4][:, :].rearrange("p (h t) -> p h t", h=HP), ACT.Copy)\
                       .then_inc(qkT_ready, 1)
                    act.wait_ge(qkT_ps, 2 * t + 2)
                    act.activation(ktring[:, :, u, :], ps[5][:, :].rearrange("p (h t) -> p h t", h=HP), ACT.Copy)\
                       .then_inc(qkT_ready, 1)

                def exps(t, u, a):
                    act.wait_ge(bias_ready, 2 * t + a + 1)
                    act.wait_ge(pT_ps, 2 * t)
                    for i in range(4):
                        h = 4 * a + 2 * (i % 2) + i // 2
                        act.activation(probs[:, a, i, :], ps[2 * a + i // 2][:, (i % 2) * D:(i % 2 + 1) * D], ACT.Exp,
                                       scale=rn[:, u % 2, h:h + 1], bias=negmax[:, u % 2, h:h + 1],
                                       accum_out=lsum[:, u % 2, h:h + 1]).then_inc(exped, 1)

                def copy_pT_B(t):
                    act.wait_ge(pT_ps, 2 * t + 2)
                    act.wait_ge(pv_done, 2 * t)
                    for i in range(2):
                        ins = act.activation(pT[:, 1, 2 * i:2 * i + 2, :, :],
                                             ps[2 + i][:, :].rearrange("p (h b q) -> p h b q", h=2, b=2), ACT.Copy)
                    ins.then_inc(pTB_ready, 1)

                def copy_oT(t):
                    act.wait_ge(oT_ps, t + 1)
                    act.activation(oT[:, :, :], ps[7][:, :].rearrange("p (h t) -> p h t", h=HP), ACT.Copy)\
                       .then_inc(oT_ready, 1)

                def step(t, u, nxt, prev):
                    if nxt:
                        copy_hT(t + 1)
                    exps(t, u, 0)
                    if nxt:
                        square(t + 1)
                    exps(t, u, 1)
                    if nxt:
                        guess_rsqrt(t + 1)
                        copy_v(t + 1, (u + 1) % G)
                    copy_pT_B(t)
                    if prev:
                        copy_oT(t - 1)
                    if nxt:
                        copy_qkT(t + 1, (u + 1) % G)

                t0 = l * NT
                copy_hT(t0); square(t0); guess_rsqrt(t0); copy_v(t0, 0); copy_qkT(t0, 0)
                for u in range(G):
                    step(t0 + u, u, True, u > 0)
                with act.Fori(1, NG - 1) as k:
                    for u in range(G):
                        step(t0 + G * k + u, u, True, True)
                for u in range(G):
                    step(t0 + G * (NG - 1) + u, u, u < G - 1, True)
                copy_oT(t0 + NT - 1)

                def gelus(g):
                    for m in range(NM):
                        act.wait_ge(f_w1, (l * NG + g) * 2 * NM + 2 * m + 1)
                        act.wait_ge(f_hid, (l * NG + g) * NM + (m - 1 if m else 0))
                        act.activation(gel[0:MW[m], m % 2, :], ps[2 + 2 * (m % 2)][0:MW[m], :], ACT.Gelu,
                                       bias=b1c[0:MW[m], 1, m:m + 1]).then_inc(f_gel, 1)

                def copy_hnT(g):
                    act.wait_ge(f_w1, (l * NG + g) * 2 * NM)
                    for c in range(DC):
                        act.wait_ge(f_hT, (l * NG + g) * DC + c + 1)
                        act.activation(hnT[:, c, :], ps[c][:, :], ACT.Identity,
                                       bias=lnc[:, 1, c:c + 1], scale=lnc[:, 0, c:c + 1]).then_inc(f_hTc, 1)

                act.wait_ge(d_ffn_w, (l + 1) * 16 * 10)
                copy_hnT(0)
                with act.Fori(0, NG - 1) as g:
                    gelus(g)
                    copy_hnT(g + 1)
                gelus(NG - 1)

        @block.tensor
        def _(pe):
            pe.wait_ge(d_const, 16 * N_CONST)
            for b in range(NB):
                for c in range(DC):
                    mm = pe.transpose(ps[b][:, c * P:c * P + CTX], ctx_sb[:, b, c * P:(c + 1) * P], ident[0:CTX, 0:CTX])
                mm.then_inc(c_T, 1)
            for b in range(NB):
                pe.wait_ge(c_Tc, b + 1)
                for c in range(DC):
                    mm = pe.matmul(ps[4 + b][0:CTX, :], ctxT[:, c, b, 0:CTX], xw[:, c, D:3 * D],
                                   start=(c == 0), stop=(c == DC - 1))
                mm.then_inc(c_kv, 1)
            for b in range(NB):
                pe.wait_ge(c_aff, 2 * b + 2)
                for c in range(DC):
                    mm = pe.matmul(ps[b][:, c * KVC:(c + 1) * KVC], kp[:, b, c * P:(c + 1) * P], vp[:, b, c, :],
                                   start=True, stop=True)
                mm.then_inc(c_kvs, 1)
            pe.wait_ge(c_done, NB)

            with pe.Fori(0, NB) as b:
                for s in range(2):
                    k = 2 * b + s
                    pe.wait_ge(a_relu, G * k)
                    for j in range(G):
                        pe.wait_ge(L["lnx"][4], G * k + j + 1)
                        for c in range(DC):
                            mm = pe.transpose(ps[j][:, c * P:(c + 1) * P], xn[:, j, c * P:(c + 1) * P], ident[:, :])
                        mm.then_inc(a_xT, 1)
                    pe.wait_ge(a_yb, WPB * b)
                    for j in range(G):
                        pe.wait_ge(a_xTc, G * k + j + 1)
                        for c in range(DC):
                            mm = pe.matmul(ps[4 + j][:, 0:D], xnT[:, j, c * P:(c + 1) * P], xw[:, c, 0:D],
                                           start=(c == 0), stop=(c == DC - 1))
                        mm.then_inc(a_q, 1)
                    for j in range(G):
                        pe.wait_ge(L["lnq"][4], G * k + j + 1)
                        for c in range(DC):
                            mm = pe.transpose(ps[j][:, c * P:(c + 1) * P], qn[:, j, c * P:(c + 1) * P], ident[:, :])
                        mm.then_inc(a_qT, 1)
                for s in range(2):
                    for j in range(G):
                        pe.wait_ge(a_qp, WPB * b + s * G + j + 1)
                        if s:
                            pe.wait_ge(a_an, WPB * b + j + 1)
                        for c in range(DC):
                            mm = pe.matmul(ps[4 + j][:, c * KVC:(c + 1) * KVC], qTs[:, c, s * G + j, :],
                                           kvs[:, bass.ds(b, 1), c, :].rearrange("p a n -> p (a n)"),
                                           start=True, stop=True)
                        mm.then_inc(a_att, 1)
                pe.wait_ge(a_an, WPB * b + WPB)
                for h in range(XH):
                    mm = pe.transpose(ps[h // 4][:, h % 4 * P:(h % 4 + 1) * P],
                                      att[:, h, :, :].rearrange("p m e -> p (m e)"), ident[:, :])
                    if h % 4 == 3:
                        mm.then_inc(a_aT, 1)
                for s in range(2):
                    k = 2 * b + s
                    if s:
                        pe.wait_ge(a_yb, G * k)
                    for j in range(G):
                        t = s * G + j
                        pe.wait_ge(a_aTc, 4 * b + t // 2 + 1)
                        for c in range(DC):
                            mm = pe.matmul(ps[4 + j][:, 0:D], attT[:, c, t * P:(t + 1) * P], dw_sb[:, c, :],
                                           start=(c == 0), stop=(c == DC - 1))
                        mm.then_inc(a_y, 1)

            pe.wait_ge(d_small, 32)
            with pe.Fori(0, LAYERS) as l:
                def project(t):
                    pe.wait_ge(hT_ready, t + 1)
                    pe.wait_ge(qkT_ready, 2 * t)
                    for i in range(3):
                        for c in range(DC):
                            mm = pe.matmul(ps[4 + i][:, :], hT[:, c, :], wqkv_sb[:, c, i * INNER:(i + 1) * INNER],
                                           start=(c == 0), stop=(c == DC - 1))
                        mm.then_inc(proj_done, 1)

                def transpose_qk(t):
                    for i, ready in enumerate((q_prod, k_prod)):
                        pe.wait_ge(ready, t + 1)
                        for hp in range(HP):
                            for a in range(2):
                                mm = pe.matmul(ps[4 + i][:, hp * P:(hp + 1) * P], rot[:, i, a, hp * P:(hp + 1) * P],
                                               ident[:, :], start=(a == 0), stop=(a == 1), is_transpose=True)
                        mm.then_inc(qkT_ps, 1)

                def score(t, u, a, half):
                    pe.wait_ge((pTA_ready, pTB_ready)[a], t)
                    if a == 0:
                        pe.wait_ge(qkT_ready, 2 * t + 2)
                    first = (u - 1) if u else 0
                    step = 1 if u else G - 1
                    for i in range(2):
                        bank = ps[2 * a + i]
                        mask = mask_sb[:, bass.ds(half, 1), u, :, :].rearrange("p x b k -> p x (b k)")
                        pe.matmul(bank[:, :], identb[:, :], mask.to_broadcast((P, 2, D)),
                                  start=True, stop=False)
                        for j in range(2):
                            rows = slice(HD * i, HD * i + HD)
                            mm = pe.matmul(bank[:, j * D:(j + 1) * D], qT[rows, 2 * a + j, :],
                                           ktring[rows, 2 * a + j, first:first + step + 1:step, :],
                                           start=False, stop=(j == 1))
                    mm.then_inc(scored, 1)

                def transpose_p(t, a):
                    pe.wait_ge(exped, 8 * t + 4 * a + 4)
                    for i in range(4):
                        for b in range(2):
                            c = (2 * (i % 2) + b) * P
                            mm = pe.transpose(ps[2 * a + i // 2][:, c:c + P], probs[:, a, i, b * P:(b + 1) * P], ident[:, :])
                    mm.then_inc(pT_ps, 1)

                def weigh(t, u, a):
                    pe.wait_ge((pTA_ready, pTB_ready)[a], t + 1)
                    if a == 0:
                        pe.wait_ge(v_ready, t + 1)
                    cur, prev = block_order(u)
                    for i in range(4):
                        h = 4 * a + 2 * (i % 2) + i // 2
                        for b in range(2):
                            v = vring[:, u if b == cur else (u - 1) % G, h * HD:(h + 1) * HD]
                            mm = pe.matmul(ps[7][:, h * HD:(h + 1) * HD], pT[:, a, i, b, :], v,
                                           start=(b == 0), stop=(b == 1))
                    mm.then_inc(pv_done, 1)

                def transpose_o(t):
                    pe.wait_ge(on_ready, t + 1)
                    for hp in range(HP):
                        mm = pe.transpose(ps[7][:, hp * P:(hp + 1) * P], onorm[:, hp * P:(hp + 1) * P], ident[:, :])
                    mm.then_inc(oT_ps, 1)

                def project_out(t):
                    pe.wait_ge(oT_ready, t + 1)
                    for hp in range(HP):
                        mm = pe.matmul(ps[6][:, 0:D], oT[:, hp, :], wo_sb[:, hp, :],
                                       start=(hp == 0), stop=(hp == HP - 1))
                    mm.then_inc(wo_done, 1)

                def step_(t, u, k, nxt, prev, before):
                    half = k & 1
                    if nxt:
                        pe.wait_ge(d_hs, 64 * (pair0 + 2 * k + (u + 1) // 2 + 1))
                        if before:
                            pe.wait_ge(x_attn, t - 1)
                        else:
                            pe.wait_ge(v_ready, t + 1)
                        for c in range(DC):
                            mm = pe.transpose(ps[6][:, c * P:(c + 1) * P], hs[:, (u + 1) % 2, c * P:(c + 1) * P],
                                              ident[:, :])
                        mm.then_inc(hT_ps, 1)
                    score(t, u, 0, half)
                    score(t, u, 1, half)
                    if nxt:
                        project(t + 1)
                    transpose_p(t, 0)
                    transpose_p(t, 1)
                    if prev:
                        transpose_o(t - 1)
                        if nxt:
                            pe.wait_ge(v_ready, t + 2)
                        else:
                            pe.wait_ge(x_attn, t - 1)
                        project_out(t - 1)
                    weigh(t, u, 0)
                    if nxt:
                        transpose_qk(t + 1)
                    weigh(t, u, 1)

                t0, pair0 = l * NT, l * (NT // 2)
                pe.wait_ge(d_attn_w, (l + 1) * 16 * 5)
                pe.wait_ge(x_ready, t0 + NT)
                pe.wait_ge(d_hs, 64 * (pair0 + 1))
                for c in range(DC):
                    mm = pe.transpose(ps[6][:, c * P:(c + 1) * P], hs[:, 0, c * P:(c + 1) * P], ident[:, :])
                mm.then_inc(hT_ps, 1)
                project(t0)
                transpose_qk(t0)
                for u in range(G):
                    step_(t0 + u, u, 0, True, u > 0, u > 1)
                with pe.Fori(1, NG - 1) as k:
                    for u in range(G):
                        step_(t0 + G * k + u, u, k, True, True, True)
                for u in range(G):
                    step_(t0 + G * (NG - 1) + u, u, NG - 1, u < G - 1, True, True)
                transpose_o(t0 + NT - 1)
                pe.wait_ge(x_attn, t0 + NT - 1)
                project_out(t0 + NT - 1)

                def transpose_hn(g):
                    for c in range(DC):
                        for j in range(G):
                            pe.wait_ge(f_hn, (l * NG + g) * G + G)
                            mm = pe.transpose(ps[c][:, j * P:(j + 1) * P], hn[:, j, c * P:(c + 1) * P], ident[:, :])
                        mm.then_inc(f_hT, 1)

                def expand(g):
                    base = (l * NG + g)
                    for m in range(NM):
                        pe.wait_ge(f_hTc, base * DC + DC)
                        pe.wait_ge(f_hid, base * NM + (m - 1 if m else 0))
                        for a, off in ((0, HID), (1, 0)):
                            bank = ps[2 + 2 * (m % 2) + a]
                            for c in range(DC):
                                w = w1_sb[:, c, off + m * MC:off + m * MC + MW[m]]
                                mm = pe.matmul(bank[0:MW[m], :], w, hnT[:, c, :], start=(c == 0), stop=(c == DC - 1))
                            mm.then_inc(f_w1, 1)

                def contract(g):
                    for j in range(G):
                        pe.wait_ge(f_hid, (l * NG + g) * NM + NM)
                        pe.wait_ge(f_x, l * NT + G * g + (j - 1 if j > 1 else 0))
                        for m in range(NM):
                            mm = pe.matmul(ps[6 + j % 2][:, 0:D], hid[0:MW[m], m, j * P:(j + 1) * P],
                                           w2_sb[0:MW[m], m, :], start=(m == 0), stop=(m == NM - 1))
                        mm.then_inc(f_w2, 1)

                pe.wait_ge(d_ffn_w, (l + 1) * 16 * 10)
                pe.wait_ge(x_attn, t0 + NT)
                transpose_hn(0)
                with pe.Fori(0, NG - 1) as g:
                    expand(g)
                    transpose_hn(g + 1)
                    contract(g)
                expand(NG - 1)
                contract(NG - 1)

        @block.vector
        def _(dve):
            dve.wait_ge(d_const, 16 * N_CONST)
            dve.memset(half_log[:, :], 0.5 * float(np.log(LN_SCALE))).then_inc(c_ones, 1)
            dve.memset(vp[:, :, :, P:KVC], 1.0).then_inc(c_ones, 1)
            dve.wait_ge(tanh_done, 1)
            dve.tensor_scalar(gT[:, :], gam_r[:, :], tanh_g[:, 0:1], None, ALU.mult)
            dve.tensor_scalar(bT[:, :], bet_r[:, :], tanh_g[:, 0:1], None, ALU.mult).then_inc(folded, 1)

            for b in range(NB):
                dve.wait_ge(c_kv, b + 1)
                for i in range(2):
                    dve.bn_stats(cst[0:CTX, 2 * b + i, :], ps[4 + b][0:CTX, i * D:(i + 1) * D]).then_inc(c_st, 1)
            dve.wait_ge(c_st, 2 * NB)
            for n in range(2 * NB):
                dve.bn_aggr(cmv[0:CTX, n, :], cst[0:CTX, n, :]).then_inc(c_ag, 1)
            dve.wait_ge(c_ag, 2 * NB)
            dve.tensor_scalar(cve[0:CTX, :], cmv[0:CTX, :, 1], EPS6, None, ALU.add).then_inc(c_ve, 1)
            dve.wait_ge(c_rs, 1)
            for b in range(NB):
                for i in range(2):
                    n = 2 * b + i
                    dve.tensor_scalar(kvh[:, b, i, :], ps[4 + b][0:CTX, i * D:(i + 1) * D], cmv[0:CTX, n, 0:1],
                                      crs[0:CTX, n:n + 1], ALU.subtract, ALU.mult).then_inc(c_norm, 1)
            halves = [kvh[:, b, i, :] for b in range(NB) for i in range(2)]
            N2 = 2 * NB
            for n, r in enumerate(halves):
                dve.wait_ge(c_norm, N2)
                dve.tensor_tensor(r, r, gam_r[0:CTX, :], ALU.mult).then_inc(c_norm, 1)
            for n, r in enumerate(halves):
                dve.wait_ge(c_norm, 2 * N2)
                dve.tensor_tensor(r, r, bet_r[0:CTX, :], ALU.add).then_inc(c_norm, 1)
            for b in range(NB):
                dve.wait_ge(c_norm, 3 * N2)
                dve.tensor_scalar(kvh[:, b, 0, :], kvh[:, b, 0, :], 0.0, EPS6, ALU.max, ALU.add).then_inc(c_norm, 1)
            for b in range(NB):
                dve.wait_ge(c_norm, 3 * N2 + NB)
                dve.tensor_scalar(kp[:, b, :], kvh[:, b, 0, :], em[:, b:b + 1], None, ALU.mult).then_inc(c_aff, 1)
                dve.wait_ge(c_ones, 2)
                dve.tensor_scalar(vp[:, b, :, 0:P], kvh[:, b, 1, :].rearrange("p (c e) -> p c e", c=DC),
                                  em[:, b:b + 1], None, ALU.mult).then_inc(c_aff, 1)
            for b in range(NB):
                dve.wait_ge(c_kvs, b + 1)
                dve.tensor_tensor(kvs[:, b, :, :], ps[b][:, 0:DC * KVC].rearrange("p (c n) -> p c n", c=DC),
                                  blocks[:, :, :], ALU.mult).then_inc(c_done, 1)
            dve.wait_ge(d_x, 16 * NG)

            def norm(t, k, src, dst, eps):
                st, ag, ve, rs, done = L[t]
                mv, var, r = cmv_of[t], cve_of[t], crs_of[t]
                dve.memset(var[:, 0:2], eps).then_inc(ag, 1)
                for j in range(G):
                    dve.bn_stats(cst_of[t][:, j, :], src(j)).then_inc(st, 1)
                dve.wait_ge(st, G * k + G)
                dve.memset(var[:, 2:G], eps).then_inc(ag, 1)
                for j in range(G):
                    dve.bn_aggr(mv[:, j, :], cst_of[t][:, j, :]).then_inc(ag, 1)
                dve.wait_ge(ag, (G + 2) * (k + 1))
                dve.tensor_tensor(var[:, :], mv[:, :, 1], var[:, :], ALU.add).then_inc(ve, 1)
                dve.wait_ge(rs, k + 1)
                for j in range(G):
                    dve.tensor_scalar(dst(j), src(j), mv[:, j, 0:1], r[:, j:j + 1], ALU.subtract, ALU.mult)\
                       .then_inc(done, 1)

            with dve.Fori(0, NB) as b:
                def x_tile(k, j):
                    return x1[:, bass.ds(G * k + j, 1), :].rearrange("p a d -> p (a d)")

                for s in range(2):
                    k = 2 * b + s
                    norm("lnx", k, lambda j: x_tile(k, j), lambda j: xn[:, j, :], EPS5)
                    dve.wait_ge(a_q, G * k + G)
                    norm("lnq", k, lambda j: ps[4 + j][:, 0:D], lambda j: qn[:, j, :], EPS6)
                for s in range(2):
                    for j in range(G):
                        n = G * (2 * b + s) + j
                        dve.wait_ge(a_att, n + 1)
                        heads = ps[4 + j][:, 0:DC * KVC].rearrange("p (c n) -> p c n", c=DC)
                        z = zinv[:, j, :].rearrange("p (c h) -> p c h", c=DC)
                        dve.tensor_scalar(z, heads[:, :, P:KVC], EPS6, None, ALU.add).then_inc(a_zd, 1)
                        dve.wait_ge(a_zd, n + 1)
                        dve.reciprocal(zinv[:, j, :], zinv[:, j, :]).then_inc(a_z, 1)
                        dve.wait_ge(a_z, n + 1)
                        for c in range(DC):
                            ins = dve.tensor_tensor(
                                att[:, c * XHC:(c + 1) * XHC, s * G + j, :],
                                heads[:, c, 0:P].rearrange("p (h e) -> p h e", h=XHC),
                                z[:, c, :].unsqueeze(2).to_broadcast((P, XHC, XD)), ALU.mult)
                        ins.then_inc(a_an, 1)
                for s in range(2):
                    k = 2 * b + s
                    for j in range(G):
                        dve.wait_ge(a_y, G * k + j + 1)
                        dve.tensor_tensor(yx[:, j, :], ps[4 + j][:, 0:D], db_r[:, :], ALU.add).then_inc(a_yb, 1)
                    dve.wait_ge(a_yb, G * k + G)
                    norm("lno", k, lambda j: yx[:, j, :], lambda j: yx[:, j, :], EPS6)
                    for j in range(G):
                        dve.wait_ge(a_b, G * k + j + 1)
                        dve.tensor_tensor(x_tile(k, j), x_tile(k, j), yx[:, j, :], ALU.add).then_inc(a_x1, 1)
                    dve.wait_ge(a_x1, G * k + G)
                    tile_slot = G * k + b + 1
                    norm("lnf", k, lambda j: x_tile(k, j),
                         lambda j: state[:, bass.ds(tile_slot + j, 1), :].rearrange("p a d -> p (a d)"), EPS5)

            with dve.Fori(0, LAYERS) as l:
                t0 = l * NT
                dve.wait_ge(d_attn_w, (l + 1) * 16 * 5)
                for i in range(2):
                    for a in range(2):
                        ins = dve.tensor_tensor(tab[:, :, i, a, :], tab[:, :, i, a, :],
                                                qks[:, i:i + 1, :].to_broadcast((P, WPB, HD)), ALU.mult)
                        if i == 1 and a == 1:
                            ins.then_inc(tab_ready, 1)
                dve.wait_ge(tab_ready, l + 1)

                def sum_squares(t):
                    dve.wait_ge(squared, 2 * t + 2)
                    dve.tensor_reduce(ssum[:, :], sq[:, :, :].rearrange("p i (h d) -> p (i h) d", h=H), AX.X, ALU.add)\
                       .then_inc(summed, 1)
                    dve.wait_ge(summed, t + 1)
                    dve.tensor_scalar(ssum[:, :], ssum[:, :], 1e-24, None, ALU.max).then_inc(clipped, 1)

                def rotate_queries(t, w):
                    dve.wait_ge(qkT_ps, 2 * t)
                    src = ps[4][:, :]
                    dve.tensor_tensor(rot[:, 0, 0, :].rearrange("p (h d) -> p h d", h=H),
                                      src.rearrange("p (h d) -> p h d", h=H),
                                      tab[:, bass.ds(w, 1), 0, 0, :].to_broadcast((P, H, HD)), ALU.mult)
                    dst = rot[:, 0, 1, :].rearrange("p (h a e) -> p h a e", h=H, a=2)
                    src = src.rearrange("p (h a e) -> p h a e", h=H, a=2)
                    for a in range(2):
                        ins = dve.tensor_tensor(
                            dst[:, :, 1 - a, :], src[:, :, a, :],
                            tab[:, bass.ds(w, 1), 0, 1, a * 32:a * 32 + 32].to_broadcast((P, H, 32)), ALU.mult)
                    ins.then_inc(q_prod, 1)

                def refine_rsqrt(t, u):
                    dve.wait_ge(guessed, t + 1)
                    dve.wait_ge(clipped, t + 1)
                    dve.tensor_tensor(ya[:, :], y0[:, :], y0[:, :], ALU.mult).then_inc(newton, 1)
                    dve.wait_ge(newton, 3 * t + 1)
                    dve.scalar_tensor_tensor(out=yb[:, :], in0=ya[:, :], scalar=-0.5, in1=ssum[:, :],
                                             op0=ALU.mult, op1=ALU.mult).then_inc(newton, 1)
                    dve.wait_ge(newton, 3 * t + 2)
                    dve.scalar_tensor_tensor(out=rn[:, u % 2, :], in0=yb[:, :], scalar=1.5, in1=y0[:, :],
                                             op0=ALU.add, op1=ALU.mult).then_inc(newton, 1)
                    dve.wait_ge(newton, 3 * t + 3)
                    dve.tensor_scalar(rn[:, u % 2, 0:H], rn[:, u % 2, 0:H], 8.0, None, ALU.mult).then_inc(rn_ready, 1)

                def normalise_keys(t, u):
                    dve.wait_ge(k_prod, t)
                    dve.tensor_tensor(khat[:, :].rearrange("p (h d) -> p h d", h=H),
                                      ps[5][:, :].rearrange("p (h d) -> p h d", h=H),
                                      rn[:, u % 2, H:2 * H].unsqueeze(2).to_broadcast((P, H, HD)), ALU.mult)\
                       .then_inc(khat_ready, 1)

                def row_max(t, u, a):
                    dve.wait_ge(scored, 2 * t + a + 1)
                    for i in range(2):
                        ins = dve.tensor_reduce(rowmax[:, u % 2, 4 * a + i:4 * a + i + 3:2],
                                                ps[2 * a + i][:, :].rearrange("p (j k) -> p j k", j=2),
                                                AX.X, ALU.max, negate=True)
                    ins.then_inc(maxed, 1)
                    dve.wait_ge(maxed, 2 * t + a + 1)
                    dve.wait_ge(rn_ready, t + 1)
                    hh = slice(4 * a, 4 * a + 4)
                    dve.tensor_tensor(negmax[:, u % 2, hh], rowmax[:, u % 2, hh], rn[:, u % 2, hh], ALU.mult)\
                       .then_inc(bias_ready, 1)

                def copy_pT_A(t):
                    dve.wait_ge(pT_ps, 2 * t + 1)
                    dve.wait_ge(pv_done, 2 * t)
                    for i in range(2):
                        ins = dve.tensor_copy(pT[:, 0, 2 * i:2 * i + 2, :, :],
                                              ps[i][:, :].rearrange("p (h b q) -> p h b q", h=2, b=2))
                    ins.then_inc(pTA_ready, 1)

                def add_to_state(t, s):
                    dve.wait_ge(wo_done, t + 1)
                    tile = state[:, bass.ds(s, 1), :].rearrange("p a d -> p (a d)")
                    dve.tensor_tensor(tile, ps[6][:, 0:D], tile, ALU.add).then_inc(x_attn, 1)

                def normalise_o(t, u):
                    dve.wait_ge(exped, 8 * t + 8)
                    dve.reciprocal(linv[:, :], lsum[:, u % 2, :]).then_inc(linv_ready, 1)
                    dve.wait_ge(linv_ready, t + 1)
                    dve.wait_ge(pv_done, 2 * t + 2)
                    dve.tensor_tensor(onorm[:, :].rearrange("p (h d) -> p h d", h=H),
                                      ps[7][:, :].rearrange("p (h d) -> p h d", h=H),
                                      linv[:, :].unsqueeze(2).to_broadcast((P, H, HD)), ALU.mult).then_inc(on_ready, 1)

                def step(t, u, w, s_prev, nxt, prev):
                    row_max(t, u, 0)
                    row_max(t, u, 1)
                    if nxt:
                        sum_squares(t + 1)
                        rotate_queries(t + 1, w)
                        refine_rsqrt(t + 1, u + 1)
                        normalise_keys(t + 1, u + 1)
                    copy_pT_A(t)
                    if prev:
                        add_to_state(t - 1, s_prev)
                    normalise_o(t, u)

                sum_squares(t0)
                rotate_queries(t0, 0)
                refine_rsqrt(t0, 0)
                normalise_keys(t0, 0)
                for u in range(G):
                    step(t0 + u, u, (u + 1) % WPB, slot(0, u - 1), True, u > 0)
                with dve.Fori(1, NG - 1) as k:
                    for u in range(G):
                        s_prev = slot(k, u - 1) if u else slot(k - 1, G - 1)
                        step(t0 + G * k + u, u, (G * k + u + 1) & (WPB - 1), s_prev, True, True)
                for u in range(G):
                    s_prev = slot(NG - 1, u - 1) if u else slot(NG - 2, G - 1)
                    step(t0 + G * (NG - 1) + u, u, (G * (NG - 1) + u + 1) % WPB, s_prev, u < G - 1, True)
                add_to_state(t0 + NT - 1, slot(NG - 1, G - 1))

                def group_norm(g):
                    base = l * NG + g
                    dve.wait_ge(d_hf, 64 * (base + 1))
                    for j in range(G):
                        dve.bn_stats(fst[:, j, 0, :], hf[:, j, :]).then_inc(f_st, 1)
                    dve.wait_ge(f_st, G * (base + 1))
                    dve.memset(fve[:, :], EPS5).then_inc(f_mv, 1)
                    for j in range(G):
                        dve.bn_aggr(fmv[:, j, :], fst[:, j, 0, :]).then_inc(f_mv, 1)
                    dve.wait_ge(f_mv, (G + 1) * (base + 1))
                    dve.tensor_tensor(fve[:, :], fmv[:, :, 1], fve[:, :], ALU.add).then_inc(f_ve, 1)
                    dve.wait_ge(f_rs, base + 1)
                    dve.wait_ge(f_hT, base * DC)
                    for j in range(G):
                        dve.tensor_scalar(hn[:, j, :], hf[:, j, :], fmv[:, j, 0:1], frs[:, j:j + 1],
                                          ALU.subtract, ALU.mult).then_inc(f_hn, 1)

                def gate(g):
                    base = l * NG + g
                    for m in range(NM):
                        dve.wait_ge(f_gel, base * NM + m + 1)
                        dve.wait_ge(f_w1, base * 2 * NM + 2 * m + 2)
                        dve.wait_ge(f_w2, l * NT + G * g)
                        dve.scalar_tensor_tensor(out=hid[0:MW[m], m, :], in0=ps[3 + 2 * (m % 2)][0:MW[m], :],
                                                 scalar=b1c[0:MW[m], 0, m:m + 1], in1=gel[0:MW[m], m % 2, :],
                                                 op0=ALU.add, op1=ALU.mult).then_inc(f_hid, 1)

                def add_group(g):
                    for j in range(G):
                        dve.wait_ge(f_w2, l * NT + G * g + j + 1)
                        tile = state[:, bass.ds(slot(g, j), 1), :].rearrange("p a d -> p (a d)")
                        dve.tensor_tensor(tile, ps[6 + j % 2][:, 0:D], tile, ALU.add).then_inc(f_x, 1)

                dve.wait_ge(d_ffn_w, (l + 1) * 16 * 10)
                group_norm(0)
                with dve.Fori(0, NG - 1) as g:
                    gate(g)
                    group_norm(g + 1)
                    add_group(g)
                gate(NG - 1)
                add_group(NG - 1)

            with dve.Fori(0, NG) as g:
                dve.wait_ge(x_ready, LAYERS * NT + G * g + G)
                s = slot(g, 0)
                dve.scalar_tensor_tensor(out=x1[:, bass.ds(G * g, G), :], in0=state[:, bass.ds(s, G), :],
                                         scalar=tanh_g[:, 1:2], in1=x1[:, bass.ds(G * g, G), :],
                                         op0=ALU.mult, op1=ALU.add).then_inc(summed_out, 1)


_INS = ["x", "ctx_1024", "mask_BxS2_ff1", "g_xattn", "g_ffn", "L0_xattn_wq", "L0_xattn_wk", "L0_xattn_wv",
        "L0_xattn_ln_gamma", "L0_xattn_ln_beta", "L0_xattn_dense_w", "L0_xattn_dense_b",
        "L0_ffn_wqkv", "L0_ffn_q_scale", "L0_ffn_k_scale", "L0_ffn_wo", "L0_ffn_ln_g", "L0_ffn_ln_b",
        "L0_ffn_w1", "L0_ffn_b1", "L0_ffn_w2", "L0_ffn_b2"]


def kernel(**inputs):
    import concourse.bacc as bacc
    from concourse.bass_utils import run_bass_kernel_spmd

    nc = bacc.Bacc("TRN2", target_bir_lowering=False, num_devices=1)
    arrays, args = {}, []

    def put(name, a):
        a = np.ascontiguousarray(a)
        arrays[name] = a
        args.append(nc.dram_tensor(name, a.shape, mybir.dt.from_np(a.dtype), kind="ExternalInput").ap())

    for name in _INS:
        put(f"in_{name}_dram", np.asarray(inputs[name]))
    put("tables_dram", position_tables())
    put("masks_dram", masks())
    put("blocks_dram", block_diagonal())
    put("ident_dram", np.eye(P, dtype=np.float32))
    out = nc.dram_tensor("out_dram", (NB, S, D), F32, kind="ExternalOutput").ap()
    program(nc, *args, out)
    r = run_bass_kernel_spmd(nc, [arrays], core_ids=[0])
    return r.results[0]["out_dram"]
```

```python
from contextlib import ExitStack

import numpy as np

import concourse.bass as bass
from concourse import mybir
from concourse.alu_op_type import AluOpType as ALU

ACT = mybir.ActivationFunctionType
AX = mybir.AxisListType
F32 = mybir.dt.float32
BF16 = mybir.dt.bfloat16
F32R = mybir.dt.float32r

P = 128
D = 256
DC = D // P
NB, S = 4, 1024
WPB = S // P
NT = NB * WPB
G = 4
NG = NT // G
SLOTS = WPB + 1
CTX = 77
XH, XD = 16, 16
XHC = P // XD
KVC = P + XHC
LAYERS = 2
H, HD = 8, 64
INNER = H * HD
HP = H // 2
HID = 682
MC = 114
NM = 6
MW = [MC] * (NM - 1) + [HID - MC * (NM - 1)]
AW = DC * 3 * INNER + HP * D
PIECES = 8
MASKED = -1e30
LN_SCALE = 2.0 ** 20
EPS5, EPS6 = 1e-5, 1e-6


def position_tables():
    half = np.arange(0, HD, 2, dtype=np.float32)
    inv = (np.float32(1.0) / np.float32(10000.0) ** (half / np.float32(HD))).astype(np.float32)
    t = np.arange(S, dtype=np.float32)
    freqs = (t[:, None] * inv[None, :]).astype(np.float32)
    freqs = np.concatenate([freqs, freqs], -1)
    base = ((half + np.float32(0.4 * HD)) / np.float32(1.4 * HD)).astype(np.float32)
    power = ((t - S // 2) / np.float32(64.0)).astype(np.float32)
    scale = (base[None, :] ** power[:, None]).astype(np.float32)
    scale = np.concatenate([scale, scale], -1)
    cos, sin = np.cos(freqs), np.sin(freqs)
    sign = np.concatenate([np.ones(HD // 2), -np.ones(HD // 2)]).astype(np.float32)
    t4 = np.stack([np.stack([cos * scale, sin * scale * sign], 1),
                   np.stack([cos / scale, sin / scale * sign], 1)], 1).astype(np.float32)
    return np.ascontiguousarray(t4.reshape(WPB, P, 2, 2, HD).transpose(1, 0, 2, 3, 4))


def block_order(u):
    return (1, 0) if u else (0, 1)


def masks():
    q, k = np.arange(P)[:, None], np.arange(P)[None, :]
    m = np.zeros((P, 2, G, 2, P), np.float32)
    for half in range(2):
        for u in range(G):
            cur, prev = block_order(u)
            m[:, half, u, cur] = np.where(k > q, MASKED, 0.0)
            m[:, half, u, prev] = MASKED if half == 0 and u == 0 else np.where(k < q, MASKED, 0.0)
    return m


def block_diagonal():
    f = np.arange(P)[:, None] // XD
    c = np.concatenate([np.arange(P) // XD, np.arange(XHC)])[None, :]
    return np.repeat((f == c).astype(np.float32)[:, None, :], DC, 1)


def program(nc, x, ctx_in, mask_in, g_xattn, g_ffn, wq, wk, wv, xg, xb, dw, db,
            wqkv, q_scale, k_scale, wo, ln_g, ln_b, w1, b1, w2, b2,
            tables_in, masks_in, blocks_in, ident_in, out):
    ctx = ExitStack()
    with ctx:
        bottom = -(-nc.sbuf_base // 64) * 64
        place = {"": bottom}

        def sb(name, shape, dt=F32, over=None, skip=0):
            words = int(np.prod(shape[1:])) * (2 if dt == BF16 else 4) // 4
            place[name] = place[over] + 4 * skip if over else place[""]
            if not over:
                place[""] += -(-words * 4 // 64) * 64
            return nc.alloc_sbuf_tensor_at(name, shape, dt, offset=place[name])

        def sem(name):
            return ctx.enter_context(nc.semaphore(name))

        state = sb("state", [P, NB * SLOTS, D])
        ident = sb("ident", [P, P])
        identb = sb("identb", [P, P], BF16)
        tanh_g = sb("tanh_g", [P, 2])
        attn_hi_sb = sb("attn_hi_sb", [P, AW], F32R)
        attn_lo_sb = sb("attn_lo_sb", [P, AW], F32R)
        attn_w = sb("attn_w", [P, AW], over="attn_lo_sb")
        w1_hi, w1_lo = (sb(n, [P, DC * 2 * HID], F32R) for n in ("w1_hi", "w1_lo"))
        w1_flat = sb("w1_flat", [P, DC * 2 * HID], over="w1_lo")
        w2_s = [sb(n, [MC, NM, D], F32R) for n in ("w2_hi", "w2_lo")]
        w2_in = sb("w2_in", [MC, NM, D], over="w2_lo")

        def attn_views(w):
            return (w[:, 0:DC * 3 * INNER].rearrange("p (c n) -> p c n", c=DC),
                    w[:, DC * 3 * INNER:AW].rearrange("p (c n) -> p c n", c=HP))

        def w1_view(w):
            return w[:, :].rearrange("p (c n) -> p c n", c=DC)

        wqkv_in, wo_in = attn_views(attn_w)
        wqkv_s, wo_s = zip(attn_views(attn_hi_sb), attn_views(attn_lo_sb))
        w1_in, w1_s = w1_view(w1_flat), (w1_view(w1_hi), w1_view(w1_lo))
        x1 = sb("x1", [P, NT, D], over="attn_hi_sb")
        lnc = sb("lnc", [P, 2, DC])
        b1c = sb("b1c", [MC, 2, NM])
        b2r = sb("b2r", [P, D])
        qks = sb("qks", [P, 2, HD])
        tab = sb("tab", [P, WPB, 2, 2, HD])
        mask_sb = sb("mask_sb", [P, 2, G, 2, P], BF16)
        hs = sb("hs", [P, 2, D])
        hT = sb("hT", [P, 2, DC, P], F32R)
        probs = sb("probs", [P, 2, 4, 2 * P])
        pT = sb("pT", [P, 2, 4, 2, P])
        kH = sb("kH", [P, 2, HP, G, P], F32R)
        kL = sb("kL", [P, HP, G, P], F32R)
        vring = sb("vring", [P, G, INNER])
        sq = sb("sq", [P, 2, INNER])
        ssum = sb("ssum", [P, 2 * H])
        lns = sb("lns", [P, 2 * H])
        y0 = sb("y0", [P, 2 * H])
        ya = sb("ya", [P, 2 * H])
        yb = sb("yb", [P, 2 * H])
        rn = sb("rn", [P, 2, 2 * H])
        khat = sb("khat", [P, INNER])
        rot = sb("rot", [P, 2, 2, INNER])
        qS = sb("qS", [P, 2, HP, P], F32R)
        negmax = sb("negmax", [P, 2, H])
        rowmax = sb("rowmax", [P, 2, H])
        lsum = sb("lsum", [P, 2, H])
        linv = sb("linv", [P, H])
        onorm = sb("onorm", [P, INNER])
        oT = sb("oT", [P, 2, HP, P], F32R)
        hf = sb("hf", [P, G, D])
        fst = sb("fst", [P, G, 2, 6])
        fmv = sb("fmv", [P, G, 2])
        fve = sb("fve", [P, G])
        frs = sb("frs", [P, G])
        hn = sb("hn", [P, G, D], over="rot")
        hnTl = sb("hnTl", [P, DC, G * P], F32R, over="rot", skip=G * D)
        hnT = sb("hnT", [P, DC, G * P], over="hnTl")
        hnTh = sb("hnTh", [P, DC, G * P], F32R, over="sq")
        hidl = sb("hidl", [P, NM, G * P], F32R, over="probs")
        hid = sb("hid", [P, NM, G * P], over="probs")
        hidh = sb("hidh", [P, NM, G * P], F32R, over="probs", skip=NM * G * P)
        gel = sb("gel", [P, 2, G * P], over="probs", skip=2 * NM * G * P)
        one = sb("one", [P, 1])
        fence = sb("fence", [P, 1])
        minus_half = sb("minus_half", [P, G])
        half_log = sb("half_log", [P, 1])

        ps = [ctx.enter_context(nc.psum_tensor(f"ps{i}", [P, 512], F32)) for i in range(8)]

        xw = sb("xw", [P, DC, 3 * D], over="w1_hi")
        dw_sb = sb("dw_sb", [P, DC, D], over="w1_hi", skip=DC * 3 * D)
        gam_r = sb("gam_r", [P, D])
        bet_r = sb("bet_r", [P, D])
        db_r = sb("db_r", [P, D])
        gT = sb("gT", [P, D])
        bT = sb("bT", [P, D])
        xgc = sb("xgc", [P, 2, DC])
        em = sb("em", [CTX, NB])
        blocks = sb("blocks", [P, DC, KVC])
        kvs = sb("kvs", [P, NB, DC, KVC], over="kH")
        cst = sb("cst", [P, 2 * G, 6])
        cmv = sb("cmv", [P, 2 * G, 2])
        cve = sb("cve", [P, 2 * G])
        crs = sb("crs", [P, 2 * G])
        eps_row = sb("eps_row", [P, D])
        mh8 = sb("mh8", [P, 2 * G])
        norms = ("lnx", "lnq", "lno0", "lno1", "lnf0", "lnf1")
        cst_of, cmv_of, cve_of, crs_of, cnm_of = (
            {t: sb(f"{t}_{w}", [P, *shape]) for t in norms}
            for w, shape in (("st", (G, 6)), ("mv", (G, 2)), ("ve", (G,)), ("rs", (G,)), ("nm", (G,))))
        minus_one = sb("minus_one", [P, G])
        kvh = sb("kvh", [CTX, NB, 2, D], over="vring")
        kp = sb("kp", [CTX, NB, D], over="sq")
        vp = sb("vp", [CTX, NB, DC, KVC], over="pT")
        zinv = sb("zinv", [P, G, XH])
        ctx_sb = sb("ctx_sb", [CTX, NB, D], over="hf")
        ctxT = sb("ctxT", [P, DC, NB, P], over="kL")
        xn = sb("xn", [P, G, D], over="probs")
        xnT = sb("xnT", [P, 2, DC, 2 * P], over="probs", skip=G * D)
        qn = sb("qn", [P, G, D], over="hf")
        reluT = sb("reluT", [P, DC, WPB, 2, S // 16], over="rot")
        qTs = sb("qTs", [P, DC, WPB, P], over="vring")
        att = sb("att", [P, XH, WPB, XD], over="pT")
        attT = sb("attT", [P, DC, S], over="kH", skip=2048)
        yx = [sb("yx0", [P, G, D], over="kL"), sb("yx1", [P, G, D], over="kL", skip=G * D)]

        d_const = sem("d_const"); d_x = sem("d_x"); d_x_first = [sem("d_x_0"), sem("d_x_1")]; d_small = sem("d_small")
        d_attn_w = sem("d_attn_w"); d_ffn_w = sem("d_ffn_w"); d_hs = sem("d_hs"); d_hf = sem("d_hf")
        d_out = sem("d_out")
        rings_zeroed = sem("rings_zeroed")
        zeroed = sem("zeroed"); consts_set = sem("consts_set"); tanh_done = sem("tanh_done")
        folded = sem("folded")
        c_T = sem("c_T"); c_Tc = sem("c_Tc"); c_kv = sem("c_kv"); c_st = sem("c_st"); c_ag = sem("c_ag")
        c_ve = sem("c_ve"); c_rs = sem("c_rs"); c_norm = sem("c_norm"); c_aff = sem("c_aff")
        c_kvs = sem("c_kvs"); c_done = sem("c_done"); c_ones = sem("c_ones")
        L = {t: [sem(f"{t}_{w}") for w in ("stats", "moments", "var", "rstd", "normed")]
             for t in norms}
        x_ready = sem("x_ready")
        L["lnf0"][4] = L["lnf1"][4] = x_ready
        L["lno0"][4] = L["lno1"][4] = sem("lno_scaled")
        n_neg = {t: sem(f"{t}_neg") for t in ("lnx", "lnq")}; n_rs = {t: sem(f"{t}_inverse") for t in ("lnx", "lnq")}
        a_xb = sem("a_xb")
        a_xT = sem("a_xT"); a_xTc = sem("a_xTc"); a_q = sem("a_q"); a_qT = sem("a_qT")
        a_relu = sem("a_relu"); a_qp = sem("a_qp"); a_att = sem("a_att"); a_zd = sem("a_zd"); a_z = sem("a_z")
        a_an = sem("a_an"); a_aT = sem("a_aT"); a_aTc = sem("a_aTc"); a_y = sem("a_y"); a_yb = sem("a_yb")
        a_g = sem("a_g"); a_b = sem("a_b"); a_x1 = sem("a_x1")
        tab_sin = sem("tab_sin"); tab_ready = sem("tab_ready")
        hT_ps = sem("hT_ps"); hT_ready = sem("hT_ready"); proj_done = sem("proj_done"); v_ready = sem("v_ready")
        squared = sem("squared"); summed = sem("summed"); clipped = sem("clipped"); logged = sem("logged")
        guessed = sem("guessed"); newton = sem("newton"); rn_ready = sem("rn_ready"); q_prod = sem("q_prod")
        khat_ready = sem("khat_ready"); k_prod = sem("k_prod"); qkT_ps = sem("qkT_ps"); q_hi = sem("q_hi"); q_lo = sem("q_lo"); k_hi = sem("k_hi"); k_lo = sem("k_lo")
        scored = sem("scored"); maxed = sem("maxed"); bias_ready = sem("bias_ready"); exped = sem("exped")
        pT_ps = sem("pT_ps"); pT0_ready = sem("pT0_ready"); pT1_ready = sem("pT1_ready"); pTB_ready = sem("pTB_ready"); pv_done = sem("pv_done")
        linv_ready = sem("linv_ready"); on_ready = sem("on_ready"); oT_ps = sem("oT_ps"); oT_ready = sem("oT_ready")
        wo_done = sem("wo_done"); x_attn = sem("x_attn")
        f_st = sem("f_st"); f_mv = sem("f_mv"); f_ve = sem("f_ve"); f_rs = sem("f_rs"); f_hn = sem("f_hn")
        f_hT = sem("f_hT"); f_hTc = sem("f_hTc"); f_w1 = sem("f_w1"); f_gel = sem("f_gel"); f_hid = sem("f_hid")
        f_w2 = sem("f_w2"); f_x = sem("f_x")
        summed_out = sem("summed_out")
        attn_hi = sem("attn_hi"); attn_lo = sem("attn_lo"); attn_lo_pool = sem("attn_lo_pool")
        w1_rounded = sem("w1_rounded"); w1_split = sem("w1_split"); w2_rounded = sem("w2_rounded"); w2_split = sem("w2_split"); d_x1 = [sem("d_x1_0"), sem("d_x1_1")]; d_x1_back = sem("d_x1_back")
        hTlo_ready = sem("hTlo_ready"); oTlo_ready = sem("oTlo_ready")
        f_hnhi = sem("f_hnhi"); f_hnlo = sem("f_hnlo"); f_hidhi = sem("f_hidhi"); f_hidlo = sem("f_hidlo")

        block = ctx.enter_context(nc.Block())

        N_CONST = 15
        HALF_SPLIT = ((0, 0), (0, 1), (1, 0))

        def f32(ap):
            return ap.bitcast(F32)

        def slot(k, u):
            v = G * k + (k >> 1) + u + 1
            return v if isinstance(v, int) else v.with_bounds(min_val=1, max_val=NB * SLOTS - G + u)

        def attn_parts():
            return [tuple(w[:, :, i * INNER:(i + 1) * INNER] for w in (wqkv_in, *wqkv_s)) for i in range(3)]\
                + [(wo_in, *wo_s)]

        x_view = x.rearrange("b (w p) d -> p (b w) d", p=P)
        out_view = out.rearrange("b (w p) d -> p (b w) d", p=P)

        @block.sync
        def _(sp):
            def load_x(k):
                sp.dma_start(state[:, slot(k, 0):slot(k, 0) + G, :], x_view[:, k * G:(k + 1) * G, :])\
                  .then_inc(d_x_first[k] if k < 2 else d_x, 16)

            sp.dma_start(ctx_sb[:, :, :], ctx_in.rearrange("b p d -> p b d")).then_inc(d_const, 16)
            sp.dma_start(ident[:, :], ident_in).then_inc(d_const, 16)
            for i, w in enumerate((wq, wk, wv)):
                sp.dma_start(xw[:, :, i * D:(i + 1) * D], w.rearrange("(c p) n -> p c n", p=P)).then_inc(d_const, 16)
            for k in range(2):
                load_x(k)
            sp.dma_start(dw_sb[:, :, :], dw.rearrange("(c p) n -> p c n", p=P)).then_inc(d_const, 16)
            sp.dma_start(blocks[:, :, :], blocks_in).then_inc(d_const, 16)
            for r, v in ((gam_r, xg), (bet_r, xb), (db_r, db)):
                sp.dma_start(r[:, :], v.partition_broadcast(P)).then_inc(d_const, 16)
            sp.dma_start(tanh_g[:, 0:1], g_xattn.partition_broadcast(P)).then_inc(d_const, 16)
            sp.dma_start(tanh_g[:, 1:2], g_ffn.partition_broadcast(P)).then_inc(d_const, 16)
            with nc.allow_non_contiguous_dma(reason="columns of small vectors"):
                sp.dma_start(xgc[:, 0, :], xg.rearrange("(c p) -> p c", p=P)).then_inc(d_const, 16)
                sp.dma_start(xgc[:, 1, :], xb.rearrange("(c p) -> p c", p=P)).then_inc(d_const, 16)
                sp.dma_start(em[:, :], mask_in.rearrange("b p -> p b")).then_inc(d_const, 16)
            for k in range(2, NG):
                load_x(k)

            def load_attn_weights(l):
                sp.dma_start(wqkv_in, wqkv[l].rearrange("(c p) n -> p c n", p=P)).then_inc(d_attn_w, 16)
                sp.dma_start(wo_in, wo[l].rearrange("(c p) n -> p c n", p=P)).then_inc(d_attn_w, 16)
                sp.dma_start(tab[:, :, :, :, :], tables_in).then_inc(d_attn_w, 16)
                sp.dma_start(qks[:, 0, :], q_scale[l].partition_broadcast(P)).then_inc(d_attn_w, 16)
                sp.dma_start(qks[:, 1, :], k_scale[l].partition_broadcast(P)).then_inc(d_attn_w, 16)

            def load_ffn_weights(l):
                sp.dma_start(w1_in, w1[l].rearrange("(c p) n -> p c n", p=P)).then_inc(d_ffn_w, 16)
                sp.dma_start(w2_in[0:MC, 0:NM - 1, :], w2[l][0:MC * (NM - 1), :].rearrange("(m p) n -> p m n", p=MC))\
                  .then_inc(d_ffn_w, 16)
                sp.dma_start(w2_in[0:MW[-1], NM - 1, :], w2[l][MC * (NM - 1):HID, :]).then_inc(d_ffn_w, 16)
                sp.dma_start(b2r[:, :], b2[l].partition_broadcast(P)).then_inc(d_ffn_w, 16)
                with nc.allow_non_contiguous_dma(reason="columns of small vectors"):
                    sp.dma_start(lnc[:, 0, :], ln_g[l].rearrange("(c p) -> p c", p=P)).then_inc(d_ffn_w, 16)
                    sp.dma_start(lnc[:, 1, :], ln_b[l].rearrange("(c p) -> p c", p=P)).then_inc(d_ffn_w, 16)
                    for a in range(2):
                        v = b1[l][a * HID:(a + 1) * HID]
                        sp.dma_start(b1c[:, a, 0:NM - 1], v[0:MC * (NM - 1)].rearrange("(m p) -> p m", p=MC))\
                          .then_inc(d_ffn_w, 16)
                        sp.dma_start(b1c[0:MW[-1], a, NM - 1:NM], v[MC * (NM - 1):HID].rearrange("(m p) -> p m", m=1))\
                          .then_inc(d_ffn_w, 16)

            def load_shifted(dst, s, s_before, n, done):
                half = slice(P, D)
                sp.dma_start(dst[:, :, 0:P], state[:, bass.ds(s, n), 0:P]).then_inc(done, 16)
                sp.dma_start(dst[1:P - 1, :, half], state[0:P - 2, bass.ds(s, n), half]).then_inc(done, 16)
                sp.dma_start(dst[P - 1:P, :, half], state[P - 2:P - 1, bass.ds(s, n), half]).then_inc(done, 16)
                sp.dma_start(dst[0:1, :, half], state[P - 1:P, bass.ds(s_before, n), half]).then_inc(done, 16)

            load_ffn_weights(0)
            load_attn_weights(0)
            for k in range(NG):
                sp.wait_ge(a_x1, G * (k + 1))
                sp.dma_start(out_view[:, k * G:(k + 1) * G, :], yx[k % 2][:, :, :]).then_inc(d_x1[k % 2], 16)
            sp.wait_ge(zeroed, 1)
            def load_pair(tile, first, before):
                sp.wait_ge(x_ready, tile + 2)
                sp.wait_ge(hT_ps, tile)
                load_shifted(hs, first, before, 2, d_hs)

            def load_group(tile, first, before):
                sp.wait_ge(x_attn, tile + G)
                sp.wait_ge(f_hn, tile)
                load_shifted(hf, first, before, G, d_hf)

            load_pair(0, 1, 0)
            for l in range(LAYERS):
                load_pair(l * NT + 2, 3, 2)
                if l:
                    sp.wait_ge(x_ready, (l + 1) * NT)
                    load_ffn_weights(l)
                with sp.Fori(l * NT + 4, (l + 1) * NT, 2) as tile:
                    first = sp.snap((tile + (tile >> 3) + 1 - l * NB * SLOTS).with_bounds(min_val=1, max_val=NB * SLOTS - 2))
                    load_pair(tile, first, sp.snap(first - 1))
                load_group(l * NT, 1, 0)
                sp.wait_ge(x_attn, (l + 1) * NT)
                load_group(l * NT + G, G + 1, G)
                if l + 1 < LAYERS:
                    load_attn_weights(l + 1)
                else:
                    for k in range(NG):
                        sp.dma_start(x1[:, k * G:(k + 1) * G, :], out_view[:, k * G:(k + 1) * G, :])\
                          .then_inc(d_x1_back, 16)
                with sp.Fori(l * NT + 2 * G, (l + 1) * NT, G) as tile:
                    first = sp.snap((tile + (tile >> 3) + 1 - l * NB * SLOTS).with_bounds(min_val=1, max_val=NB * SLOTS - G))
                    load_group(tile, first, sp.snap(first - 1))
                if l + 1 < LAYERS:
                    load_pair((l + 1) * NT, 1, 0)
            with sp.Fori(0, NG) as g:
                sp.wait_ge(summed_out, g + 1)
                sp.dma_start(out_view[:, bass.ds(g * G, G), :], x1[:, bass.ds(g * G, G), :]).then_inc(d_out, 16)
            sp.wait_ge(d_out, 16 * NG)

        @block.gpsimd
        def _(pool):
            pool.dma_start(mask_sb[:, :, :, :, :], masks_in).then_inc(d_small, 16)
            pool.dma_start(identb[:, :], ident_in).then_inc(d_small, 16)
            pool.memset(one[:, :], 1.0)
            pool.memset(minus_one[:, :], -1.0)
            pool.memset(minus_half[:, :], -0.5)
            pool.memset(eps_row[:, :], EPS6)
            pool.memset(mh8[:, :], -0.5).then_inc(consts_set, 1)
            pool.memset(state[:, :, :].rearrange("p (b s) d -> p b s d", b=NB)[:, :, 0, :], 0.0).then_inc(zeroed, 1)
            pool.wait_ge(consts_set, 1)

            pool.wait_ge(c_ve, 1)
            pool.tensor_tensor(crs[0:CTX, :], cve[0:CTX, :], mh8[0:CTX, :], ALU.pow).then_inc(c_rs, 1)

            def rstd(t, k):
                pool.wait_ge(L[t][2], k + 1)
                pool.tensor_tensor(crs_of[t][:, :], cve_of[t][:, :], mh8[:, 0:G], ALU.pow).then_inc(L[t][3], 1)

            def rstd_and_shift(t, k):
                pool.wait_ge(L[t][2], k + 1)
                pool.wait_ge(L[t][4], G * k)
                pool.tensor_tensor(crs_of[t][:, :], cve_of[t][:, :], mh8[:, 0:G], ALU.pow).then_inc(n_rs[t], 1)
                pool.tensor_tensor(cnm_of[t][:, :], cmv_of[t][:, :, 0], minus_one[:, :], ALU.mult).then_inc(n_neg[t], 1)
                pool.wait_ge(n_rs[t], k + 1)
                pool.wait_ge(n_neg[t], k + 1)
                pool.tensor_tensor(cnm_of[t][:, :], cnm_of[t][:, :], crs_of[t][:, :], ALU.mult).then_inc(L[t][3], 1)

            def add_beta(k):
                pool.wait_ge(folded, 1)
                for j in range(G):
                    pool.wait_ge(L["lnx"][4], G * k + j + 1)
                    tile = state[:, bass.ds(slot(k, j), 1), :].rearrange("p a d -> p (a d)")
                    pool.tensor_tensor(tile, tile, bT[:, :], ALU.add).then_inc(a_xb, 1)

            for k in range(2):
                rstd_and_shift("lnx", k)
                rstd_and_shift("lnq", k)
                add_beta(k)

            def sequence(b, nxt):
                k = 2 * b + 2
                if nxt:
                    rstd_and_shift("lnx", k)
                    rstd_and_shift("lnq", k)
                    rstd_and_shift("lnx", k + 1)
                    add_beta(k)
                rstd("lno0", b)
                rstd("lno1", b)
                rstd("lnf0", b)
                if nxt:
                    rstd_and_shift("lnq", k + 1)
                rstd("lnf1", b)
                if nxt:
                    add_beta(k + 1)

            with pool.Fori(0, NB - 1) as b:
                sequence(b, True)
            sequence(NB - 1, False)

            for s in range(2):
                pool.wait_ge(d_x1[s], 16 * NB)
            with pool.Fori(0, LAYERS) as l:
                for i, (loaded, hi, lo) in enumerate(attn_parts()[2:4]):
                    pool.wait_ge(attn_hi, 4 * l + i + 3)
                    pool.tensor_tensor(lo, loaded, f32(hi), ALU.subtract).then_inc(attn_lo_pool, 1)
                pool.wait_ge(x_ready, (l + 1) * NT)
                pool.tensor_tensor(fence[:, :], one[:, :], one[:, :], ALU.mult)
                for i in range(2):
                    pool.memset(f32(kH[:, i, :, G - 1, :]), 0.0).then_inc(rings_zeroed, 1)
                pool.memset(f32(kL[:, :, G - 1, :]), 0.0).then_inc(rings_zeroed, 1)
                pool.memset(vring[:, G - 1, :], 0.0).then_inc(rings_zeroed, 1)

                def rotate_keys(t, w):
                    pool.wait_ge(khat_ready, t + 1)
                    pool.wait_ge(qkT_ps, 2 * t)
                    src = khat[:, :].rearrange("p (h d) -> p h d", h=H)
                    pool.tensor_tensor(rot[:, 1, 0, :].rearrange("p (h d) -> p h d", h=H), src,
                                       tab[:, bass.ds(w, 1), 1, 0, :].to_broadcast((P, H, HD)), ALU.mult)
                    dst = rot[:, 1, 1, :].rearrange("p (h a e) -> p h a e", h=H, a=2)
                    src = khat[:, :].rearrange("p (h a e) -> p h a e", h=H, a=2)
                    for a in range(2):
                        ins = pool.tensor_tensor(
                            dst[:, :, 1 - a, :], src[:, :, a, :],
                            tab[:, bass.ds(w, 1), 1, 1, a * 32:a * 32 + 32].to_broadcast((P, H, 32)), ALU.mult)
                    ins.then_inc(k_prod, 1)

                def split_w1(k):
                    width = DC * 2 * HID // PIECES
                    piece = bass.ds(k * width, width)
                    pool.wait_ge(d_ffn_w, (l + 1) * 16 * 10)
                    pool.tensor_tensor(w1_hi[:, piece], w1_flat[:, piece], one[:, 0:1].to_broadcast((P, width)), ALU.mult)\
                        .then_inc(w1_rounded, 1)
                    pool.wait_ge(w1_rounded, l * PIECES + k + 1)
                    pool.tensor_tensor(fence[:, :], one[:, :], one[:, :], ALU.mult)
                    pool.tensor_tensor(w1_lo[:, piece], w1_flat[:, piece], f32(w1_hi[:, piece]), ALU.subtract)\
                        .then_inc(w1_split, 1)

                def split_w2():
                    parts = ((slice(0, MC), slice(0, NM - 1)), (slice(0, MW[-1]), slice(NM - 1, NM)))
                    for rows, m in parts:
                        width = (m.stop - m.start) * D
                        pool.tensor_tensor(w2_s[0][rows, m, :].rearrange("p m n -> p (m n)"),
                                           w2_in[rows, m, :].rearrange("p m n -> p (m n)"),
                                           one[rows, 0:1].to_broadcast((rows.stop, width)), ALU.mult).then_inc(w2_rounded, 1)
                    for i, (rows, m) in enumerate(parts):
                        pool.wait_ge(w2_rounded, 2 * l + i + 1)
                        pool.tensor_tensor(w2_s[1][rows, m, :], w2_in[rows, m, :], f32(w2_s[0][rows, m, :]),
                                           ALU.subtract).then_inc(w2_split, 1)

                pool.wait_ge(tab_ready, l + 1)
                rotate_keys(l * NT, 0)
                with pool.Fori(0, NG - 1) as k:
                    for u in range(G):
                        rotate_keys(l * NT + G * k + u + 1, (G * k + u + 1) & (WPB - 1))
                        if u == 1:
                            split_w1(k)
                split_w1(PIECES - 1)
                split_w2()
                for u in range(G - 1):
                    rotate_keys(l * NT + G * (NG - 1) + u + 1, (G * (NG - 1) + u + 1) % WPB)

                def group_rstd(g):
                    pool.wait_ge(f_ve, l * NG + g + 1)
                    pool.tensor_tensor(frs[:, :], fve[:, :], minus_half[:, :], ALU.pow).then_inc(f_rs, 1)

                def add_b2(g):
                    for j in range(G):
                        pool.wait_ge(f_x, l * NT + G * g + j + 1)
                        tile = state[:, bass.ds(slot(g, j), 1), :].rearrange("p a d -> p (a d)")
                        pool.tensor_tensor(tile, tile, b2r[:, :], ALU.add).then_inc(x_ready, 1)

                def split_hnT(g):
                    for c in range(DC):
                        pool.wait_ge(f_hnhi, (l * NG + g) * DC + c + 1)
                        pool.tensor_tensor(hnTl[:, c, :], hnT[:, c, :], f32(hnTh[:, c, :]), ALU.subtract)\
                            .then_inc(f_hnlo, 1)

                def split_hid(g, nxt):
                    for m in range(NM):
                        pool.wait_ge(f_hidhi, (l * NG + g) * NM + m + 1)
                        pool.tensor_tensor(hidl[0:MW[m], m, :], hid[0:MW[m], m, :], f32(hidh[0:MW[m], m, :]),
                                           ALU.subtract).then_inc(f_hidlo, 1)
                        if nxt and m == 1:
                            group_rstd(g + 1)

                group_rstd(0)
                split_hnT(0)
                with pool.Fori(0, NG - 1) as g:
                    split_hid(g, True)
                    split_hnT(g + 1)
                    add_b2(g)
                split_hid(NG - 1, False)
                add_b2(NG - 1)

        @block.scalar
        def _(act):
            act.wait_ge(d_const, 16 * N_CONST)
            act.activation(tanh_g[:, :], tanh_g[:, :], ACT.Tanh).then_inc(tanh_done, 1)

            for b in range(NB):
                act.wait_ge(c_T, b + 1)
                act.activation(ctxT[:, :, b, 0:CTX], ps[b][:, 0:D].rearrange("p (c t) -> p c t", c=DC)[:, :, 0:CTX],
                               ACT.Copy).then_inc(c_Tc, 1)

            def normalise(t, k, src, dst):
                for j in range(G):
                    act.wait_ge(L[t][3], k + 1)
                    act.activation(dst[:, j, :], src(j), ACT.Identity, bias=cnm_of[t][:, j:j + 1],
                                   scale=crs_of[t][:, j:j + 1]).then_inc(L[t][4], 1)

            def x_in(k):
                normalise("lnx", k, lambda j: state[:, bass.ds(slot(k, j), 1), :].rearrange("p a d -> p (a d)"), xn)
                for i in range(2):
                    act.wait_ge(a_xT, 2 * k + i + 1)
                    act.activation(xnT[:, i, :, :], ps[i][:, :].rearrange("p (c t) -> p c t", c=DC), ACT.Copy)\
                       .then_inc(a_xTc, 1)

            def q_in(k):
                normalise("lnq", k, lambda j: ps[2 + j // 2][:, (j % 2) * D:(j % 2 + 1) * D], qn)

            def q_out(k, s):
                for i in range(2):
                    act.wait_ge(a_qT, 2 * k + i + 1)
                    a0 = (2 * s + i) * 2 * P // 16
                    for c in range(DC):
                        act.activation(reluT[:, c, :, :, a0:a0 + 2 * P // 16],
                                       ps[i][:, c * D:(c + 1) * D].rearrange("p (a i m) -> p m i a", i=2, m=WPB),
                                       ACT.Relu, bias=xgc[:, 1, c:c + 1], scale=xgc[:, 0, c:c + 1]).then_inc(a_relu, 1)

            for k in range(2):
                x_in(k)
                q_in(k)
                q_out(k, k)

            def sequence(b, nxt):
                k = 2 * b + 2
                if nxt:
                    x_in(k)
                for n in range(4):
                    act.wait_ge(a_aT, 4 * b + n + 1)
                    act.activation(attT[:, :, n * 2 * P:(n + 1) * 2 * P].rearrange("p i (h a) -> p i h a", h=4),
                                   ps[4 + n][:, :].rearrange("p (h i a) -> p i h a", h=4, i=2), ACT.Copy)\
                       .then_inc(a_aTc, 1)
                if nxt:
                    q_in(k)
                    q_out(k, 0)
                    x_in(k + 1)
                    q_in(k + 1)
                    q_out(k + 1, 1)

            with act.Fori(0, NB - 1) as b:
                sequence(b, True)
            sequence(NB - 1, False)

            with act.Fori(0, LAYERS) as l:
                act.preload_act_table_set("natural_log_exp_and_others")
                act.wait_ge(d_attn_w, (l + 1) * 16 * 5)
                for loaded, hi, _ in attn_parts():
                    act.activation(hi, loaded, ACT.Copy).then_inc(attn_hi, 1)

                def copy_hT(t):
                    act.wait_ge(hT_ps, t + 1)
                    act.activation(hT[:, 0, :, :], ps[6][:, 0:D].rearrange("p (c t) -> p c t", c=DC), ACT.Copy)\
                       .then_inc(hT_ready, 1)

                def square(t, n):
                    act.wait_ge(summed, 2 * t + n)
                    act.wait_ge(proj_done, 3 * t + n + 2)
                    if n:
                        act.wait_ge(q_prod, t + 1)
                    act.activation(sq[:, n, :], ps[5 - n][:, :], ACT.Square).then_inc(squared, 1)

                def guess_rsqrt(t, n):
                    cols = slice(n * H, n * H + H)
                    act.wait_ge(clipped, 2 * t + n + 1)
                    act.activation(lns[:, cols], ssum[:, cols], ACT.Ln, scale=LN_SCALE).then_inc(logged, 1)
                    act.wait_ge(logged, 2 * t + n + 1)
                    act.activation(y0[:, cols], lns[:, cols], ACT.Exp, scale=-0.5, bias=half_log[:, 0:1]).then_inc(guessed, 1)

                def copy_v(t, u):
                    act.wait_ge(proj_done, 3 * t + 1)
                    act.activation(vring[:, u, :], ps[6][:, :], ACT.Copy).then_inc(v_ready, 1)

                def round_qk(t, u):
                    for i in range(2):
                        own = slice(HD * i, HD * i + HD)
                        act.wait_ge(qkT_ps, 2 * t + 1)
                        act.activation(qS[own, i, :, :], ps[4][own, :].rearrange("p (h t) -> p h t", h=HP), ACT.Copy)\
                           .then_inc(q_hi, 1)
                    for i in range(2):
                        own = slice(HD * i, HD * i + HD)
                        act.wait_ge(qkT_ps, 2 * t + 2)
                        for j in (i, 1 - i):
                            act.activation(kH[HD * j:HD * j + HD, i, :, u, :],
                                           ps[5][own, :].rearrange("p (h t) -> p h t", h=HP), ACT.Copy).then_inc(k_hi, 1)

                def exps(t, u, a, which=range(4)):
                    act.wait_ge(pT_ps, 2 * t)
                    for i in which:
                        h = 4 * a + 2 * (i % 2) + i // 2
                        act.wait_ge(bias_ready, 4 * t + 2 * a + i // 2 + 1)
                        act.activation(probs[:, a, i, :], ps[2 * a + i // 2][:, (i % 2) * D:(i % 2 + 1) * D], ACT.Exp,
                                       scale=rn[:, u % 2, H + h:H + h + 1], bias=negmax[:, u % 2, h:h + 1],
                                       accum_out=lsum[:, u % 2, h:h + 1]).then_inc(exped, 1)

                def copy_pT_1(t):
                    act.wait_ge(pT_ps, 2 * t + 1)
                    act.wait_ge(pv_done, 2 * t)
                    act.activation(pT[:, 0, 2:4, :, :], ps[1][:, :].rearrange("p (h b q) -> p h b q", h=2, b=2),
                                   ACT.Copy).then_inc(pT1_ready, 1)

                def copy_pT_B(t):
                    act.wait_ge(pT_ps, 2 * t + 2)
                    act.wait_ge(pv_done, 2 * t)
                    for i in range(2):
                        ins = act.activation(pT[:, 1, 2 * i:2 * i + 2, :, :],
                                             ps[2 + i][:, :].rearrange("p (h b q) -> p h b q", h=2, b=2), ACT.Copy)
                    ins.then_inc(pTB_ready, 1)

                def step(t, u, nxt, prev, next2):
                    exps(t, u, 0)
                    if nxt:
                        square(t + 1, 0)
                    exps(t, u, 1)
                    if nxt:
                        guess_rsqrt(t + 1, 0)
                    copy_pT_1(t)
                    copy_pT_B(t)
                    if nxt:
                        square(t + 1, 1)
                        guess_rsqrt(t + 1, 1)
                    if next2:
                        copy_hT(t + 2)
                    if nxt:
                        round_qk(t + 1, (u + 1) % G)
                    if next2:
                        copy_v(t + 2, (u + 2) % G)

                t0 = l * NT
                act.wait_ge(rings_zeroed, 4 * (l + 1))
                copy_hT(t0); copy_v(t0, 0); square(t0, 0); guess_rsqrt(t0, 0); square(t0, 1); guess_rsqrt(t0, 1)
                copy_hT(t0 + 1); round_qk(t0, 0); copy_v(t0 + 1, 1)
                for u in range(G):
                    step(t0 + u, u, True, u > 0, True)
                with act.Fori(1, NG - 1) as k:
                    for u in range(G):
                        step(t0 + G * k + u, u, True, True, True)
                for u in range(G):
                    step(t0 + G * (NG - 1) + u, u, u < G - 1, True, u < G - 2)

                def gelus(g):
                    for m in range(NM):
                        act.wait_ge(f_w1, (l * NG + g) * 2 * NM + 2 * m + 1)
                        act.wait_ge(f_hid, (l * NG + g) * NM + (m - 1 if m else 0))
                        act.activation(gel[0:MW[m], m % 2, :], ps[2 + 2 * (m % 2)][0:MW[m], :], ACT.Gelu,
                                       bias=b1c[0:MW[m], 1, m:m + 1]).then_inc(f_gel, 1)

                def copy_hnT(g):
                    act.wait_ge(f_w1, (l * NG + g) * 2 * NM)
                    for c in range(DC):
                        act.wait_ge(f_hT, (l * NG + g) * DC + c + 1)
                        act.activation(hnT[:, c, :], ps[c][:, :], ACT.Identity,
                                       bias=lnc[:, 1, c:c + 1], scale=lnc[:, 0, c:c + 1]).then_inc(f_hTc, 1)

                act.wait_ge(d_ffn_w, (l + 1) * 16 * 10)
                copy_hnT(0)
                with act.Fori(0, NG - 1) as g:
                    gelus(g)
                    copy_hnT(g + 1)
                gelus(NG - 1)

        @block.tensor
        def _(pe):
            pe.wait_ge(d_const, 16 * N_CONST)
            for b in range(NB):
                for c in range(DC):
                    mm = pe.transpose(ps[b][:, c * P:c * P + CTX], ctx_sb[:, b, c * P:(c + 1) * P], ident[0:CTX, 0:CTX])
                mm.then_inc(c_T, 1)
            for b in range(NB):
                pe.wait_ge(c_Tc, b + 1)
                for c in range(DC):
                    mm = pe.matmul(ps[4 + b][0:CTX, :], ctxT[:, c, b, 0:CTX], xw[:, c, D:3 * D],
                                   start=(c == 0), stop=(c == DC - 1))
                mm.then_inc(c_kv, 1)
            def key_values():
                for b in range(NB):
                    pe.wait_ge(c_aff, 2 * b + 2)
                    for c in range(DC):
                        mm = pe.matmul(ps[4 + b][:, c * KVC:(c + 1) * KVC], kp[:, b, c * P:(c + 1) * P], vp[:, b, c, :],
                                       start=True, stop=True)
                    mm.then_inc(c_kvs, 1)

            def transposes_x(k):
                for i in range(2):
                    pe.wait_ge(a_relu, 4 * k)
                    for jj in range(2):
                        pe.wait_ge(L["lnx"][4], G * k + 2 * i + jj + 1)
                        for c in range(DC):
                            mm = pe.transpose(ps[i][:, c * D + jj * P:c * D + (jj + 1) * P],
                                              xn[:, 2 * i + jj, c * P:(c + 1) * P], ident[:, :])
                    mm.then_inc(a_xT, 1)

            def queries(k):
                for i in range(2):
                    pe.wait_ge(L["lnq"][4], G * k)
                    pe.wait_ge(a_xTc, 2 * k + i + 1)
                    for jj in range(2):
                        for c in range(DC):
                            mm = pe.matmul(ps[2 + i][:, jj * D:(jj + 1) * D], xnT[:, i, c, jj * P:(jj + 1) * P],
                                           xw[:, c, 0:D], start=(c == 0), stop=(c == DC - 1))
                    mm.then_inc(a_q, 1)

            def transposes_q(k):
                for i in range(2):
                    for jj in range(2):
                        pe.wait_ge(L["lnq"][4], G * k + 2 * i + jj + 1)
                        for c in range(DC):
                            mm = pe.transpose(ps[i][:, c * D + jj * P:c * D + (jj + 1) * P],
                                              qn[:, 2 * i + jj, c * P:(c + 1) * P], ident[:, :])
                    mm.then_inc(a_qT, 1)

            def attend(b, s):
                for j in range(G):
                    m = s * G + j
                    pe.wait_ge(a_qp, 2 * b + s + 1)
                    if s:
                        pe.wait_ge(a_an, WPB * b + j + 1)
                    for c in range(DC):
                        mm = pe.matmul(ps[4 + j][:, c * KVC:(c + 1) * KVC], qTs[:, c, m, :],
                                       kvs[:, bass.ds(b, 1), c, :].rearrange("p a n -> p (a n)"),
                                       start=True, stop=True)
                    mm.then_inc(a_att, 1)

            def transposes_att(b):
                pe.wait_ge(a_an, WPB * b + WPB)
                for h in range(XH):
                    mm = pe.transpose(ps[4 + h // 4][:, h % 4 * P:(h % 4 + 1) * P],
                                      att[:, h, :, :].rearrange("p m e -> p (m e)"), ident[:, :])
                    if h % 4 == 3:
                        mm.then_inc(a_aT, 1)

            def dense(b, s):
                for j in range(G):
                    t = s * G + j
                    pe.wait_ge(a_aTc, 4 * b + (2 * s + 2 if j < 2 else max(t // 2, 2 * s + 1) + 1))
                    for c in range(DC):
                        mm = pe.matmul(ps[4 + t // 2][:, (t % 2) * D:(t % 2 + 1) * D], attT[:, c, t * P:(t + 1) * P],
                                       dw_sb[:, c, :], start=(c == 0), stop=(c == DC - 1))
                    if j % 2:
                        mm.then_inc(a_y, 1)

            pe.wait_ge(c_Tc, NB)
            for k in range(2):
                transposes_x(k)
                queries(k)
                if k == 0:
                    key_values()
                transposes_q(k)
            pe.wait_ge(c_done, NB)

            def sequence(b, nxt):
                k = 2 * b + 2
                pe.wait_ge(a_yb, WPB * b)
                attend(b, 0)
                if nxt:
                    transposes_x(k)
                attend(b, 1)
                if nxt:
                    queries(k)
                transposes_att(b)
                dense(b, 0)
                if nxt:
                    transposes_q(k)
                dense(b, 1)
                if nxt:
                    transposes_x(k + 1)
                if nxt:
                    queries(k + 1)
                    transposes_q(k + 1)

            with pe.Fori(0, NB - 1) as b:
                sequence(b, True)
            sequence(NB - 1, False)

            pe.wait_ge(d_small, 32)
            with pe.Fori(0, LAYERS) as l:
                def project(t, which):
                    pe.wait_ge(hTlo_ready, t + 1)
                    for i in which:
                        for c in range(DC):
                            for n, (a, b) in enumerate(HALF_SPLIT):
                                mm = pe.matmul(ps[4 + i][:, :], hT[:, a, c, :],
                                               wqkv_s[b][:, c, i * INNER:(i + 1) * INNER],
                                               start=(c == n == 0), stop=(c == DC - 1 and n == 2))
                        mm.then_inc(proj_done, 1)

                def transpose_qk(t):
                    for i, ready in enumerate((q_prod, k_prod)):
                        pe.wait_ge(ready, t + 1)
                        if i == 0:
                            pe.wait_ge(squared, 2 * t + 2)
                        for hp in range(HP):
                            for a in range(2):
                                mm = pe.matmul(ps[4 + i][:, hp * P:(hp + 1) * P], rot[:, i, a, hp * P:(hp + 1) * P],
                                               ident[:, :], start=(a == 0), stop=(a == 1), is_transpose=True)
                        mm.then_inc(qkT_ps, 1)

                def score(t, u, a, half):
                    for ready in ((pT0_ready, pT1_ready), (pTB_ready,))[a]:
                        pe.wait_ge(ready, t)
                    first = (u - 1) if u else 0
                    step = 1 if u else G - 1
                    blocks2 = slice(first, first + step + 1, step)
                    for i in range(2):
                        own = slice(HD * i, HD * i + HD)
                        bank = ps[2 * a + i]
                        mask = mask_sb[:, bass.ds(half, 1), u, :, :].rearrange("p x b k -> p x (b k)")
                        pe.matmul(bank[:, :], identb[:, :], mask.to_broadcast((P, 2, D)),
                                  start=True, stop=False)
                        if a == 0:
                            pe.wait_ge(q_lo, 2 * t + i + 1)
                            pe.wait_ge(k_hi, 4 * t + 2 * i + 2)
                            pe.wait_ge(k_lo, 2 * t + i + 1)
                        for j in range(2):
                            pe.matmul(bank[:, j * D:(j + 1) * D], qS[:, i, 2 * a + j, :], kH[:, i, 2 * a + j, blocks2, :],
                                      start=False, stop=False)
                            mm = pe.matmul(bank[:, j * D:(j + 1) * D], qS[own, i, 2 * a + j, :],
                                           kL[own, 2 * a + j, blocks2, :], start=False, stop=(j == 1))
                        mm.then_inc(scored, 1)

                def transpose_p(t, a):
                    pe.wait_ge(exped, 8 * t + 4 * a + 4)
                    for i in range(4):
                        for b in range(2):
                            c = (2 * (i % 2) + b) * P
                            mm = pe.transpose(ps[2 * a + i // 2][:, c:c + P], probs[:, a, i, b * P:(b + 1) * P], ident[:, :])
                    mm.then_inc(pT_ps, 1)

                def weigh(t, u, a):
                    for ready in ((pT0_ready, pT1_ready), (pTB_ready,))[a]:
                        pe.wait_ge(ready, t + 1)
                    pe.wait_ge(oTlo_ready, t)
                    if a == 0:
                        pe.wait_ge(v_ready, t + 1)
                    cur, prev = block_order(u)
                    for i in range(4):
                        h = 4 * a + 2 * (i % 2) + i // 2
                        for b in range(2):
                            v = vring[:, u if b == cur else (u - 1) % G, h * HD:(h + 1) * HD]
                            mm = pe.matmul(ps[7][:, h * HD:(h + 1) * HD], pT[:, a, i, b, :], v,
                                           start=(b == 0), stop=(b == 1))
                    mm.then_inc(pv_done, 1)

                def transpose_o(t):
                    pe.wait_ge(on_ready, t + 1)
                    for hp in range(HP):
                        mm = pe.transpose(ps[7][:, hp * P:(hp + 1) * P], onorm[:, hp * P:(hp + 1) * P], ident[:, :])
                    mm.then_inc(oT_ps, 1)

                def project_out(t):
                    pe.wait_ge(oTlo_ready, t + 1)
                    for hp in range(HP):
                        for n, (a, b) in enumerate(HALF_SPLIT):
                            mm = pe.matmul(ps[6][:, 0:D], oT[:, a, hp, :], wo_s[b][:, hp, :],
                                           start=(hp == n == 0), stop=(hp == HP - 1 and n == 2))
                    mm.then_inc(wo_done, 1)

                def step_(t, u, k, nxt, prev, next2):
                    half = k & 1
                    score(t, u, 0, half)
                    score(t, u, 1, half)
                    if nxt:
                        project(t + 1, (1, 0))
                    if prev:
                        transpose_o(t - 1)
                    transpose_p(t, 0)
                    transpose_p(t, 1)
                    if prev:
                        if nxt:
                            pe.wait_ge(v_ready, t + 2)
                        else:
                            pe.wait_ge(x_attn, t - 1)
                        project_out(t - 1)
                    weigh(t, u, 0)
                    if next2:
                        transpose_h(t + 2, k, u + 2, prev)
                    if nxt:
                        transpose_qk(t + 1)
                    weigh(t, u, 1)
                    if next2:
                        project(t + 2, (2,))

                def transpose_h(t, k, u, before):
                    pe.wait_ge(d_hs, 64 * (pair0 + 2 * k + u // 2 + 1))
                    if before:
                        pe.wait_ge(x_attn, t - 2)
                    else:
                        pe.wait_ge(v_ready, t)
                    for c in range(DC):
                        mm = pe.transpose(ps[6][:, c * P:(c + 1) * P], hs[:, u % 2, c * P:(c + 1) * P], ident[:, :])
                    mm.then_inc(hT_ps, 1)

                t0, pair0 = l * NT, l * (NT // 2)
                pe.wait_ge(x_ready, t0 + NT)
                pe.wait_ge(d_hs, 64 * (pair0 + 1))
                for c in range(DC):
                    mm = pe.transpose(ps[6][:, c * P:(c + 1) * P], hs[:, 0, c * P:(c + 1) * P], ident[:, :])
                mm.then_inc(hT_ps, 1)
                pe.wait_ge(attn_lo, (l + 1) * 2)
                pe.wait_ge(attn_lo_pool, (l + 1) * 2)
                project(t0, (2, 1, 0))
                transpose_h(t0 + 1, 0, 1, False)
                transpose_qk(t0)
                project(t0 + 1, (2,))
                for u in range(G):
                    step_(t0 + u, u, 0, True, u > 0, True)
                with pe.Fori(1, NG - 1) as k:
                    for u in range(G):
                        step_(t0 + G * k + u, u, k, True, True, True)
                for u in range(G):
                    step_(t0 + G * (NG - 1) + u, u, NG - 1, u < G - 1, True, u < G - 2)
                transpose_o(t0 + NT - 1)
                pe.wait_ge(x_attn, t0 + NT - 1)
                project_out(t0 + NT - 1)

                def transpose_hn(g):
                    for c in range(DC):
                        for j in range(G):
                            pe.wait_ge(f_hn, (l * NG + g) * G + G)
                            mm = pe.transpose(ps[c][:, j * P:(j + 1) * P], hn[:, j, c * P:(c + 1) * P], ident[:, :])
                        mm.then_inc(f_hT, 1)

                def expand(g):
                    base = (l * NG + g)
                    for m in range(NM):
                        pe.wait_ge(f_hid, base * NM + (m - 1 if m else 0))
                        for a, off in ((0, HID), (1, 0)):
                            bank = ps[2 + 2 * (m % 2) + a]
                            for c in range(DC):
                                pe.wait_ge(f_hnlo, base * DC + c + 1)
                                cols = slice(off + m * MC, off + m * MC + MW[m])
                                for n, (i, j) in enumerate(HALF_SPLIT):
                                    mm = pe.matmul(bank[0:MW[m], :], w1_s[i][:, c, cols],
                                                   (hnTh, hnTl)[j][:, c, :],
                                                   start=(c == n == 0), stop=(c == DC - 1 and n == 2))
                            mm.then_inc(f_w1, 1)

                def contract(g):
                    for pair in range(G // 2):
                        for chunks in (range(NM - 1), (NM - 1,)):
                            pe.wait_ge(f_hidlo, (l * NG + g) * NM + chunks[-1] + 1)
                            for j in (2 * pair, 2 * pair + 1):
                                if chunks[0] == 0:
                                    pe.wait_ge(f_x, l * NT + G * g + (j - 1 if pair else 0))
                                for m in chunks:
                                    for n, (a, b) in enumerate(HALF_SPLIT):
                                        mm = pe.matmul(ps[6 + j % 2][:, 0:D],
                                                       (hidh, hidl)[a][0:MW[m], m, j * P:(j + 1) * P],
                                                       w2_s[b][0:MW[m], m, :],
                                                       start=(m == n == 0), stop=(m == NM - 1 and n == 2))
                                if chunks[-1] == NM - 1:
                                    mm.then_inc(f_w2, 1)

                pe.wait_ge(w1_split, (l + 1) * PIECES)
                pe.wait_ge(w2_split, (l + 1) * 2)
                pe.wait_ge(x_attn, t0 + NT)
                transpose_hn(0)
                with pe.Fori(0, NG - 1) as g:
                    expand(g)
                    transpose_hn(g + 1)
                    contract(g)
                expand(NG - 1)
                contract(NG - 1)

        @block.vector
        def _(dve):
            dve.wait_ge(d_const, 16 * N_CONST)
            dve.memset(half_log[:, :], 0.5 * float(np.log(LN_SCALE))).then_inc(c_ones, 1)
            dve.memset(vp[:, :, :, P:KVC], 1.0).then_inc(c_ones, 1)
            dve.wait_ge(tanh_done, 1)
            dve.tensor_scalar(gT[:, :], gam_r[:, :], tanh_g[:, 0:1], None, ALU.mult)
            dve.tensor_scalar(bT[:, :], bet_r[:, :], tanh_g[:, 0:1], None, ALU.mult).then_inc(folded, 1)

            for b in range(NB):
                dve.wait_ge(c_kv, b + 1)
                for i in range(2):
                    dve.bn_stats(cst[0:CTX, 2 * b + i, :], ps[4 + b][0:CTX, i * D:(i + 1) * D]).then_inc(c_st, 1)
            dve.wait_ge(c_st, 2 * NB)
            for n in range(2 * NB):
                dve.bn_aggr(cmv[0:CTX, n, :], cst[0:CTX, n, :]).then_inc(c_ag, 1)
            dve.wait_ge(c_ag, 2 * NB)
            dve.tensor_scalar(cve[0:CTX, :], cmv[0:CTX, :, 1], EPS6, None, ALU.add).then_inc(c_ve, 1)
            def stats(t, k, src, eps):
                st, ag, ve, rs, done = L[t]
                mv, var = cmv_of[t], cve_of[t]
                dve.wait_ge(rs, k)
                dve.memset(var[:, 0:2], eps).then_inc(ag, 1)
                for j in range(G):
                    dve.bn_stats(cst_of[t][:, j, :], src(j)).then_inc(st, 1)
                dve.wait_ge(st, G * k + G)
                dve.memset(var[:, 2:G], eps).then_inc(ag, 1)
                for j in range(G):
                    dve.bn_aggr(mv[:, j, :], cst_of[t][:, j, :]).then_inc(ag, 1)
                dve.wait_ge(ag, (G + 2) * (k + 1))
                dve.tensor_tensor(var[:, :], mv[:, :, 1], var[:, :], ALU.add).then_inc(ve, 1)

            def x_tile(k, j):
                return state[:, bass.ds(slot(k, j), 1), :].rearrange("p a d -> p (a d)")

            def x_stats(k):
                if isinstance(k, int) and k < 2:
                    dve.wait_ge(d_x_first[k], 16)
                else:
                    dve.wait_ge(d_x, 16 * (NG - 2))
                stats("lnx", k, lambda j: x_tile(k, j), EPS5)

            def q_stats(k):
                dve.wait_ge(a_q, 2 * k + 2)
                stats("lnq", k, lambda j: ps[2 + j // 2][:, (j % 2) * D:(j % 2 + 1) * D], EPS6)

            def divide(b, s):
                for j in range(G):
                    n = WPB * b + G * s + j
                    dve.wait_ge(a_att, n + 1)
                    heads = ps[4 + j][:, 0:DC * KVC].rearrange("p (c n) -> p c n", c=DC)
                    z = zinv[:, j, :].rearrange("p (c h) -> p c h", c=DC)
                    dve.tensor_scalar(z, heads[:, :, P:KVC], EPS6, None, ALU.add).then_inc(a_zd, 1)
                    dve.wait_ge(a_zd, n + 1)
                    dve.reciprocal(zinv[:, j, :], zinv[:, j, :]).then_inc(a_z, 1)
                    dve.wait_ge(a_z, n + 1)
                    for c in range(DC):
                        ins = dve.tensor_tensor(
                            att[:, c * XHC:(c + 1) * XHC, s * G + j, :],
                            heads[:, c, 0:P].rearrange("p (h e) -> p h e", h=XHC),
                            z[:, c, :].unsqueeze(2).to_broadcast((P, XHC, XD)), ALU.mult)
                    ins.then_inc(a_an, 1)

            def add_eps(b):
                for s in range(2):
                    dve.wait_ge(a_relu, WPB * b + WPB)
                    dve.wait_ge(a_att, WPB * b)
                    dve.tensor_scalar(qTs[:, :, G * s:G * s + G, :],
                                      reluT[:, :, G * s:G * s + G, :, :].rearrange("p c m i a -> p c m (i a)"),
                                      EPS6, None, ALU.add).then_inc(a_qp, 1)

            def y_stats(b, s):
                dve.wait_ge(d_x1[s], 16 * b)
                dve.wait_ge(x_ready, WPB * b)
                for j in range(G):
                    t = s * G + j
                    dve.wait_ge(a_y, 4 * b + t // 2 + 1)
                    dve.tensor_tensor(yx[s][:, j, :], ps[4 + t // 2][:, (t % 2) * D:(t % 2 + 1) * D], db_r[:, :], ALU.add)\
                       .then_inc(a_yb, 1)
                dve.wait_ge(a_yb, WPB * b + s * G + G)
                stats(f"lno{s}", b, lambda j: yx[s][:, j, :], EPS6)

            def residual(b, s):
                t = f"lno{s}"
                dve.wait_ge(L[t][3], b + 1)
                for j in range(G):
                    dve.scalar_tensor_tensor(out=yx[s][:, j, :], in0=yx[s][:, j, :], scalar=cmv_of[t][:, j, 0:1],
                                             in1=gT[:, :], op0=ALU.subtract, op1=ALU.mult).then_inc(L[t][4], 1)
                for j in range(G):
                    dve.wait_ge(L[t][4], WPB * b + s * G + j + 1)
                    dve.wait_ge(a_xb, WPB * b + WPB)
                    dve.scalar_tensor_tensor(out=yx[s][:, j, :], in0=yx[s][:, j, :], scalar=crs_of[t][:, j:j + 1],
                                             in1=x_tile(2 * b + s, j), op0=ALU.mult, op1=ALU.add).then_inc(a_x1, 1)
                dve.wait_ge(a_x1, WPB * b + s * G + G)
                stats(f"lnf{s}", b, lambda j: yx[s][:, j, :], EPS5)

            def inner_input(b, s):
                t = f"lnf{s}"
                dve.wait_ge(L[t][3], b + 1)
                for j in range(G):
                    dve.tensor_scalar(x_tile(2 * b + s, j), yx[s][:, j, :], cmv_of[t][:, j, 0:1], crs_of[t][:, j:j + 1],
                                      ALU.subtract, ALU.mult).then_inc(x_ready, 1)

            def context_features():
                dve.wait_ge(c_rs, 1)
                for b in range(NB):
                    for i in range(2):
                        n = 2 * b + i
                        dve.tensor_scalar(kvh[:, b, i, :], ps[4 + b][0:CTX, i * D:(i + 1) * D], cmv[0:CTX, n, 0:1],
                                          crs[0:CTX, n:n + 1], ALU.subtract, ALU.mult).then_inc(c_norm, 1)
                halves = [kvh[:, b, i, :] for b in range(NB) for i in range(2)]
                N2 = 2 * NB
                for n, r in enumerate(halves):
                    dve.wait_ge(c_norm, N2)
                    dve.tensor_tensor(r, r, gam_r[0:CTX, :], ALU.mult).then_inc(c_norm, 1)
                for n, r in enumerate(halves):
                    dve.wait_ge(c_norm, 2 * N2)
                    dve.tensor_tensor(r, r, bet_r[0:CTX, :], ALU.add).then_inc(c_norm, 1)
                for b in range(NB):
                    dve.wait_ge(c_norm, 3 * N2)
                    dve.tensor_scalar(kvh[:, b, 0, :], kvh[:, b, 0, :], 0.0, EPS6, ALU.max, ALU.add).then_inc(c_norm, 1)
                for b in range(NB):
                    dve.wait_ge(c_norm, 3 * N2 + NB)
                    dve.tensor_scalar(kp[:, b, :], kvh[:, b, 0, :], em[:, b:b + 1], None, ALU.mult).then_inc(c_aff, 1)
                    dve.wait_ge(c_ones, 2)
                    dve.tensor_scalar(vp[:, b, :, 0:P], kvh[:, b, 1, :].rearrange("p (c e) -> p c e", c=DC),
                                      em[:, b:b + 1], None, ALU.mult).then_inc(c_aff, 1)

            def mask_key_values():
                for b in range(NB):
                    dve.wait_ge(c_kvs, b + 1)
                    dve.tensor_tensor(kvs[:, b, :, :], ps[4 + b][:, 0:DC * KVC].rearrange("p (c n) -> p c n", c=DC),
                                      blocks[:, :, :], ALU.mult).then_inc(c_done, 1)

            x_stats(0)
            context_features()
            q_stats(0)
            x_stats(1)
            mask_key_values()
            q_stats(1)

            def sequence(b, nxt):
                k = 2 * b + 2
                add_eps(b)
                if nxt:
                    x_stats(k)
                divide(b, 0)
                divide(b, 1)
                if nxt:
                    q_stats(k)
                    x_stats(k + 1)
                y_stats(b, 0)
                y_stats(b, 1)
                residual(b, 0)
                if nxt:
                    q_stats(k + 1)
                residual(b, 1)
                for s in range(2):
                    inner_input(b, s)

            with dve.Fori(0, NB - 1) as b:
                sequence(b, True)
            sequence(NB - 1, False)

            with dve.Fori(0, LAYERS) as l:
                t0 = l * NT
                for i, (loaded, hi, lo) in enumerate(attn_parts()[0:2]):
                    dve.wait_ge(attn_hi, 4 * l + i + 1)
                    dve.tensor_tensor(lo, loaded, f32(hi), ALU.subtract).then_inc(attn_lo, 1)
                dve.wait_ge(d_attn_w, (l + 1) * 16 * 5)
                for i in range(2):
                    for a in range(2):
                        ins = dve.tensor_tensor(tab[:, :, i, a, :], tab[:, :, i, a, :],
                                                qks[:, i:i + 1, :].to_broadcast((P, WPB, HD)), ALU.mult)
                        if i == 1 and a == 1:
                            ins.then_inc(tab_ready, 1)
                dve.wait_ge(tab_ready, l + 1)

                def split_hT(t):
                    dve.wait_ge(hT_ready, t + 1)
                    dve.tensor_tensor(hT[:, 1, :, :], ps[6][:, 0:D].rearrange("p (c t) -> p c t", c=DC),
                                      f32(hT[:, 0, :, :]), ALU.subtract).then_inc(hTlo_ready, 1)

                def split_oT(t):
                    dve.wait_ge(oT_ps, t + 1)
                    dve.tensor_copy(oT[:, 0, :, :], ps[7][:, :].rearrange("p (h t) -> p h t", h=HP)).then_inc(oT_ready, 1)
                    dve.wait_ge(oT_ready, t + 1)
                    dve.tensor_tensor(oT[:, 1, :, :], ps[7][:, :].rearrange("p (h t) -> p h t", h=HP),
                                      f32(oT[:, 0, :, :]), ALU.subtract).then_inc(oTlo_ready, 1)

                def sum_squares(t, n):
                    cols = slice(n * H, n * H + H)
                    dve.wait_ge(squared, 2 * t + n + 1)
                    dve.tensor_reduce(ssum[:, cols], sq[:, n, :].rearrange("p (h d) -> p h d", h=H), AX.X, ALU.add)\
                       .then_inc(summed, 1)
                    dve.wait_ge(summed, 2 * t + n + 1)
                    dve.tensor_scalar(ssum[:, cols], ssum[:, cols], 1e-24, None, ALU.max).then_inc(clipped, 1)

                def rotate_queries(t, w):
                    dve.wait_ge(proj_done, 3 * t + 3)
                    dve.wait_ge(qkT_ps, 2 * t)
                    src = ps[4][:, :]
                    dve.tensor_tensor(rot[:, 0, 0, :].rearrange("p (h d) -> p h d", h=H),
                                      src.rearrange("p (h d) -> p h d", h=H),
                                      tab[:, bass.ds(w, 1), 0, 0, :].to_broadcast((P, H, HD)), ALU.mult)
                    dst = rot[:, 0, 1, :].rearrange("p (h a e) -> p h a e", h=H, a=2)
                    src = src.rearrange("p (h a e) -> p h a e", h=H, a=2)
                    for a in range(2):
                        ins = dve.tensor_tensor(
                            dst[:, :, 1 - a, :], src[:, :, a, :],
                            tab[:, bass.ds(w, 1), 0, 1, a * 32:a * 32 + 32].to_broadcast((P, H, 32)), ALU.mult)
                    ins.then_inc(q_prod, 1)

                def refine_rsqrt(t, u, n):
                    cols = slice(n * H, n * H + H)
                    dve.wait_ge(guessed, 2 * t + n + 1)
                    dve.tensor_tensor(ya[:, cols], y0[:, cols], y0[:, cols], ALU.mult).then_inc(newton, 1)
                    dve.wait_ge(newton, 7 * t + 3 * n + 1)
                    dve.scalar_tensor_tensor(out=yb[:, cols], in0=ya[:, cols], scalar=-0.5, in1=ssum[:, cols],
                                             op0=ALU.mult, op1=ALU.mult).then_inc(newton, 1)
                    dve.wait_ge(newton, 7 * t + 3 * n + 2)
                    dve.scalar_tensor_tensor(out=rn[:, u % 2, cols], in0=yb[:, cols], scalar=1.5, in1=y0[:, cols],
                                             op0=ALU.add, op1=ALU.mult).then_inc(newton, 1)
                    if n:
                        dve.wait_ge(newton, 7 * t + 6)
                        dve.tensor_scalar(rn[:, u % 2, cols], rn[:, u % 2, cols], 8.0, None, ALU.mult).then_inc(newton, 1)

                def normalise_keys(t, u):
                    dve.wait_ge(newton, 7 * t + 3)
                    dve.wait_ge(k_prod, t)
                    dve.tensor_tensor(khat[:, :].rearrange("p (h d) -> p h d", h=H),
                                      ps[5][:, :].rearrange("p (h d) -> p h d", h=H),
                                      rn[:, u % 2, 0:H].unsqueeze(2).to_broadcast((P, H, HD)), ALU.mult)\
                       .then_inc(khat_ready, 1)

                def split_qk(t, u):
                    for i in range(2):
                        own, other = (slice(HD * j, HD * j + HD) for j in (i, 1 - i))
                        dve.wait_ge(q_hi, 2 * t + i + 1)
                        dve.tensor_tensor(qS[other, i, :, :], ps[4][own, :].rearrange("p (h t) -> p h t", h=HP),
                                          f32(qS[own, i, :, :]), ALU.subtract).then_inc(q_lo, 1)
                    for i in range(2):
                        own = slice(HD * i, HD * i + HD)
                        dve.wait_ge(k_hi, 4 * t + 2 * i + 2)
                        dve.tensor_tensor(kL[own, :, u, :], ps[5][own, :].rearrange("p (h t) -> p h t", h=HP),
                                          f32(kH[own, i, :, u, :]), ALU.subtract).then_inc(k_lo, 1)

                def row_max(t, u, a):
                    for i in range(2):
                        heads = slice(4 * a + i, 4 * a + i + 3, 2)
                        dve.wait_ge(scored, 4 * t + 2 * a + i + 1)
                        dve.tensor_reduce(rowmax[:, u % 2, heads], ps[2 * a + i][:, :].rearrange("p (j k) -> p j k", j=2),
                                          AX.X, ALU.max, negate=True).then_inc(maxed, 1)
                        dve.wait_ge(maxed, 4 * t + 2 * a + i + 1)
                        dve.wait_ge(newton, 7 * t + 7)
                        dve.tensor_tensor(negmax[:, u % 2, heads], rowmax[:, u % 2, heads],
                                          rn[:, u % 2, H + heads.start:H + heads.stop:2], ALU.mult).then_inc(bias_ready, 1)

                def copy_pT_0(t):
                    dve.wait_ge(pT_ps, 2 * t + 1)
                    dve.wait_ge(pv_done, 2 * t)
                    dve.tensor_copy(pT[:, 0, 0:2, :, :], ps[0][:, :].rearrange("p (h b q) -> p h b q", h=2, b=2))\
                       .then_inc(pT0_ready, 1)

                def add_to_state(t, s):
                    dve.wait_ge(wo_done, t + 1)
                    tile = state[:, bass.ds(s, 1), :].rearrange("p a d -> p (a d)")
                    dve.tensor_tensor(tile, ps[6][:, 0:D], tile, ALU.add).then_inc(x_attn, 1)

                def normalise_o(t, u):
                    dve.wait_ge(exped, 8 * t + 8)
                    dve.reciprocal(linv[:, :], lsum[:, u % 2, :]).then_inc(linv_ready, 1)
                    dve.wait_ge(linv_ready, t + 1)
                    dve.wait_ge(pv_done, 2 * t + 2)
                    dve.tensor_tensor(onorm[:, :].rearrange("p (h d) -> p h d", h=H),
                                      ps[7][:, :].rearrange("p (h d) -> p h d", h=H),
                                      linv[:, :].unsqueeze(2).to_broadcast((P, H, HD)), ALU.mult).then_inc(on_ready, 1)

                def group_stats(g):
                    base = l * NG + g
                    dve.wait_ge(d_hf, 64 * (base + 1))
                    for j in range(G):
                        dve.bn_stats(fst[:, j, 0, :], hf[:, j, :]).then_inc(f_st, 1)
                    dve.wait_ge(f_st, G * (base + 1))
                    dve.memset(fve[:, :], EPS5).then_inc(f_mv, 1)
                    for j in range(G):
                        dve.bn_aggr(fmv[:, j, :], fst[:, j, 0, :]).then_inc(f_mv, 1)
                    dve.wait_ge(f_mv, (G + 1) * (base + 1))
                    dve.tensor_tensor(fve[:, :], fmv[:, :, 1], fve[:, :], ALU.add).then_inc(f_ve, 1)

                def step(t, u, w, s_prev, nxt, prev, next2=True):
                    row_max(t, u, 0)
                    if prev:
                        normalise_o(t - 1, u - 1)
                    row_max(t, u, 1)
                    if nxt:
                        sum_squares(t + 1, 0)
                    if prev:
                        split_oT(t - 1)
                    if nxt:
                        refine_rsqrt(t + 1, u + 1, 0)
                        normalise_keys(t + 1, u + 1)
                    if u == G - 1 and not nxt:
                        group_stats(0)
                    copy_pT_0(t)
                    if nxt:
                        rotate_queries(t + 1, w)
                    if prev:
                        add_to_state(t - 1, s_prev)
                    if nxt:
                        sum_squares(t + 1, 1)
                        refine_rsqrt(t + 1, u + 1, 1)
                    if next2:
                        split_hT(t + 2)
                    if nxt:
                        split_qk(t + 1, (u + 1) % G)

                split_hT(t0)
                sum_squares(t0, 0)
                rotate_queries(t0, 0)
                refine_rsqrt(t0, 0, 0)
                normalise_keys(t0, 0)
                sum_squares(t0, 1)
                refine_rsqrt(t0, 0, 1)
                split_hT(t0 + 1)
                split_qk(t0, 0)
                for u in range(G):
                    step(t0 + u, u, (u + 1) % WPB, slot(0, u - 1), True, u > 0)
                with dve.Fori(1, NG - 1) as k:
                    for u in range(G):
                        s_prev = slot(k, u - 1) if u else slot(k - 1, G - 1)
                        step(t0 + G * k + u, u, (G * k + u + 1) & (WPB - 1), s_prev, True, True)
                for u in range(G):
                    s_prev = slot(NG - 1, u - 1) if u else slot(NG - 2, G - 1)
                    step(t0 + G * (NG - 1) + u, u, (G * (NG - 1) + u + 1) % WPB, s_prev, u < G - 1, True, u < G - 2)
                normalise_o(t0 + NT - 1, G - 1)
                split_oT(t0 + NT - 1)
                add_to_state(t0 + NT - 1, slot(NG - 1, G - 1))

                def group_apply(g):
                    base = l * NG + g
                    dve.wait_ge(f_rs, base + 1)
                    dve.wait_ge(f_hT, base * DC)
                    for j in range(G):
                        dve.tensor_scalar(hn[:, j, :], hf[:, j, :], fmv[:, j, 0:1], frs[:, j:j + 1],
                                          ALU.subtract, ALU.mult).then_inc(f_hn, 1)

                def round_hnT(g):
                    for c in range(DC):
                        dve.wait_ge(f_hTc, (l * NG + g) * DC + c + 1)
                        dve.tensor_copy(hnTh[:, c, :], hnT[:, c, :]).then_inc(f_hnhi, 1)

                def gate(g, nxt):
                    base = l * NG + g
                    for m in range(NM):
                        dve.wait_ge(f_gel, base * NM + m + 1)
                        dve.wait_ge(f_w1, base * 2 * NM + 2 * m + 2)
                        dve.wait_ge(f_w2, l * NT + G * g)
                        dve.scalar_tensor_tensor(out=hid[0:MW[m], m, :], in0=ps[3 + 2 * (m % 2)][0:MW[m], :],
                                                 scalar=b1c[0:MW[m], 0, m:m + 1], in1=gel[0:MW[m], m % 2, :],
                                                 op0=ALU.add, op1=ALU.mult).then_inc(f_hid, 1)
                        dve.wait_ge(f_hid, base * NM + m + 1)
                        dve.tensor_copy(hidh[0:MW[m], m, :], hid[0:MW[m], m, :]).then_inc(f_hidhi, 1)
                        if nxt and m == 1:
                            group_stats(g + 1)
                        if nxt and m == 3:
                            group_apply(g + 1)

                def add_group(g):
                    for j in range(G):
                        dve.wait_ge(f_w2, l * NT + G * g + j + 1)
                        tile = state[:, bass.ds(slot(g, j), 1), :].rearrange("p a d -> p (a d)")
                        dve.tensor_tensor(tile, ps[6 + j % 2][:, 0:D], tile, ALU.add).then_inc(f_x, 1)

                dve.wait_ge(d_ffn_w, (l + 1) * 16 * 10)
                group_apply(0)
                round_hnT(0)
                with dve.Fori(0, NG - 1) as g:
                    gate(g, True)
                    round_hnT(g + 1)
                    add_group(g)
                gate(NG - 1, False)
                add_group(NG - 1)

            with dve.Fori(0, NG) as g:
                dve.wait_ge(x_ready, LAYERS * NT + G * g + G)
                dve.wait_ge(d_x1_back, 16 * NG)
                s = slot(g, 0)
                dve.scalar_tensor_tensor(out=x1[:, bass.ds(G * g, G), :], in0=state[:, bass.ds(s, G), :],
                                         scalar=tanh_g[:, 1:2], in1=x1[:, bass.ds(G * g, G), :],
                                         op0=ALU.mult, op1=ALU.add).then_inc(summed_out, 1)


_INS = ["x", "ctx_1024", "mask_BxS2_ff1", "g_xattn", "g_ffn", "L0_xattn_wq", "L0_xattn_wk", "L0_xattn_wv",
        "L0_xattn_ln_gamma", "L0_xattn_ln_beta", "L0_xattn_dense_w", "L0_xattn_dense_b",
        "L0_ffn_wqkv", "L0_ffn_q_scale", "L0_ffn_k_scale", "L0_ffn_wo", "L0_ffn_ln_g", "L0_ffn_ln_b",
        "L0_ffn_w1", "L0_ffn_b1", "L0_ffn_w2", "L0_ffn_b2"]


def kernel(**inputs):
    import concourse.bacc as bacc
    from concourse.bass_utils import run_bass_kernel_spmd

    nc = bacc.Bacc("TRN2", target_bir_lowering=False, num_devices=1)
    arrays, args = {}, []

    def put(name, a):
        a = np.ascontiguousarray(a)
        arrays[name] = a
        args.append(nc.dram_tensor(name, a.shape, mybir.dt.from_np(a.dtype), kind="ExternalInput").ap())

    for name in _INS:
        put(f"in_{name}_dram", np.asarray(inputs[name]))
    put("tables_dram", position_tables())
    put("masks_dram", masks())
    put("blocks_dram", block_diagonal())
    put("ident_dram", np.eye(P, dtype=np.float32))
    out = nc.dram_tensor("out_dram", (NB, S, D), F32, kind="ExternalOutput").ap()
    program(nc, *args, out)
    r = run_bass_kernel_spmd(nc, [arrays], core_ids=[0])
    return r.results[0]["out_dram"]
```

```python
from contextlib import ExitStack

import numpy as np

import concourse.bass as bass
from concourse import mybir
from concourse.alu_op_type import AluOpType as ALU

ACT = mybir.ActivationFunctionType
AX = mybir.AxisListType
F32 = mybir.dt.float32
BF16 = mybir.dt.bfloat16
F32R = mybir.dt.float32r

P = 128
D = 256
DC = D // P
NB, S = 4, 1024
WPB = S // P
NT = NB * WPB
G = 4
NG = NT // G
SLOTS = WPB + 1
CTX = 77
XH, XD = 16, 16
XHC = P // XD
KVC = P + XHC
LAYERS = 2
H, HD = 8, 64
INNER = H * HD
HP = H // 2
HID = 682
MC = 114
NM = 6
MW = [MC] * (NM - 1) + [HID - MC * (NM - 1)]
AW = DC * 3 * INNER + HP * D
PIECES = 8
MASKED = -1e30
LN_SCALE = 2.0 ** 20
EPS5, EPS6 = 1e-5, 1e-6


def position_tables():
    half = np.arange(0, HD, 2, dtype=np.float32)
    inv = (np.float32(1.0) / np.float32(10000.0) ** (half / np.float32(HD))).astype(np.float32)
    t = np.arange(S, dtype=np.float32)
    freqs = (t[:, None] * inv[None, :]).astype(np.float32)
    freqs = np.concatenate([freqs, freqs], -1)
    base = ((half + np.float32(0.4 * HD)) / np.float32(1.4 * HD)).astype(np.float32)
    power = ((t - S // 2) / np.float32(64.0)).astype(np.float32)
    scale = (base[None, :] ** power[:, None]).astype(np.float32)
    scale = np.concatenate([scale, scale], -1)
    cos, sin = np.cos(freqs), np.sin(freqs)
    sign = np.concatenate([np.ones(HD // 2), -np.ones(HD // 2)]).astype(np.float32)
    t4 = np.stack([np.stack([cos * scale, sin * scale * sign], 1),
                   np.stack([cos / scale, sin / scale * sign], 1)], 1).astype(np.float32)
    return np.ascontiguousarray(t4.reshape(WPB, P, 2, 2, HD).transpose(1, 0, 2, 3, 4))


def block_order(u):
    return (1, 0) if u else (0, 1)


def masks():
    q, k = np.arange(P)[:, None], np.arange(P)[None, :]
    m = np.zeros((P, 2, G, 2, P), np.float32)
    for half in range(2):
        for u in range(G):
            cur, prev = block_order(u)
            m[:, half, u, cur] = np.where(k > q, MASKED, 0.0)
            m[:, half, u, prev] = MASKED if half == 0 and u == 0 else np.where(k < q, MASKED, 0.0)
    return m


def block_diagonal():
    f = np.arange(P)[:, None] // XD
    c = np.concatenate([np.arange(P) // XD, np.arange(XHC)])[None, :]
    return np.repeat((f == c).astype(np.float32)[:, None, :], DC, 1)


def program(nc, x, ctx_in, mask_in, g_xattn, g_ffn, wq, wk, wv, xg, xb, dw, db,
            wqkv, q_scale, k_scale, wo, ln_g, ln_b, w1, b1, w2, b2,
            tables_in, masks_in, blocks_in, ident_in, out):
    ctx = ExitStack()
    with ctx:
        bottom = -(-nc.sbuf_base // 64) * 64
        place = {"": bottom}

        def sb(name, shape, dt=F32, over=None, skip=0):
            words = int(np.prod(shape[1:])) * (2 if dt == BF16 else 4) // 4
            place[name] = place[over] + 4 * skip if over else place[""]
            if not over:
                place[""] += -(-words * 4 // 64) * 64
            return nc.alloc_sbuf_tensor_at(name, shape, dt, offset=place[name])

        def sem(name):
            return ctx.enter_context(nc.semaphore(name))

        state = sb("state", [P, NB * SLOTS, D])
        ident = sb("ident", [P, P])
        identb = sb("identb", [P, P], BF16)
        tanh_g = sb("tanh_g", [P, 2])
        attn_hi_sb = sb("attn_hi_sb", [P, AW], F32R)
        attn_lo_sb = sb("attn_lo_sb", [P, AW], F32R)
        attn_w = sb("attn_w", [P, AW], over="attn_lo_sb")
        w1_hi, w1_lo = (sb(n, [P, DC * 2 * HID], F32R) for n in ("w1_hi", "w1_lo"))
        w1_flat = sb("w1_flat", [P, DC * 2 * HID], over="w1_lo")
        w2_s = [sb(n, [MC, NM, D], F32R) for n in ("w2_hi", "w2_lo")]
        w2_in = sb("w2_in", [MC, NM, D], over="w2_lo")

        def attn_views(w):
            return (w[:, 0:DC * 3 * INNER].rearrange("p (c n) -> p c n", c=DC),
                    w[:, DC * 3 * INNER:AW].rearrange("p (c n) -> p c n", c=HP))

        def w1_view(w):
            return w[:, :].rearrange("p (c n) -> p c n", c=DC)

        wqkv_in, wo_in = attn_views(attn_w)
        wqkv_s, wo_s = zip(attn_views(attn_hi_sb), attn_views(attn_lo_sb))
        w1_in, w1_s = w1_view(w1_flat), (w1_view(w1_hi), w1_view(w1_lo))
        x1 = sb("x1", [P, NT, D], over="attn_hi_sb")
        lnc = sb("lnc", [P, 2, DC])
        b1c = sb("b1c", [MC, 2, NM])
        b2r = sb("b2r", [P, D])
        qks = sb("qks", [P, 2, HD])
        tab = sb("tab", [P, WPB, 2, 2, HD])
        mask_sb = sb("mask_sb", [P, 2, G, 2, P], BF16)
        hs = sb("hs", [P, 2, D])
        hT = sb("hT", [P, 2, DC, P], F32R)
        probs = sb("probs", [P, 2, 4, 2 * P])
        pT = sb("pT", [P, 2, 4, 2, P])
        kH = sb("kH", [P, 2, HP, G, P], F32R)
        kL = sb("kL", [P, HP, G, P], F32R)
        vring = sb("vring", [P, G, INNER])
        sq = sb("sq", [P, 2, INNER])
        ssum = sb("ssum", [P, 2 * H])
        lns = sb("lns", [P, 2 * H])
        y0 = sb("y0", [P, 2 * H])
        ya = sb("ya", [P, 2 * H])
        yb = sb("yb", [P, 2 * H])
        rn = sb("rn", [P, 2, 2 * H])
        khat = sb("khat", [P, INNER])
        rot = sb("rot", [P, 2, 2, INNER])
        qS = sb("qS", [P, 2, HP, P], F32R)
        negmax = sb("negmax", [P, 2, H])
        rowmax = sb("rowmax", [P, 2, H])
        lsum = sb("lsum", [P, 2, H])
        linv = sb("linv", [P, H])
        onorm = sb("onorm", [P, INNER])
        oT = sb("oT", [P, 2, HP, P], F32R)
        hf = sb("hf", [P, G, D])
        fst = sb("fst", [P, G, 2, 6])
        fmv = sb("fmv", [P, G, 2])
        fve = sb("fve", [P, G])
        frs = sb("frs", [P, G])
        hn = sb("hn", [P, G, D], over="rot")
        hnTl = sb("hnTl", [P, DC, G * P], F32R, over="rot", skip=G * D)
        hnT = sb("hnT", [P, DC, G * P], over="hnTl")
        hnTh = sb("hnTh", [P, DC, G * P], F32R, over="sq")
        hidl = sb("hidl", [P, NM, G * P], F32R, over="probs")
        hid = sb("hid", [P, NM, G * P], over="probs")
        hidh = sb("hidh", [P, NM, G * P], F32R, over="probs", skip=NM * G * P)
        gel = sb("gel", [P, 2, G * P], over="probs", skip=2 * NM * G * P)
        one = sb("one", [P, 1])
        fence = sb("fence", [P, 1])
        minus_half = sb("minus_half", [P, G])
        half_log = sb("half_log", [P, 1])

        ps = [ctx.enter_context(nc.psum_tensor(f"ps{i}", [P, 512], F32)) for i in range(8)]

        xw = sb("xw", [P, DC, 3 * D], over="w1_hi")
        dw_sb = sb("dw_sb", [P, DC, D], over="w1_hi", skip=DC * 3 * D)
        gam_r = sb("gam_r", [P, D])
        bet_r = sb("bet_r", [P, D])
        db_r = sb("db_r", [P, D])
        gT = sb("gT", [P, D])
        bT = sb("bT", [P, D])
        xgc = sb("xgc", [P, 2, DC])
        em = sb("em", [CTX, NB])
        blocks = sb("blocks", [P, DC, KVC])
        kvs = sb("kvs", [P, NB, DC, KVC], over="kH")
        cst = sb("cst", [P, 2 * G, 6])
        cmv = sb("cmv", [P, 2 * G, 2])
        cve = sb("cve", [P, 2 * G])
        crs = sb("crs", [P, 2 * G])
        eps_row = sb("eps_row", [P, D])
        mh8 = sb("mh8", [P, 2 * G])
        norms = ("lnx", "lnq", "lno0", "lno1", "lnf0", "lnf1")
        cst_of, cmv_of, cve_of, crs_of, cnm_of = (
            {t: sb(f"{t}_{w}", [P, *shape]) for t in norms}
            for w, shape in (("st", (G, 6)), ("mv", (G, 2)), ("ve", (G,)), ("rs", (G,)), ("nm", (G,))))
        minus_one = sb("minus_one", [P, G])
        kvh = sb("kvh", [CTX, NB, 2, D], over="vring")
        kp = sb("kp", [CTX, NB, D], over="sq")
        vp = sb("vp", [CTX, NB, DC, KVC], over="pT")
        zinv = sb("zinv", [P, G, XH])
        ctx_sb = sb("ctx_sb", [CTX, NB, D], over="hf")
        ctxT = sb("ctxT", [P, DC, NB, P], over="kL")
        xn = sb("xn", [P, G, D], over="probs")
        xnT = sb("xnT", [P, 2, DC, 2 * P], over="probs", skip=G * D)
        qn = sb("qn", [P, G, D], over="hf")
        reluT = sb("reluT", [P, DC, WPB, 2, S // 16], over="rot")
        qTs = sb("qTs", [P, DC, WPB, P], over="vring")
        att = sb("att", [P, XH, WPB, XD], over="pT")
        attT = sb("attT", [P, DC, S], over="kH", skip=2048)
        yx = [sb("yx0", [P, G, D], over="kL"), sb("yx1", [P, G, D], over="kL", skip=G * D)]

        def sems(names):
            return [sem(n) for n in names.split()]

        d_const, d_x, d_small, d_attn_w, d_ffn_w, d_hs, d_hf, d_x1_back, d_out = sems(
            "d_const d_x d_small d_attn_w d_ffn_w d_hs d_hf d_x1_back d_out")
        d_x_first = sems("d_x_0 d_x_1")
        d_x1 = sems("d_x1_0 d_x1_1")
        consts_set, zeroed, rings_zeroed, ones_set, tanh_done, folded, tab_ready = sems(
            "consts_set zeroed rings_zeroed ones_set tanh_done folded tab_ready")
        attn_hi, attn_lo, attn_lo_pool, w1_rounded, w1_split, w2_rounded, w2_split = sems(
            "attn_hi attn_lo attn_lo_pool w1_rounded w1_split w2_rounded w2_split")
        ctxT_ps, ctxT_ready, ctx_projected, ctx_stats, ctx_moments, ctx_var, ctx_rstd, ctx_normed, ctx_features = sems(
            "ctxT_ps ctxT_ready ctx_projected ctx_stats ctx_moments ctx_var ctx_rstd ctx_normed ctx_features")
        key_values_ps, key_values_ready = sems("key_values_ps key_values_ready")
        NORM = {t: sems(f"{t}_stats {t}_moments {t}_var {t}_rstd {t}_normed") for t in ("lnx", "lnq")}
        NORM |= {t: sems(f"{t}_stats {t}_moments {t}_var {t}_rstd") for t in ("lno0", "lno1", "lnf0", "lnf1")}
        x_ready = sem("x_ready")
        y_scaled = sem("y_scaled")
        for t in range(2):
            NORM[f"lno{t}"].append(y_scaled)
            NORM[f"lnf{t}"].append(x_ready)
        mean_negated = {t: sem(f"{t}_mean_negated") for t in ("lnx", "lnq", "lnf0", "lnf1")}
        std_inverted = {t: sem(f"{t}_std_inverted") for t in ("lnx", "lnq", "lnf0", "lnf1")}
        beta_added, xT_ps, xT_ready, queries_ps, qT_ps, relu_ready, qprime_ready, attended = sems(
            "beta_added xT_ps xT_ready queries_ps qT_ps relu_ready qprime_ready attended")
        z_sums_ready, z_ready, att_ready, attT_ps, attT_ready, dense_done, y_ready, x1_ready = sems(
            "z_sums_ready z_ready att_ready attT_ps attT_ready dense_done y_ready x1_ready")
        hT_ps, hT_ready, hTlo_ready, proj_done, v_ready, squared, summed, clipped, logged, guessed, newton = sems(
            "hT_ps hT_ready hTlo_ready proj_done v_ready squared summed clipped logged guessed newton")
        q_prod, khat_ready, k_prod, qkT_ps, q_hi, q_lo, k_hi, k_lo = sems(
            "q_prod khat_ready k_prod qkT_ps q_hi q_lo k_hi k_lo")
        scored, maxed, bias_ready, exped, pT_ps, pTA_ready, pTB_ready, pv_done = sems(
            "scored maxed bias_ready exped pT_ps pTA_ready pTB_ready pv_done")
        linv_ready, on_ready, oT_ps, oT_ready, oTlo_ready, wo_done, x_attn = sems(
            "linv_ready on_ready oT_ps oT_ready oTlo_ready wo_done x_attn")
        ffn_stats, ffn_moments, ffn_var, ffn_rstd, hn_ready, hnT_ps, hnT_ready, hnT_hi, hnT_lo = sems(
            "ffn_stats ffn_moments ffn_var ffn_rstd hn_ready hnT_ps hnT_ready hnT_hi hnT_lo")
        expanded, gelu_ready, hid_ready, hid_hi, hid_lo, contracted, x_ffn, summed_out = sems(
            "expanded gelu_ready hid_ready hid_hi hid_lo contracted x_ffn summed_out")

        block = ctx.enter_context(nc.Block())

        N_CONST = 15
        HALF_SPLIT = ((0, 0), (0, 1), (1, 0))

        def f32(ap):
            return ap.bitcast(F32)

        def slot(k, u):
            v = G * k + (k >> 1) + u + 1
            return v if isinstance(v, int) else v.with_bounds(min_val=1, max_val=NB * SLOTS - G + u)

        def attn_parts():
            return [tuple(w[:, :, i * INNER:(i + 1) * INNER] for w in (wqkv_in, *wqkv_s)) for i in range(3)]\
                + [(wo_in, *wo_s)]

        x_view = x.rearrange("b (w p) d -> p (b w) d", p=P)
        out_view = out.rearrange("b (w p) d -> p (b w) d", p=P)

        @block.sync
        def _(sp):
            def load_x(k):
                sp.dma_start(state[:, slot(k, 0):slot(k, 0) + G, :], x_view[:, k * G:(k + 1) * G, :])\
                  .then_inc(d_x_first[k] if k < 2 else d_x, 16)

            sp.dma_start(ctx_sb[:, :, :], ctx_in.rearrange("b p d -> p b d")).then_inc(d_const, 16)
            sp.dma_start(ident[:, :], ident_in).then_inc(d_const, 16)
            for i, w in enumerate((wq, wk, wv)):
                sp.dma_start(xw[:, :, i * D:(i + 1) * D], w.rearrange("(c p) n -> p c n", p=P)).then_inc(d_const, 16)
            for k in range(2):
                load_x(k)
            sp.dma_start(dw_sb[:, :, :], dw.rearrange("(c p) n -> p c n", p=P)).then_inc(d_const, 16)
            sp.dma_start(blocks[:, :, :], blocks_in).then_inc(d_const, 16)
            for r, v in ((gam_r, xg), (bet_r, xb), (db_r, db)):
                sp.dma_start(r[:, :], v.partition_broadcast(P)).then_inc(d_const, 16)
            sp.dma_start(tanh_g[:, 0:1], g_xattn.partition_broadcast(P)).then_inc(d_const, 16)
            sp.dma_start(tanh_g[:, 1:2], g_ffn.partition_broadcast(P)).then_inc(d_const, 16)
            with nc.allow_non_contiguous_dma(reason="columns of small vectors"):
                sp.dma_start(xgc[:, 0, :], xg.rearrange("(c p) -> p c", p=P)).then_inc(d_const, 16)
                sp.dma_start(xgc[:, 1, :], xb.rearrange("(c p) -> p c", p=P)).then_inc(d_const, 16)
                sp.dma_start(em[:, :], mask_in.rearrange("b p -> p b")).then_inc(d_const, 16)
            for k in range(2, NG):
                load_x(k)

            def load_attn_weights(l):
                sp.dma_start(wqkv_in, wqkv[l].rearrange("(c p) n -> p c n", p=P)).then_inc(d_attn_w, 16)
                sp.dma_start(wo_in, wo[l].rearrange("(c p) n -> p c n", p=P)).then_inc(d_attn_w, 16)
                sp.dma_start(tab[:, :, :, :, :], tables_in).then_inc(d_attn_w, 16)
                sp.dma_start(qks[:, 0, :], q_scale[l].partition_broadcast(P)).then_inc(d_attn_w, 16)
                sp.dma_start(qks[:, 1, :], k_scale[l].partition_broadcast(P)).then_inc(d_attn_w, 16)

            def load_ffn_weights(l):
                sp.dma_start(w1_in, w1[l].rearrange("(c p) n -> p c n", p=P)).then_inc(d_ffn_w, 16)
                sp.dma_start(w2_in[0:MC, 0:NM - 1, :], w2[l][0:MC * (NM - 1), :].rearrange("(m p) n -> p m n", p=MC))\
                  .then_inc(d_ffn_w, 16)
                sp.dma_start(w2_in[0:MW[-1], NM - 1, :], w2[l][MC * (NM - 1):HID, :]).then_inc(d_ffn_w, 16)
                sp.dma_start(b2r[:, :], b2[l].partition_broadcast(P)).then_inc(d_ffn_w, 16)
                with nc.allow_non_contiguous_dma(reason="columns of small vectors"):
                    sp.dma_start(lnc[:, 0, :], ln_g[l].rearrange("(c p) -> p c", p=P)).then_inc(d_ffn_w, 16)
                    sp.dma_start(lnc[:, 1, :], ln_b[l].rearrange("(c p) -> p c", p=P)).then_inc(d_ffn_w, 16)
                    for a in range(2):
                        v = b1[l][a * HID:(a + 1) * HID]
                        sp.dma_start(b1c[:, a, 0:NM - 1], v[0:MC * (NM - 1)].rearrange("(m p) -> p m", p=MC))\
                          .then_inc(d_ffn_w, 16)
                        sp.dma_start(b1c[0:MW[-1], a, NM - 1:NM], v[MC * (NM - 1):HID].rearrange("(m p) -> p m", m=1))\
                          .then_inc(d_ffn_w, 16)

            def load_shifted(dst, s, s_before, n, done):
                half = slice(P, D)
                sp.dma_start(dst[:, :, 0:P], state[:, bass.ds(s, n), 0:P]).then_inc(done, 16)
                sp.dma_start(dst[1:P - 1, :, half], state[0:P - 2, bass.ds(s, n), half]).then_inc(done, 16)
                sp.dma_start(dst[P - 1:P, :, half], state[P - 2:P - 1, bass.ds(s, n), half]).then_inc(done, 16)
                sp.dma_start(dst[0:1, :, half], state[P - 1:P, bass.ds(s_before, n), half]).then_inc(done, 16)

            load_ffn_weights(0)
            load_attn_weights(0)
            for k in range(NG):
                sp.wait_ge(x1_ready, G * (k + 1))
                sp.dma_start(out_view[:, k * G:(k + 1) * G, :], yx[k % 2][:, :, :]).then_inc(d_x1[k % 2], 16)
            sp.wait_ge(zeroed, 1)
            def load_pair(tile, first, before):
                sp.wait_ge(x_ready, tile + 2)
                sp.wait_ge(hT_ps, tile)
                load_shifted(hs, first, before, 2, d_hs)

            def load_group(tile, first, before):
                sp.wait_ge(x_attn, tile + G)
                sp.wait_ge(hn_ready, tile)
                load_shifted(hf, first, before, G, d_hf)

            load_pair(0, 1, 0)
            for l in range(LAYERS):
                load_pair(l * NT + 2, 3, 2)
                if l:
                    sp.wait_ge(x_ready, (l + 1) * NT)
                    load_ffn_weights(l)
                with sp.Fori(l * NT + 4, (l + 1) * NT, 2) as tile:
                    first = sp.snap((tile + (tile >> 3) + 1 - l * NB * SLOTS).with_bounds(min_val=1, max_val=NB * SLOTS - 2))
                    load_pair(tile, first, sp.snap(first - 1))
                load_group(l * NT, 1, 0)
                sp.wait_ge(x_attn, (l + 1) * NT)
                load_group(l * NT + G, G + 1, G)
                if l + 1 < LAYERS:
                    load_attn_weights(l + 1)
                else:
                    for k in range(NG):
                        sp.dma_start(x1[:, k * G:(k + 1) * G, :], out_view[:, k * G:(k + 1) * G, :])\
                          .then_inc(d_x1_back, 16)
                with sp.Fori(l * NT + 2 * G, (l + 1) * NT, G) as tile:
                    first = sp.snap((tile + (tile >> 3) + 1 - l * NB * SLOTS).with_bounds(min_val=1, max_val=NB * SLOTS - G))
                    load_group(tile, first, sp.snap(first - 1))
                if l + 1 < LAYERS:
                    load_pair((l + 1) * NT, 1, 0)
            with sp.Fori(0, NG) as g:
                sp.wait_ge(summed_out, g + 1)
                sp.dma_start(out_view[:, bass.ds(g * G, G), :], x1[:, bass.ds(g * G, G), :]).then_inc(d_out, 16)
            sp.wait_ge(d_out, 16 * NG)

        @block.gpsimd
        def _(pool):
            pool.dma_start(mask_sb[:, :, :, :, :], masks_in).then_inc(d_small, 16)
            pool.dma_start(identb[:, :], ident_in).then_inc(d_small, 16)
            pool.memset(one[:, :], 1.0)
            pool.memset(minus_one[:, :], -1.0)
            pool.memset(minus_half[:, :], -0.5)
            pool.memset(eps_row[:, :], EPS6)
            pool.memset(mh8[:, :], -0.5).then_inc(consts_set, 1)
            pool.memset(state[:, :, :].rearrange("p (b s) d -> p b s d", b=NB)[:, :, 0, :], 0.0).then_inc(zeroed, 1)
            pool.wait_ge(consts_set, 1)

            pool.wait_ge(ctx_var, 1)
            pool.tensor_tensor(crs[0:CTX, :], cve[0:CTX, :], mh8[0:CTX, :], ALU.pow).then_inc(ctx_rstd, 1)

            def rstd(t, k):
                pool.wait_ge(NORM[t][2], k + 1)
                pool.tensor_tensor(crs_of[t][:, :], cve_of[t][:, :], mh8[:, 0:G], ALU.pow).then_inc(NORM[t][3], 1)

            def rstd_and_shift(t, k):
                pool.wait_ge(NORM[t][2], k + 1)
                pool.wait_ge(NORM[t][4], G * k)
                pool.tensor_tensor(crs_of[t][:, :], cve_of[t][:, :], mh8[:, 0:G], ALU.pow).then_inc(std_inverted[t], 1)
                pool.tensor_tensor(cnm_of[t][:, :], cmv_of[t][:, :, 0], minus_one[:, :], ALU.mult).then_inc(mean_negated[t], 1)
                pool.wait_ge(std_inverted[t], k + 1)
                pool.wait_ge(mean_negated[t], k + 1)
                pool.tensor_tensor(cnm_of[t][:, :], cnm_of[t][:, :], crs_of[t][:, :], ALU.mult).then_inc(NORM[t][3], 1)

            def add_beta(k):
                pool.wait_ge(folded, 1)
                for j in range(G):
                    pool.wait_ge(NORM["lnx"][4], G * k + j + 1)
                    tile = state[:, bass.ds(slot(k, j), 1), :].rearrange("p a d -> p (a d)")
                    pool.tensor_tensor(tile, tile, bT[:, :], ALU.add).then_inc(beta_added, 1)

            for k in range(2):
                rstd_and_shift("lnx", k)
                rstd_and_shift("lnq", k)
                add_beta(k)

            def sequence(b, nxt):
                k = 2 * b + 2
                if nxt:
                    rstd_and_shift("lnx", k)
                    rstd_and_shift("lnq", k)
                    rstd_and_shift("lnx", k + 1)
                    add_beta(k)
                rstd("lno0", b)
                rstd("lno1", b)
                (rstd_and_shift if nxt else rstd)("lnf0", b)
                if nxt:
                    rstd_and_shift("lnq", k + 1)
                (rstd_and_shift if nxt else rstd)("lnf1", b)
                if nxt:
                    add_beta(k + 1)

            with pool.Fori(0, NB - 1) as b:
                sequence(b, True)
            sequence(NB - 1, False)

            for s in range(2):
                pool.wait_ge(d_x1[s], 16 * NB)
            with pool.Fori(0, LAYERS) as l:
                for i, (loaded, hi, lo) in enumerate(attn_parts()[2:4]):
                    pool.wait_ge(attn_hi, 4 * l + i + 3)
                    pool.tensor_tensor(lo, loaded, f32(hi), ALU.subtract).then_inc(attn_lo_pool, 1)
                pool.wait_ge(x_ready, (l + 1) * NT)
                pool.tensor_tensor(fence[:, :], one[:, :], one[:, :], ALU.mult)
                for i in range(2):
                    pool.memset(f32(kH[:, i, :, G - 1, :]), 0.0).then_inc(rings_zeroed, 1)
                pool.memset(f32(kL[:, :, G - 1, :]), 0.0).then_inc(rings_zeroed, 1)
                pool.memset(vring[:, G - 1, :], 0.0).then_inc(rings_zeroed, 1)

                def rotate_keys(t, w):
                    pool.wait_ge(khat_ready, t + 1)
                    pool.wait_ge(qkT_ps, 2 * t)
                    src = khat[:, :].rearrange("p (h d) -> p h d", h=H)
                    pool.tensor_tensor(rot[:, 1, 0, :].rearrange("p (h d) -> p h d", h=H), src,
                                       tab[:, bass.ds(w, 1), 1, 0, :].to_broadcast((P, H, HD)), ALU.mult)
                    dst = rot[:, 1, 1, :].rearrange("p (h a e) -> p h a e", h=H, a=2)
                    src = khat[:, :].rearrange("p (h a e) -> p h a e", h=H, a=2)
                    for a in range(2):
                        ins = pool.tensor_tensor(
                            dst[:, :, 1 - a, :], src[:, :, a, :],
                            tab[:, bass.ds(w, 1), 1, 1, a * 32:a * 32 + 32].to_broadcast((P, H, 32)), ALU.mult)
                    ins.then_inc(k_prod, 1)

                def split_w1(k):
                    width = DC * 2 * HID // PIECES
                    piece = bass.ds(k * width, width)
                    pool.wait_ge(d_ffn_w, (l + 1) * 16 * 10)
                    pool.tensor_tensor(w1_hi[:, piece], w1_flat[:, piece], one[:, 0:1].to_broadcast((P, width)), ALU.mult)\
                        .then_inc(w1_rounded, 1)
                    pool.wait_ge(w1_rounded, l * PIECES + k + 1)
                    pool.tensor_tensor(fence[:, :], one[:, :], one[:, :], ALU.mult)
                    pool.tensor_tensor(w1_lo[:, piece], w1_flat[:, piece], f32(w1_hi[:, piece]), ALU.subtract)\
                        .then_inc(w1_split, 1)

                def split_w2():
                    parts = ((slice(0, MC), slice(0, NM - 1)), (slice(0, MW[-1]), slice(NM - 1, NM)))
                    for rows, m in parts:
                        width = (m.stop - m.start) * D
                        pool.tensor_tensor(w2_s[0][rows, m, :].rearrange("p m n -> p (m n)"),
                                           w2_in[rows, m, :].rearrange("p m n -> p (m n)"),
                                           one[rows, 0:1].to_broadcast((rows.stop, width)), ALU.mult).then_inc(w2_rounded, 1)
                    for i, (rows, m) in enumerate(parts):
                        pool.wait_ge(w2_rounded, 2 * l + i + 1)
                        pool.tensor_tensor(w2_s[1][rows, m, :], w2_in[rows, m, :], f32(w2_s[0][rows, m, :]),
                                           ALU.subtract).then_inc(w2_split, 1)

                pool.wait_ge(tab_ready, l + 1)
                rotate_keys(l * NT, 0)
                with pool.Fori(0, NG - 1) as k:
                    for u in range(G):
                        rotate_keys(l * NT + G * k + u + 1, (G * k + u + 1) & (WPB - 1))
                        if u == 1:
                            split_w1(k)
                split_w1(PIECES - 1)
                split_w2()
                for u in range(G - 1):
                    rotate_keys(l * NT + G * (NG - 1) + u + 1, (G * (NG - 1) + u + 1) % WPB)

                def group_rstd(g):
                    pool.wait_ge(ffn_var, l * NG + g + 1)
                    pool.tensor_tensor(frs[:, :], fve[:, :], minus_half[:, :], ALU.pow).then_inc(ffn_rstd, 1)

                def add_b2(g):
                    for j in range(G):
                        pool.wait_ge(x_ffn, l * NT + G * g + j + 1)
                        tile = state[:, bass.ds(slot(g, j), 1), :].rearrange("p a d -> p (a d)")
                        pool.tensor_tensor(tile, tile, b2r[:, :], ALU.add).then_inc(x_ready, 1)

                def split_hnT(g):
                    for c in range(DC):
                        pool.wait_ge(hnT_hi, (l * NG + g) * DC + c + 1)
                        pool.tensor_tensor(hnTl[:, c, :], hnT[:, c, :], f32(hnTh[:, c, :]), ALU.subtract)\
                            .then_inc(hnT_lo, 1)

                def split_hid(g, nxt):
                    for m in range(NM):
                        pool.wait_ge(hid_hi, (l * NG + g) * NM + m + 1)
                        pool.tensor_tensor(hidl[0:MW[m], m, :], hid[0:MW[m], m, :], f32(hidh[0:MW[m], m, :]),
                                           ALU.subtract).then_inc(hid_lo, 1)
                        if nxt and m == 1:
                            group_rstd(g + 1)

                group_rstd(0)
                split_hnT(0)
                with pool.Fori(0, NG - 1) as g:
                    split_hid(g, True)
                    split_hnT(g + 1)
                    add_b2(g)
                split_hid(NG - 1, False)
                add_b2(NG - 1)

        @block.scalar
        def _(act):
            act.wait_ge(d_const, 16 * N_CONST)
            act.activation(tanh_g[:, :], tanh_g[:, :], ACT.Tanh).then_inc(tanh_done, 1)

            for b in range(NB):
                act.wait_ge(ctxT_ps, b + 1)
                act.activation(ctxT[:, :, b, 0:CTX], ps[b][:, 0:D].rearrange("p (c t) -> p c t", c=DC)[:, :, 0:CTX],
                               ACT.Copy).then_inc(ctxT_ready, 1)

            def normalise(t, k, src, dst):
                for j in range(G):
                    act.wait_ge(NORM[t][3], k + 1)
                    act.activation(dst(j), src(j), ACT.Identity, bias=cnm_of[t][:, j:j + 1],
                                   scale=crs_of[t][:, j:j + 1]).then_inc(NORM[t][4], 1)

            def x_tile(k, j):
                return state[:, bass.ds(slot(k, j), 1), :].rearrange("p a d -> p (a d)")

            def x_in(k):
                normalise("lnx", k, lambda j: x_tile(k, j), lambda j: xn[:, j, :])
                for i in range(2):
                    act.wait_ge(xT_ps, 2 * k + i + 1)
                    act.activation(xnT[:, i, :, :], ps[i][:, :].rearrange("p (c t) -> p c t", c=DC), ACT.Copy)\
                       .then_inc(xT_ready, 1)

            def q_in(k):
                normalise("lnq", k, lambda j: ps[2 + j // 2][:, (j % 2) * D:(j % 2 + 1) * D], lambda j: qn[:, j, :])

            def inner_input(b, s):
                normalise(f"lnf{s}", b, lambda j: yx[s][:, j, :], lambda j: x_tile(2 * b + s, j))

            def q_out(k, s):
                for i in range(2):
                    act.wait_ge(qT_ps, 2 * k + i + 1)
                    a0 = (2 * s + i) * 2 * P // 16
                    for c in range(DC):
                        act.activation(reluT[:, c, :, :, a0:a0 + 2 * P // 16],
                                       ps[i][:, c * D:(c + 1) * D].rearrange("p (a i m) -> p m i a", i=2, m=WPB),
                                       ACT.Relu, bias=xgc[:, 1, c:c + 1], scale=xgc[:, 0, c:c + 1]).then_inc(relu_ready, 1)

            for k in range(2):
                x_in(k)
                q_in(k)
                q_out(k, k)

            def sequence(b, nxt):
                k = 2 * b + 2
                if nxt:
                    x_in(k)
                for n in range(4):
                    act.wait_ge(attT_ps, 4 * b + n + 1)
                    act.activation(attT[:, :, n * 2 * P:(n + 1) * 2 * P].rearrange("p i (h a) -> p i h a", h=4),
                                   ps[4 + n][:, :].rearrange("p (h i a) -> p i h a", h=4, i=2), ACT.Copy)\
                       .then_inc(attT_ready, 1)
                if nxt:
                    q_in(k)
                    q_out(k, 0)
                    x_in(k + 1)
                    q_in(k + 1)
                    q_out(k + 1, 1)
                    for s in range(2):
                        inner_input(b, s)

            with act.Fori(0, NB - 1) as b:
                sequence(b, True)
            sequence(NB - 1, False)

            with act.Fori(0, LAYERS) as l:
                act.preload_act_table_set("natural_log_exp_and_others")
                act.wait_ge(d_attn_w, (l + 1) * 16 * 5)
                for loaded, hi, _ in attn_parts():
                    act.activation(hi, loaded, ACT.Copy).then_inc(attn_hi, 1)

                def copy_hT(t):
                    act.wait_ge(hT_ps, t + 1)
                    act.activation(hT[:, 0, :, :], ps[6][:, 0:D].rearrange("p (c t) -> p c t", c=DC), ACT.Copy)\
                       .then_inc(hT_ready, 1)

                def square(t, n):
                    act.wait_ge(summed, 2 * t + n)
                    act.wait_ge(proj_done, 3 * t + n + 2)
                    if n:
                        act.wait_ge(q_prod, t + 1)
                    act.activation(sq[:, n, :], ps[5 - n][:, :], ACT.Square).then_inc(squared, 1)

                def guess_rsqrt(t, n):
                    cols = slice(n * H, n * H + H)
                    act.wait_ge(clipped, 2 * t + n + 1)
                    act.activation(lns[:, cols], ssum[:, cols], ACT.Ln, scale=LN_SCALE).then_inc(logged, 1)
                    act.wait_ge(logged, 2 * t + n + 1)
                    act.activation(y0[:, cols], lns[:, cols], ACT.Exp, scale=-0.5, bias=half_log[:, 0:1]).then_inc(guessed, 1)

                def copy_v(t, u):
                    act.wait_ge(proj_done, 3 * t + 1)
                    act.activation(vring[:, u, :], ps[6][:, :], ACT.Copy).then_inc(v_ready, 1)

                def round_qk(t, u):
                    for i in range(2):
                        own = slice(HD * i, HD * i + HD)
                        act.wait_ge(qkT_ps, 2 * t + 1)
                        act.activation(qS[own, i, :, :], ps[4][own, :].rearrange("p (h t) -> p h t", h=HP), ACT.Copy)\
                           .then_inc(q_hi, 1)
                    for i in range(2):
                        own = slice(HD * i, HD * i + HD)
                        act.wait_ge(qkT_ps, 2 * t + 2)
                        for j in (i, 1 - i):
                            act.activation(kH[HD * j:HD * j + HD, i, :, u, :],
                                           ps[5][own, :].rearrange("p (h t) -> p h t", h=HP), ACT.Copy).then_inc(k_hi, 1)

                def exps(t, u, a, which=range(4)):
                    act.wait_ge(pT_ps, 2 * t)
                    for i in which:
                        h = 4 * a + 2 * (i % 2) + i // 2
                        act.wait_ge(bias_ready, 4 * t + 2 * a + i // 2 + 1)
                        act.activation(probs[:, a, i, :], ps[2 * a + i // 2][:, (i % 2) * D:(i % 2 + 1) * D], ACT.Exp,
                                       scale=rn[:, u % 2, H + h:H + h + 1], bias=negmax[:, u % 2, h:h + 1],
                                       accum_out=lsum[:, u % 2, h:h + 1]).then_inc(exped, 1)

                def copy_pT(t, a):
                    act.wait_ge(pT_ps, 2 * t + a + 1)
                    act.wait_ge(pv_done, 2 * t)
                    for i in range(2):
                        ins = act.activation(pT[:, a, 2 * i:2 * i + 2, :, :],
                                             ps[2 * a + i][:, :].rearrange("p (h b q) -> p h b q", h=2, b=2), ACT.Copy)
                    ins.then_inc((pTA_ready, pTB_ready)[a], 1)

                def step(t, u, nxt, prev, next2):
                    exps(t, u, 0)
                    if nxt:
                        square(t + 1, 0)
                    exps(t, u, 1)
                    if nxt:
                        guess_rsqrt(t + 1, 0)
                    copy_pT(t, 0)
                    copy_pT(t, 1)
                    if nxt:
                        square(t + 1, 1)
                        guess_rsqrt(t + 1, 1)
                    if next2:
                        copy_hT(t + 2)
                    if nxt:
                        round_qk(t + 1, (u + 1) % G)
                    if next2:
                        copy_v(t + 2, (u + 2) % G)

                t0 = l * NT
                act.wait_ge(rings_zeroed, 4 * (l + 1))
                copy_hT(t0); copy_v(t0, 0); square(t0, 0); guess_rsqrt(t0, 0); square(t0, 1); guess_rsqrt(t0, 1)
                copy_hT(t0 + 1); round_qk(t0, 0); copy_v(t0 + 1, 1)
                for u in range(G):
                    step(t0 + u, u, True, u > 0, True)
                with act.Fori(1, NG - 1) as k:
                    for u in range(G):
                        step(t0 + G * k + u, u, True, True, True)
                for u in range(G):
                    step(t0 + G * (NG - 1) + u, u, u < G - 1, True, u < G - 2)

                def gelus(g):
                    for m in range(NM):
                        act.wait_ge(expanded, (l * NG + g) * 2 * NM + 2 * m + 1)
                        act.wait_ge(hid_ready, (l * NG + g) * NM + (m - 1 if m else 0))
                        act.activation(gel[0:MW[m], m % 2, :], ps[2 + 2 * (m % 2)][0:MW[m], :], ACT.Gelu,
                                       bias=b1c[0:MW[m], 1, m:m + 1]).then_inc(gelu_ready, 1)

                def copy_hnT(g):
                    act.wait_ge(expanded, (l * NG + g) * 2 * NM)
                    for c in range(DC):
                        act.wait_ge(hnT_ps, (l * NG + g) * DC + c + 1)
                        act.activation(hnT[:, c, :], ps[c][:, :], ACT.Identity,
                                       bias=lnc[:, 1, c:c + 1], scale=lnc[:, 0, c:c + 1]).then_inc(hnT_ready, 1)

                act.wait_ge(d_ffn_w, (l + 1) * 16 * 10)
                copy_hnT(0)
                with act.Fori(0, NG - 1) as g:
                    gelus(g)
                    copy_hnT(g + 1)
                gelus(NG - 1)

        @block.tensor
        def _(pe):
            pe.wait_ge(d_const, 16 * N_CONST)
            for b in range(NB):
                for c in range(DC):
                    mm = pe.transpose(ps[b][:, c * P:c * P + CTX], ctx_sb[:, b, c * P:(c + 1) * P], ident[0:CTX, 0:CTX])
                mm.then_inc(ctxT_ps, 1)
            for b in range(NB):
                pe.wait_ge(ctxT_ready, b + 1)
                for c in range(DC):
                    mm = pe.matmul(ps[4 + b][0:CTX, :], ctxT[:, c, b, 0:CTX], xw[:, c, D:3 * D],
                                   start=(c == 0), stop=(c == DC - 1))
                mm.then_inc(ctx_projected, 1)
            def key_values():
                for b in range(NB):
                    pe.wait_ge(ctx_features, 2 * b + 2)
                    for c in range(DC):
                        mm = pe.matmul(ps[4 + b][:, c * KVC:(c + 1) * KVC], kp[:, b, c * P:(c + 1) * P], vp[:, b, c, :],
                                       start=True, stop=True)
                    mm.then_inc(key_values_ps, 1)

            def transposes_x(k):
                for i in range(2):
                    pe.wait_ge(relu_ready, 4 * k)
                    for jj in range(2):
                        pe.wait_ge(NORM["lnx"][4], G * k + 2 * i + jj + 1)
                        for c in range(DC):
                            mm = pe.transpose(ps[i][:, c * D + jj * P:c * D + (jj + 1) * P],
                                              xn[:, 2 * i + jj, c * P:(c + 1) * P], ident[:, :])
                    mm.then_inc(xT_ps, 1)

            def queries(k):
                for i in range(2):
                    pe.wait_ge(NORM["lnq"][4], G * k)
                    pe.wait_ge(xT_ready, 2 * k + i + 1)
                    for jj in range(2):
                        for c in range(DC):
                            mm = pe.matmul(ps[2 + i][:, jj * D:(jj + 1) * D], xnT[:, i, c, jj * P:(jj + 1) * P],
                                           xw[:, c, 0:D], start=(c == 0), stop=(c == DC - 1))
                    mm.then_inc(queries_ps, 1)

            def transposes_q(k):
                for i in range(2):
                    for jj in range(2):
                        pe.wait_ge(NORM["lnq"][4], G * k + 2 * i + jj + 1)
                        for c in range(DC):
                            mm = pe.transpose(ps[i][:, c * D + jj * P:c * D + (jj + 1) * P],
                                              qn[:, 2 * i + jj, c * P:(c + 1) * P], ident[:, :])
                    mm.then_inc(qT_ps, 1)

            def attend(b, s):
                for j in range(G):
                    m = s * G + j
                    pe.wait_ge(qprime_ready, 2 * b + s + 1)
                    if s:
                        pe.wait_ge(att_ready, WPB * b + j + 1)
                    for c in range(DC):
                        mm = pe.matmul(ps[4 + j][:, c * KVC:(c + 1) * KVC], qTs[:, c, m, :],
                                       kvs[:, bass.ds(b, 1), c, :].rearrange("p a n -> p (a n)"),
                                       start=True, stop=True)
                    mm.then_inc(attended, 1)

            def transposes_att(b):
                pe.wait_ge(att_ready, WPB * b + WPB)
                for h in range(XH):
                    mm = pe.transpose(ps[4 + h // 4][:, h % 4 * P:(h % 4 + 1) * P],
                                      att[:, h, :, :].rearrange("p m e -> p (m e)"), ident[:, :])
                    if h % 4 == 3:
                        mm.then_inc(attT_ps, 1)

            def dense(b, s):
                for j in range(G):
                    t = s * G + j
                    pe.wait_ge(attT_ready, 4 * b + (2 * s + 2 if j < 2 else max(t // 2, 2 * s + 1) + 1))
                    for c in range(DC):
                        mm = pe.matmul(ps[4 + t // 2][:, (t % 2) * D:(t % 2 + 1) * D], attT[:, c, t * P:(t + 1) * P],
                                       dw_sb[:, c, :], start=(c == 0), stop=(c == DC - 1))
                    if j % 2:
                        mm.then_inc(dense_done, 1)

            pe.wait_ge(ctxT_ready, NB)
            for k in range(2):
                transposes_x(k)
                queries(k)
                if k == 0:
                    key_values()
                transposes_q(k)
            pe.wait_ge(key_values_ready, NB)

            def sequence(b, nxt):
                k = 2 * b + 2
                pe.wait_ge(y_ready, WPB * b)
                attend(b, 0)
                if nxt:
                    transposes_x(k)
                attend(b, 1)
                if nxt:
                    queries(k)
                transposes_att(b)
                dense(b, 0)
                if nxt:
                    transposes_q(k)
                dense(b, 1)
                if nxt:
                    transposes_x(k + 1)
                if nxt:
                    queries(k + 1)
                    transposes_q(k + 1)

            with pe.Fori(0, NB - 1) as b:
                sequence(b, True)
            sequence(NB - 1, False)

            pe.wait_ge(d_small, 32)
            with pe.Fori(0, LAYERS) as l:
                def project(t, which):
                    pe.wait_ge(hTlo_ready, t + 1)
                    for i in which:
                        for c in range(DC):
                            for n, (a, b) in enumerate(HALF_SPLIT):
                                mm = pe.matmul(ps[4 + i][:, :], hT[:, a, c, :],
                                               wqkv_s[b][:, c, i * INNER:(i + 1) * INNER],
                                               start=(c == n == 0), stop=(c == DC - 1 and n == 2))
                        mm.then_inc(proj_done, 1)

                def transpose_qk(t):
                    for i, ready in enumerate((q_prod, k_prod)):
                        pe.wait_ge(ready, t + 1)
                        if i == 0:
                            pe.wait_ge(squared, 2 * t + 2)
                        for hp in range(HP):
                            for a in range(2):
                                mm = pe.matmul(ps[4 + i][:, hp * P:(hp + 1) * P], rot[:, i, a, hp * P:(hp + 1) * P],
                                               ident[:, :], start=(a == 0), stop=(a == 1), is_transpose=True)
                        mm.then_inc(qkT_ps, 1)

                def score(t, u, a, half):
                    pe.wait_ge((pTA_ready, pTB_ready)[a], t)
                    first = (u - 1) if u else 0
                    step = 1 if u else G - 1
                    key_blocks = slice(first, first + step + 1, step)
                    for i in range(2):
                        own = slice(HD * i, HD * i + HD)
                        bank = ps[2 * a + i]
                        mask = mask_sb[:, bass.ds(half, 1), u, :, :].rearrange("p x b k -> p x (b k)")
                        pe.matmul(bank[:, :], identb[:, :], mask.to_broadcast((P, 2, D)),
                                  start=True, stop=False)
                        if a == 0:
                            pe.wait_ge(q_lo, 2 * t + i + 1)
                            pe.wait_ge(k_hi, 4 * t + 2 * i + 2)
                            pe.wait_ge(k_lo, 2 * t + i + 1)
                        for j in range(2):
                            pe.matmul(bank[:, j * D:(j + 1) * D], qS[:, i, 2 * a + j, :], kH[:, i, 2 * a + j, key_blocks, :],
                                      start=False, stop=False)
                            mm = pe.matmul(bank[:, j * D:(j + 1) * D], qS[own, i, 2 * a + j, :],
                                           kL[own, 2 * a + j, key_blocks, :], start=False, stop=(j == 1))
                        mm.then_inc(scored, 1)

                def transpose_p(t, a):
                    for i in range(4):
                        pe.wait_ge(exped, 8 * t + 4 * a + 2 * (i // 2) + 2)
                        for b in range(2):
                            c = (2 * (i % 2) + b) * P
                            mm = pe.transpose(ps[2 * a + i // 2][:, c:c + P], probs[:, a, i, b * P:(b + 1) * P], ident[:, :])
                    mm.then_inc(pT_ps, 1)

                def weigh(t, u, a):
                    pe.wait_ge((pTA_ready, pTB_ready)[a], t + 1)
                    pe.wait_ge(oTlo_ready, t)
                    if a == 0:
                        pe.wait_ge(v_ready, t + 1)
                    cur, prev = block_order(u)
                    for i in range(4):
                        h = 4 * a + 2 * (i % 2) + i // 2
                        for b in range(2):
                            v = vring[:, u if b == cur else (u - 1) % G, h * HD:(h + 1) * HD]
                            mm = pe.matmul(ps[7][:, h * HD:(h + 1) * HD], pT[:, a, i, b, :], v,
                                           start=(b == 0), stop=(b == 1))
                    mm.then_inc(pv_done, 1)

                def transpose_o(t):
                    pe.wait_ge(on_ready, t + 1)
                    for hp in range(HP):
                        mm = pe.transpose(ps[7][:, hp * P:(hp + 1) * P], onorm[:, hp * P:(hp + 1) * P], ident[:, :])
                    mm.then_inc(oT_ps, 1)

                def project_out(t):
                    pe.wait_ge(oTlo_ready, t + 1)
                    for hp in range(HP):
                        for n, (a, b) in enumerate(HALF_SPLIT):
                            mm = pe.matmul(ps[6][:, 0:D], oT[:, a, hp, :], wo_s[b][:, hp, :],
                                           start=(hp == n == 0), stop=(hp == HP - 1 and n == 2))
                    mm.then_inc(wo_done, 1)

                def step_tile(t, u, k, nxt, prev, next2):
                    half = k & 1
                    score(t, u, 0, half)
                    score(t, u, 1, half)
                    if nxt:
                        project(t + 1, (1, 0))
                    if prev:
                        transpose_o(t - 1)
                    transpose_p(t, 0)
                    transpose_p(t, 1)
                    if prev:
                        if nxt:
                            pe.wait_ge(v_ready, t + 2)
                        else:
                            pe.wait_ge(x_attn, t - 1)
                        project_out(t - 1)
                    weigh(t, u, 0)
                    if next2:
                        transpose_h(t + 2, k, u + 2, prev)
                    if nxt:
                        transpose_qk(t + 1)
                    weigh(t, u, 1)
                    if next2:
                        project(t + 2, (2,))

                def transpose_h(t, k, u, before):
                    pe.wait_ge(d_hs, 64 * (pair0 + 2 * k + u // 2 + 1))
                    if before:
                        pe.wait_ge(x_attn, t - 2)
                    else:
                        pe.wait_ge(v_ready, t)
                    for c in range(DC):
                        mm = pe.transpose(ps[6][:, c * P:(c + 1) * P], hs[:, u % 2, c * P:(c + 1) * P], ident[:, :])
                    mm.then_inc(hT_ps, 1)

                t0, pair0 = l * NT, l * (NT // 2)
                pe.wait_ge(x_ready, t0 + NT)
                pe.wait_ge(d_hs, 64 * (pair0 + 1))
                for c in range(DC):
                    mm = pe.transpose(ps[6][:, c * P:(c + 1) * P], hs[:, 0, c * P:(c + 1) * P], ident[:, :])
                mm.then_inc(hT_ps, 1)
                pe.wait_ge(attn_lo, (l + 1) * 2)
                pe.wait_ge(attn_lo_pool, (l + 1) * 2)
                project(t0, (2, 1, 0))
                transpose_h(t0 + 1, 0, 1, False)
                transpose_qk(t0)
                project(t0 + 1, (2,))
                for u in range(G):
                    step_tile(t0 + u, u, 0, True, u > 0, True)
                with pe.Fori(1, NG - 1) as k:
                    for u in range(G):
                        step_tile(t0 + G * k + u, u, k, True, True, True)
                for u in range(G):
                    step_tile(t0 + G * (NG - 1) + u, u, NG - 1, u < G - 1, True, u < G - 2)
                transpose_o(t0 + NT - 1)
                pe.wait_ge(x_attn, t0 + NT - 1)
                project_out(t0 + NT - 1)

                def transpose_hn(g):
                    for c in range(DC):
                        for j in range(G):
                            pe.wait_ge(hn_ready, (l * NG + g) * G + G)
                            mm = pe.transpose(ps[c][:, j * P:(j + 1) * P], hn[:, j, c * P:(c + 1) * P], ident[:, :])
                        mm.then_inc(hnT_ps, 1)

                def expand(g):
                    base = (l * NG + g)
                    for m in range(NM):
                        pe.wait_ge(hid_ready, base * NM + (m - 1 if m else 0))
                        for a, off in ((0, HID), (1, 0)):
                            bank = ps[2 + 2 * (m % 2) + a]
                            for c in range(DC):
                                pe.wait_ge(hnT_lo, base * DC + c + 1)
                                cols = slice(off + m * MC, off + m * MC + MW[m])
                                for n, (i, j) in enumerate(HALF_SPLIT):
                                    mm = pe.matmul(bank[0:MW[m], :], w1_s[i][:, c, cols],
                                                   (hnTh, hnTl)[j][:, c, :],
                                                   start=(c == n == 0), stop=(c == DC - 1 and n == 2))
                            mm.then_inc(expanded, 1)

                def contract(g):
                    for pair in range(G // 2):
                        for chunks in (range(NM - 1), (NM - 1,)):
                            pe.wait_ge(hid_lo, (l * NG + g) * NM + chunks[-1] + 1)
                            for j in (2 * pair, 2 * pair + 1):
                                if chunks[0] == 0:
                                    pe.wait_ge(x_ffn, l * NT + G * g + (j - 1 if pair else 0))
                                for m in chunks:
                                    for n, (a, b) in enumerate(HALF_SPLIT):
                                        mm = pe.matmul(ps[6 + j % 2][:, 0:D],
                                                       (hidh, hidl)[a][0:MW[m], m, j * P:(j + 1) * P],
                                                       w2_s[b][0:MW[m], m, :],
                                                       start=(m == n == 0), stop=(m == NM - 1 and n == 2))
                                if chunks[-1] == NM - 1:
                                    mm.then_inc(contracted, 1)

                pe.wait_ge(w1_split, (l + 1) * PIECES)
                pe.wait_ge(w2_split, (l + 1) * 2)
                pe.wait_ge(x_attn, t0 + NT)
                transpose_hn(0)
                with pe.Fori(0, NG - 1) as g:
                    expand(g)
                    transpose_hn(g + 1)
                    contract(g)
                expand(NG - 1)
                contract(NG - 1)

        @block.vector
        def _(dve):
            dve.wait_ge(d_const, 16 * N_CONST)
            dve.memset(half_log[:, :], 0.5 * float(np.log(LN_SCALE))).then_inc(ones_set, 1)
            dve.memset(vp[:, :, :, P:KVC], 1.0).then_inc(ones_set, 1)
            dve.wait_ge(tanh_done, 1)
            dve.tensor_scalar(gT[:, :], gam_r[:, :], tanh_g[:, 0:1], None, ALU.mult)
            dve.tensor_scalar(bT[:, :], bet_r[:, :], tanh_g[:, 0:1], None, ALU.mult).then_inc(folded, 1)

            for b in range(NB):
                dve.wait_ge(ctx_projected, b + 1)
                for i in range(2):
                    dve.bn_stats(cst[0:CTX, 2 * b + i, :], ps[4 + b][0:CTX, i * D:(i + 1) * D]).then_inc(ctx_stats, 1)
            dve.wait_ge(ctx_stats, 2 * NB)
            for n in range(2 * NB):
                dve.bn_aggr(cmv[0:CTX, n, :], cst[0:CTX, n, :]).then_inc(ctx_moments, 1)
            dve.wait_ge(ctx_moments, 2 * NB)
            dve.tensor_scalar(cve[0:CTX, :], cmv[0:CTX, :, 1], EPS6, None, ALU.add).then_inc(ctx_var, 1)
            def stats(t, k, src, eps):
                st, ag, ve, rs, done = NORM[t]
                mv, var = cmv_of[t], cve_of[t]
                dve.wait_ge(rs, k)
                dve.memset(var[:, 0:2], eps).then_inc(ag, 1)
                for j in range(G):
                    dve.bn_stats(cst_of[t][:, j, :], src(j)).then_inc(st, 1)
                dve.wait_ge(st, G * k + G)
                dve.memset(var[:, 2:G], eps).then_inc(ag, 1)
                for j in range(G):
                    dve.bn_aggr(mv[:, j, :], cst_of[t][:, j, :]).then_inc(ag, 1)
                dve.wait_ge(ag, (G + 2) * (k + 1))
                dve.tensor_tensor(var[:, :], mv[:, :, 1], var[:, :], ALU.add).then_inc(ve, 1)

            def x_tile(k, j):
                return state[:, bass.ds(slot(k, j), 1), :].rearrange("p a d -> p (a d)")

            def x_stats(k):
                if isinstance(k, int) and k < 2:
                    dve.wait_ge(d_x_first[k], 16)
                else:
                    dve.wait_ge(d_x, 16 * (NG - 2))
                stats("lnx", k, lambda j: x_tile(k, j), EPS5)

            def q_stats(k):
                dve.wait_ge(queries_ps, 2 * k + 2)
                stats("lnq", k, lambda j: ps[2 + j // 2][:, (j % 2) * D:(j % 2 + 1) * D], EPS6)

            def divide(b, s):
                for j in range(G):
                    n = WPB * b + G * s + j
                    dve.wait_ge(attended, n + 1)
                    heads = ps[4 + j][:, 0:DC * KVC].rearrange("p (c n) -> p c n", c=DC)
                    z = zinv[:, j, :].rearrange("p (c h) -> p c h", c=DC)
                    dve.tensor_scalar(z, heads[:, :, P:KVC], EPS6, None, ALU.add).then_inc(z_sums_ready, 1)
                    dve.wait_ge(z_sums_ready, n + 1)
                    dve.reciprocal(zinv[:, j, :], zinv[:, j, :]).then_inc(z_ready, 1)
                    dve.wait_ge(z_ready, n + 1)
                    for c in range(DC):
                        ins = dve.tensor_tensor(
                            att[:, c * XHC:(c + 1) * XHC, s * G + j, :],
                            heads[:, c, 0:P].rearrange("p (h e) -> p h e", h=XHC),
                            z[:, c, :].unsqueeze(2).to_broadcast((P, XHC, XD)), ALU.mult)
                    ins.then_inc(att_ready, 1)

            def add_eps(b):
                for s in range(2):
                    dve.wait_ge(relu_ready, WPB * b + WPB)
                    dve.wait_ge(attended, WPB * b)
                    dve.tensor_scalar(qTs[:, :, G * s:G * s + G, :],
                                      reluT[:, :, G * s:G * s + G, :, :].rearrange("p c m i a -> p c m (i a)"),
                                      EPS6, None, ALU.add).then_inc(qprime_ready, 1)

            def y_stats(b, s):
                dve.wait_ge(d_x1[s], 16 * b)
                dve.wait_ge(x_ready, WPB * b)
                for j in range(G):
                    t = s * G + j
                    dve.wait_ge(dense_done, 4 * b + t // 2 + 1)
                    dve.tensor_tensor(yx[s][:, j, :], ps[4 + t // 2][:, (t % 2) * D:(t % 2 + 1) * D], db_r[:, :], ALU.add)\
                       .then_inc(y_ready, 1)
                dve.wait_ge(y_ready, WPB * b + s * G + G)
                stats(f"lno{s}", b, lambda j: yx[s][:, j, :], EPS6)

            def residual(b, s):
                t = f"lno{s}"
                dve.wait_ge(NORM[t][3], b + 1)
                for j in range(G):
                    dve.scalar_tensor_tensor(out=yx[s][:, j, :], in0=yx[s][:, j, :], scalar=cmv_of[t][:, j, 0:1],
                                             in1=gT[:, :], op0=ALU.subtract, op1=ALU.mult).then_inc(NORM[t][4], 1)
                for j in range(G):
                    dve.wait_ge(NORM[t][4], WPB * b + s * G + j + 1)
                    dve.wait_ge(beta_added, WPB * b + WPB)
                    dve.scalar_tensor_tensor(out=yx[s][:, j, :], in0=yx[s][:, j, :], scalar=crs_of[t][:, j:j + 1],
                                             in1=x_tile(2 * b + s, j), op0=ALU.mult, op1=ALU.add).then_inc(x1_ready, 1)
                dve.wait_ge(x1_ready, WPB * b + s * G + G)
                stats(f"lnf{s}", b, lambda j: yx[s][:, j, :], EPS5)

            def inner_input(b, s):
                t = f"lnf{s}"
                dve.wait_ge(NORM[t][3], b + 1)
                for j in range(G):
                    dve.tensor_scalar(x_tile(2 * b + s, j), yx[s][:, j, :], cmv_of[t][:, j, 0:1], crs_of[t][:, j:j + 1],
                                      ALU.subtract, ALU.mult).then_inc(x_ready, 1)

            def context_features():
                dve.wait_ge(ctx_rstd, 1)
                for b in range(NB):
                    for i in range(2):
                        n = 2 * b + i
                        dve.tensor_scalar(kvh[:, b, i, :], ps[4 + b][0:CTX, i * D:(i + 1) * D], cmv[0:CTX, n, 0:1],
                                          crs[0:CTX, n:n + 1], ALU.subtract, ALU.mult).then_inc(ctx_normed, 1)
                halves = [kvh[:, b, i, :] for b in range(NB) for i in range(2)]
                N2 = 2 * NB
                for n, r in enumerate(halves):
                    dve.wait_ge(ctx_normed, N2)
                    dve.tensor_tensor(r, r, gam_r[0:CTX, :], ALU.mult).then_inc(ctx_normed, 1)
                for n, r in enumerate(halves):
                    dve.wait_ge(ctx_normed, 2 * N2)
                    dve.tensor_tensor(r, r, bet_r[0:CTX, :], ALU.add).then_inc(ctx_normed, 1)
                for b in range(NB):
                    dve.wait_ge(ctx_normed, 3 * N2)
                    dve.tensor_scalar(kvh[:, b, 0, :], kvh[:, b, 0, :], 0.0, EPS6, ALU.max, ALU.add).then_inc(ctx_normed, 1)
                for b in range(NB):
                    dve.wait_ge(ctx_normed, 3 * N2 + NB)
                    dve.tensor_scalar(kp[:, b, :], kvh[:, b, 0, :], em[:, b:b + 1], None, ALU.mult).then_inc(ctx_features, 1)
                    dve.wait_ge(ones_set, 2)
                    dve.tensor_scalar(vp[:, b, :, 0:P], kvh[:, b, 1, :].rearrange("p (c e) -> p c e", c=DC),
                                      em[:, b:b + 1], None, ALU.mult).then_inc(ctx_features, 1)

            def mask_key_values():
                for b in range(NB):
                    dve.wait_ge(key_values_ps, b + 1)
                    dve.tensor_tensor(kvs[:, b, :, :], ps[4 + b][:, 0:DC * KVC].rearrange("p (c n) -> p c n", c=DC),
                                      blocks[:, :, :], ALU.mult).then_inc(key_values_ready, 1)

            x_stats(0)
            context_features()
            q_stats(0)
            x_stats(1)
            mask_key_values()
            q_stats(1)

            def sequence(b, nxt):
                k = 2 * b + 2
                add_eps(b)
                if nxt:
                    x_stats(k)
                divide(b, 0)
                divide(b, 1)
                if nxt:
                    q_stats(k)
                    x_stats(k + 1)
                y_stats(b, 0)
                y_stats(b, 1)
                residual(b, 0)
                if nxt:
                    q_stats(k + 1)
                residual(b, 1)
                if not nxt:
                    for s in range(2):
                        inner_input(b, s)

            with dve.Fori(0, NB - 1) as b:
                sequence(b, True)
            sequence(NB - 1, False)

            with dve.Fori(0, LAYERS) as l:
                t0 = l * NT
                for i, (loaded, hi, lo) in enumerate(attn_parts()[0:2]):
                    dve.wait_ge(attn_hi, 4 * l + i + 1)
                    dve.tensor_tensor(lo, loaded, f32(hi), ALU.subtract).then_inc(attn_lo, 1)
                dve.wait_ge(d_attn_w, (l + 1) * 16 * 5)
                for i in range(2):
                    for a in range(2):
                        ins = dve.tensor_tensor(tab[:, :, i, a, :], tab[:, :, i, a, :],
                                                qks[:, i:i + 1, :].to_broadcast((P, WPB, HD)), ALU.mult)
                        if i == 1 and a == 1:
                            ins.then_inc(tab_ready, 1)
                dve.wait_ge(tab_ready, l + 1)

                def split_hT(t):
                    dve.wait_ge(hT_ready, t + 1)
                    dve.tensor_tensor(hT[:, 1, :, :], ps[6][:, 0:D].rearrange("p (c t) -> p c t", c=DC),
                                      f32(hT[:, 0, :, :]), ALU.subtract).then_inc(hTlo_ready, 1)

                def split_oT(t):
                    dve.wait_ge(oT_ps, t + 1)
                    dve.tensor_copy(oT[:, 0, :, :], ps[7][:, :].rearrange("p (h t) -> p h t", h=HP)).then_inc(oT_ready, 1)
                    dve.wait_ge(oT_ready, t + 1)
                    dve.tensor_tensor(oT[:, 1, :, :], ps[7][:, :].rearrange("p (h t) -> p h t", h=HP),
                                      f32(oT[:, 0, :, :]), ALU.subtract).then_inc(oTlo_ready, 1)

                def sum_squares(t, n):
                    cols = slice(n * H, n * H + H)
                    dve.wait_ge(squared, 2 * t + n + 1)
                    dve.tensor_reduce(ssum[:, cols], sq[:, n, :].rearrange("p (h d) -> p h d", h=H), AX.X, ALU.add)\
                       .then_inc(summed, 1)
                    dve.wait_ge(summed, 2 * t + n + 1)
                    dve.tensor_scalar(ssum[:, cols], ssum[:, cols], 1e-24, None, ALU.max).then_inc(clipped, 1)

                def rotate_queries(t, w):
                    dve.wait_ge(proj_done, 3 * t + 3)
                    dve.wait_ge(qkT_ps, 2 * t)
                    src = ps[4][:, :]
                    dve.tensor_tensor(rot[:, 0, 0, :].rearrange("p (h d) -> p h d", h=H),
                                      src.rearrange("p (h d) -> p h d", h=H),
                                      tab[:, bass.ds(w, 1), 0, 0, :].to_broadcast((P, H, HD)), ALU.mult)
                    dst = rot[:, 0, 1, :].rearrange("p (h a e) -> p h a e", h=H, a=2)
                    src = src.rearrange("p (h a e) -> p h a e", h=H, a=2)
                    for a in range(2):
                        ins = dve.tensor_tensor(
                            dst[:, :, 1 - a, :], src[:, :, a, :],
                            tab[:, bass.ds(w, 1), 0, 1, a * 32:a * 32 + 32].to_broadcast((P, H, 32)), ALU.mult)
                    ins.then_inc(q_prod, 1)

                def refine_rsqrt(t, u, n):
                    cols = slice(n * H, n * H + H)
                    dve.wait_ge(guessed, 2 * t + n + 1)
                    dve.tensor_tensor(ya[:, cols], y0[:, cols], y0[:, cols], ALU.mult).then_inc(newton, 1)
                    dve.wait_ge(newton, 7 * t + 3 * n + 1)
                    dve.scalar_tensor_tensor(out=yb[:, cols], in0=ya[:, cols], scalar=-0.5, in1=ssum[:, cols],
                                             op0=ALU.mult, op1=ALU.mult).then_inc(newton, 1)
                    dve.wait_ge(newton, 7 * t + 3 * n + 2)
                    dve.scalar_tensor_tensor(out=rn[:, u % 2, cols], in0=yb[:, cols], scalar=1.5, in1=y0[:, cols],
                                             op0=ALU.add, op1=ALU.mult).then_inc(newton, 1)
                    if n:
                        dve.wait_ge(newton, 7 * t + 6)
                        dve.tensor_scalar(rn[:, u % 2, cols], rn[:, u % 2, cols], 8.0, None, ALU.mult).then_inc(newton, 1)

                def normalise_keys(t, u):
                    dve.wait_ge(newton, 7 * t + 3)
                    dve.wait_ge(k_prod, t)
                    dve.tensor_tensor(khat[:, :].rearrange("p (h d) -> p h d", h=H),
                                      ps[5][:, :].rearrange("p (h d) -> p h d", h=H),
                                      rn[:, u % 2, 0:H].unsqueeze(2).to_broadcast((P, H, HD)), ALU.mult)\
                       .then_inc(khat_ready, 1)

                def split_qk(t, u):
                    for i in range(2):
                        own, other = (slice(HD * j, HD * j + HD) for j in (i, 1 - i))
                        dve.wait_ge(q_hi, 2 * t + i + 1)
                        dve.tensor_tensor(qS[other, i, :, :], ps[4][own, :].rearrange("p (h t) -> p h t", h=HP),
                                          f32(qS[own, i, :, :]), ALU.subtract).then_inc(q_lo, 1)
                    for i in range(2):
                        own = slice(HD * i, HD * i + HD)
                        dve.wait_ge(k_hi, 4 * t + 2 * i + 2)
                        dve.tensor_tensor(kL[own, :, u, :], ps[5][own, :].rearrange("p (h t) -> p h t", h=HP),
                                          f32(kH[own, i, :, u, :]), ALU.subtract).then_inc(k_lo, 1)

                def row_max(t, u, a):
                    for i in range(2):
                        heads = slice(4 * a + i, 4 * a + i + 3, 2)
                        dve.wait_ge(scored, 4 * t + 2 * a + i + 1)
                        dve.tensor_reduce(rowmax[:, u % 2, heads], ps[2 * a + i][:, :].rearrange("p (j k) -> p j k", j=2),
                                          AX.X, ALU.max, negate=True).then_inc(maxed, 1)
                        dve.wait_ge(maxed, 4 * t + 2 * a + i + 1)
                        dve.wait_ge(newton, 7 * t + 7)
                        dve.tensor_tensor(negmax[:, u % 2, heads], rowmax[:, u % 2, heads],
                                          rn[:, u % 2, H + heads.start:H + heads.stop:2], ALU.mult).then_inc(bias_ready, 1)

                def add_to_state(t, s):
                    dve.wait_ge(wo_done, t + 1)
                    tile = state[:, bass.ds(s, 1), :].rearrange("p a d -> p (a d)")
                    dve.tensor_tensor(tile, ps[6][:, 0:D], tile, ALU.add).then_inc(x_attn, 1)

                def normalise_o(t, u):
                    dve.wait_ge(exped, 8 * t + 8)
                    dve.reciprocal(linv[:, :], lsum[:, u % 2, :]).then_inc(linv_ready, 1)
                    dve.wait_ge(linv_ready, t + 1)
                    dve.wait_ge(pv_done, 2 * t + 2)
                    dve.tensor_tensor(onorm[:, :].rearrange("p (h d) -> p h d", h=H),
                                      ps[7][:, :].rearrange("p (h d) -> p h d", h=H),
                                      linv[:, :].unsqueeze(2).to_broadcast((P, H, HD)), ALU.mult).then_inc(on_ready, 1)

                def group_stats(g):
                    base = l * NG + g
                    dve.wait_ge(d_hf, 64 * (base + 1))
                    for j in range(G):
                        dve.bn_stats(fst[:, j, 0, :], hf[:, j, :]).then_inc(ffn_stats, 1)
                    dve.wait_ge(ffn_stats, G * (base + 1))
                    dve.memset(fve[:, :], EPS5).then_inc(ffn_moments, 1)
                    for j in range(G):
                        dve.bn_aggr(fmv[:, j, :], fst[:, j, 0, :]).then_inc(ffn_moments, 1)
                    dve.wait_ge(ffn_moments, (G + 1) * (base + 1))
                    dve.tensor_tensor(fve[:, :], fmv[:, :, 1], fve[:, :], ALU.add).then_inc(ffn_var, 1)

                def step(t, u, w, s_prev, nxt, prev, next2=True):
                    row_max(t, u, 0)
                    if prev:
                        normalise_o(t - 1, u - 1)
                    row_max(t, u, 1)
                    if nxt:
                        sum_squares(t + 1, 0)
                    if prev:
                        split_oT(t - 1)
                    if nxt:
                        refine_rsqrt(t + 1, u + 1, 0)
                        normalise_keys(t + 1, u + 1)
                    if u == G - 1 and not nxt:
                        group_stats(0)
                    if nxt:
                        rotate_queries(t + 1, w)
                    if prev:
                        add_to_state(t - 1, s_prev)
                    if nxt:
                        sum_squares(t + 1, 1)
                        refine_rsqrt(t + 1, u + 1, 1)
                    if next2:
                        split_hT(t + 2)
                    if nxt:
                        split_qk(t + 1, (u + 1) % G)

                split_hT(t0)
                sum_squares(t0, 0)
                rotate_queries(t0, 0)
                refine_rsqrt(t0, 0, 0)
                normalise_keys(t0, 0)
                sum_squares(t0, 1)
                refine_rsqrt(t0, 0, 1)
                split_hT(t0 + 1)
                split_qk(t0, 0)
                for u in range(G):
                    step(t0 + u, u, (u + 1) % WPB, slot(0, u - 1), True, u > 0)
                with dve.Fori(1, NG - 1) as k:
                    for u in range(G):
                        s_prev = slot(k, u - 1) if u else slot(k - 1, G - 1)
                        step(t0 + G * k + u, u, (G * k + u + 1) & (WPB - 1), s_prev, True, True)
                for u in range(G):
                    s_prev = slot(NG - 1, u - 1) if u else slot(NG - 2, G - 1)
                    step(t0 + G * (NG - 1) + u, u, (G * (NG - 1) + u + 1) % WPB, s_prev, u < G - 1, True, u < G - 2)
                normalise_o(t0 + NT - 1, G - 1)
                split_oT(t0 + NT - 1)
                add_to_state(t0 + NT - 1, slot(NG - 1, G - 1))

                def group_apply(g):
                    base = l * NG + g
                    dve.wait_ge(ffn_rstd, base + 1)
                    dve.wait_ge(hnT_ps, base * DC)
                    for j in range(G):
                        dve.tensor_scalar(hn[:, j, :], hf[:, j, :], fmv[:, j, 0:1], frs[:, j:j + 1],
                                          ALU.subtract, ALU.mult).then_inc(hn_ready, 1)

                def round_hnT(g):
                    for c in range(DC):
                        dve.wait_ge(hnT_ready, (l * NG + g) * DC + c + 1)
                        dve.tensor_copy(hnTh[:, c, :], hnT[:, c, :]).then_inc(hnT_hi, 1)

                def gate(g, nxt):
                    base = l * NG + g
                    for m in range(NM):
                        dve.wait_ge(gelu_ready, base * NM + m + 1)
                        dve.wait_ge(expanded, base * 2 * NM + 2 * m + 2)
                        dve.wait_ge(contracted, l * NT + G * g)
                        dve.scalar_tensor_tensor(out=hid[0:MW[m], m, :], in0=ps[3 + 2 * (m % 2)][0:MW[m], :],
                                                 scalar=b1c[0:MW[m], 0, m:m + 1], in1=gel[0:MW[m], m % 2, :],
                                                 op0=ALU.add, op1=ALU.mult).then_inc(hid_ready, 1)
                        dve.wait_ge(hid_ready, base * NM + m + 1)
                        dve.tensor_copy(hidh[0:MW[m], m, :], hid[0:MW[m], m, :]).then_inc(hid_hi, 1)
                        if nxt and m == 1:
                            group_stats(g + 1)
                        if nxt and m == 3:
                            group_apply(g + 1)

                def add_group(g):
                    for j in range(G):
                        dve.wait_ge(contracted, l * NT + G * g + j + 1)
                        tile = state[:, bass.ds(slot(g, j), 1), :].rearrange("p a d -> p (a d)")
                        dve.tensor_tensor(tile, ps[6 + j % 2][:, 0:D], tile, ALU.add).then_inc(x_ffn, 1)

                dve.wait_ge(d_ffn_w, (l + 1) * 16 * 10)
                group_apply(0)
                round_hnT(0)
                with dve.Fori(0, NG - 1) as g:
                    gate(g, True)
                    round_hnT(g + 1)
                    add_group(g)
                gate(NG - 1, False)
                add_group(NG - 1)

            with dve.Fori(0, NG) as g:
                dve.wait_ge(x_ready, LAYERS * NT + G * g + G)
                dve.wait_ge(d_x1_back, 16 * NG)
                s = slot(g, 0)
                dve.scalar_tensor_tensor(out=x1[:, bass.ds(G * g, G), :], in0=state[:, bass.ds(s, G), :],
                                         scalar=tanh_g[:, 1:2], in1=x1[:, bass.ds(G * g, G), :],
                                         op0=ALU.mult, op1=ALU.add).then_inc(summed_out, 1)


_INS = ["x", "ctx_1024", "mask_BxS2_ff1", "g_xattn", "g_ffn", "L0_xattn_wq", "L0_xattn_wk", "L0_xattn_wv",
        "L0_xattn_ln_gamma", "L0_xattn_ln_beta", "L0_xattn_dense_w", "L0_xattn_dense_b",
        "L0_ffn_wqkv", "L0_ffn_q_scale", "L0_ffn_k_scale", "L0_ffn_wo", "L0_ffn_ln_g", "L0_ffn_ln_b",
        "L0_ffn_w1", "L0_ffn_b1", "L0_ffn_w2", "L0_ffn_b2"]


def kernel(**inputs):
    import concourse.bacc as bacc
    from concourse.bass_utils import run_bass_kernel_spmd

    nc = bacc.Bacc("TRN2", target_bir_lowering=False, num_devices=1)
    arrays, args = {}, []

    def put(name, a):
        a = np.ascontiguousarray(a)
        arrays[name] = a
        args.append(nc.dram_tensor(name, a.shape, mybir.dt.from_np(a.dtype), kind="ExternalInput").ap())

    for name in _INS:
        put(f"in_{name}_dram", np.asarray(inputs[name]))
    put("tables_dram", position_tables())
    put("masks_dram", masks())
    put("blocks_dram", block_diagonal())
    put("ident_dram", np.eye(P, dtype=np.float32))
    out = nc.dram_tensor("out_dram", (NB, S, D), F32, kind="ExternalOutput").ap()
    program(nc, *args, out)
    r = run_bass_kernel_spmd(nc, [arrays], core_ids=[0])
    return r.results[0]["out_dram"]
```
